# Optimizing a Trainium2 kernel written in Bass

```python
import numpy as np
import jax
import jax.numpy as jnp

def _softmax(x, axis=-1):
    return jax.nn.softmax(x, axis=axis)

def _gelu(x):
    return jax.nn.gelu(x, approximate=True)

def _silu(x):
    return jax.nn.silu(x)

def _sigmoid(x):
    return jax.nn.sigmoid(x)

def _layernorm(x, axis=-1, eps=1e-05):
    m = jnp.mean(x, axis=axis, keepdims=True)
    v = jnp.var(x, axis=axis, keepdims=True)
    return (x - m) / jnp.sqrt(v + eps)

def _scatter_add(tgt, idx, src, axis=0):
    return tgt.at[idx].add(src)

def _segment_sum(src, seg, n):
    return jax.ops.segment_sum(src, seg, n)
kernel_name = 'mk_decoder_postln_d2_seqx_r8_8bd1a4'

def setup_inputs(seed: int=0):
    np.random.seed(seed)
    _w = jnp.asarray

    def _rec_inputs():
        import jax
        import jax.numpy as jnp
        _rk = jax.random.key(seed)
        x = -0.0002928 + 1 * jax.random.normal(jax.random.fold_in(_rk, 1), (2, 512, 128), jnp.float32)
        _lenS = 512 - jax.random.randint(jax.random.fold_in(_rk, 7), (2,), 0, max(1, 512 // 4) + 1, jnp.int32)
        _lenS2 = 77 - jax.random.randint(jax.random.fold_in(_rk, 8), (2,), 0, max(1, 77 // 4) + 1, jnp.int32)
        _ctx_1024P = jax.random.normal(jax.random.fold_in(_rk, 11), (2, 16, 128), jnp.float32)
        _ctx_1024c = jax.random.dirichlet(jax.random.fold_in(_rk, 511), 0.3 * jnp.ones((16,), jnp.float32), (2, 77))
        _ctx_1024t = jnp.einsum('bsk,bkd->bsd', _ctx_1024c, _ctx_1024P)
        _ctx_1024t = _ctx_1024t * jax.lax.rsqrt(jnp.mean(jnp.square(_ctx_1024t)) + 1e-12) * 0.953939
        ctx_1024 = -1.39393e-06 + 0.999914 * (_ctx_1024t + 0.3 * jax.random.normal(jax.random.fold_in(_rk, 611), (2, 77, 128), jnp.float32))
        return (x, ctx_1024)
    x, ctx_1024 = _rec_inputs()

    def _L0_attn_setup():
        import jax, jax.numpy as jnp
        import numpy as np
        N_EMBD = 128
        N_HEAD = 16
        SEQ = 256
        BATCH = 2
        NEG = -1000000000.0
        key = jax.random.key(seed)
        k0, k1, k2 = jax.random.split(key, 3)
        return {'hidden_states': jax.random.normal(k0, (BATCH, SEQ, N_EMBD), dtype=jnp.float32), 'w_attn': jax.random.normal(k1, (3 * N_EMBD, N_EMBD), dtype=jnp.float32) * 0.02, 'b_attn': jnp.zeros((3 * N_EMBD,), dtype=jnp.float32), 'w_proj': jax.random.normal(k2, (N_EMBD, N_EMBD), dtype=jnp.float32) * 0.02, 'b_proj': jnp.zeros((N_EMBD,), dtype=jnp.float32)}
    _L0_attn_all = _L0_attn_setup()
    _L0_attn_in = {k: v for k, v in _L0_attn_all.items() if k in ('w_attn', 'b_attn', 'w_proj', 'b_proj')}
    del _L0_attn_all

    def _L0_xattn_setup():
        import jax, jax.numpy as jnp
        import numpy as np
        import math
        D_MODEL = 128
        NUM_HEADS = 8
        D_HEAD = D_MODEL // NUM_HEADS
        D_FF = 4 * D_MODEL
        LN_EPS = 1e-05

        def _layer_norm(x, g, b):
            mu = jnp.mean(x, axis=-1, keepdims=True)
            var = jnp.mean((x - mu) ** 2, axis=-1, keepdims=True)
            return (x - mu) * jax.lax.rsqrt(var + LN_EPS) * g + b
        key = jax.random.key(seed)
        ks = jax.random.split(key, 16)
        B, Sq, Sk = (2, 256, 256)
        s = 1.0 / math.sqrt(D_MODEL)
        inp = {'query': jax.random.normal(ks[0], (B, Sq, D_MODEL), jnp.float32), 'key': jax.random.normal(ks[1], (B, Sk, D_MODEL), jnp.float32), 'value': jax.random.normal(ks[2], (B, Sk, D_MODEL), jnp.float32), 'Wq': jax.random.normal(ks[3], (D_MODEL, D_MODEL), jnp.float32) * s, 'Wk': jax.random.normal(ks[4], (D_MODEL, D_MODEL), jnp.float32) * s, 'Wv': jax.random.normal(ks[5], (D_MODEL, D_MODEL), jnp.float32) * s, 'Wo': jax.random.normal(ks[6], (D_MODEL, D_MODEL), jnp.float32) * s, 'lambda_param': jnp.asarray(0.8, jnp.float32), 'ln1_g': jnp.ones((D_MODEL,), jnp.float32), 'ln1_b': jnp.zeros((D_MODEL,), jnp.float32), 'ln2_g': jnp.ones((D_MODEL,), jnp.float32), 'ln2_b': jnp.zeros((D_MODEL,), jnp.float32), 'ffn_w1': jax.random.normal(ks[7], (D_MODEL, D_FF), jnp.float32) * s, 'ffn_b1': jnp.zeros((D_FF,), jnp.float32), 'ffn_w2': jax.random.normal(ks[8], (D_FF, D_MODEL), jnp.float32) * (1.0 / math.sqrt(D_FF)), 'ffn_b2': jnp.zeros((D_MODEL,), jnp.float32)}
        return inp
    _L0_xattn_all = _L0_xattn_setup()
    _L0_xattn_in = {k: v for k, v in _L0_xattn_all.items() if k in ('Wq', 'Wk', 'Wv', 'Wo', 'lambda_param', 'ln1_g', 'ln1_b', 'ln2_g', 'ln2_b', 'ffn_w1', 'ffn_b1', 'ffn_w2', 'ffn_b2')}
    del _L0_xattn_all

    def _L0_ffn_setup():
        import jax, jax.numpy as jnp
        import numpy as np
        TOP_K = 2
        key = jax.random.key(seed)
        ks = jax.random.split(key, 6)
        B, S, D, E = (8, 512, 128, 8)
        s = 1.0 / np.sqrt(D)
        return {'x': jax.random.normal(ks[0], (B, S, D), dtype=jnp.float32), 'Wr': jax.random.normal(ks[1], (D, E), dtype=jnp.float32) * s, 'br': jnp.zeros((E,), dtype=jnp.float32), 'W1': jax.random.normal(ks[2], (E, D, D), dtype=jnp.float32) * s, 'b1': jnp.zeros((E, D), dtype=jnp.float32), 'W2': jax.random.normal(ks[3], (E, D, D), dtype=jnp.float32) * s, 'b2': jnp.zeros((E, D), dtype=jnp.float32)}
    _L0_ffn_all = _L0_ffn_setup()
    _L0_ffn_in = {k: v for k, v in _L0_ffn_all.items() if k in ('Wr', 'br', 'W1', 'b1', 'W2', 'b2')}
    del _L0_ffn_all

    def _L1_attn_setup():
        import jax, jax.numpy as jnp
        import numpy as np
        import math
        B, T, C = (8, 256, 128)
        N_LAYER, LAYER_ID = (24, 12)

        def wkv_scan(w_decay, u, k, v):
            w = -jnp.exp(w_decay)
            kt = jnp.swapaxes(k, 0, 1)
            vt = jnp.swapaxes(v, 0, 1)
            Bn, Cn = (k.shape[0], k.shape[2])
            aa0 = jnp.zeros((Bn, Cn), k.dtype)
            bb0 = jnp.zeros((Bn, Cn), k.dtype)
            pp0 = jnp.full((Bn, Cn), -1e+38, k.dtype)

            def step(carry, kv):
                aa, bb, pp = carry
                k_t, v_t = kv
                ww = u + k_t
                q = jnp.maximum(pp, ww)
                e1 = jnp.exp(pp - q)
                e2 = jnp.exp(ww - q)
                y = (e1 * aa + e2 * v_t) / (e1 * bb + e2)
                ww2 = pp + w
                q2 = jnp.maximum(ww2, k_t)
                e1 = jnp.exp(ww2 - q2)
                e2 = jnp.exp(k_t - q2)
                return ((e1 * aa + e2 * v_t, e1 * bb + e2, q2), y)
            _, ys = jax.lax.scan(step, (aa0, bb0, pp0), (kt, vt))
            return jnp.swapaxes(ys, 0, 1)
        key = jax.random.key(seed)
        ks = jax.random.split(key, 8)
        ratio_0_to_1 = LAYER_ID / (N_LAYER - 1)
        ratio_1_to_almost0 = 1.0 - LAYER_ID / N_LAYER
        h = np.arange(C, dtype=np.float64)
        time_decay = (-5 + 8 * (h / (C - 1)) ** (0.7 + 1.3 * ratio_0_to_1)).astype(np.float32)
        zigzag = np.array([(i + 1) % 3 - 1 for i in range(C)], dtype=np.float64) * 0.5
        time_first = (np.ones(C) * math.log(0.3) + zigzag).astype(np.float32)
        xpos = np.arange(C, dtype=np.float64) / C
        time_mix_k = (xpos ** ratio_1_to_almost0).astype(np.float32).reshape(1, 1, C)
        time_mix_v = (xpos ** ratio_1_to_almost0 + 0.3 * ratio_0_to_1).astype(np.float32).reshape(1, 1, C)
        time_mix_r = (xpos ** (0.5 * ratio_1_to_almost0)).astype(np.float32).reshape(1, 1, C)
        scale = 1.0 / math.sqrt(C)
        return {'x': jax.random.normal(ks[0], (B, T, C), jnp.float32), 'time_decay': jnp.asarray(time_decay), 'time_first': jnp.asarray(time_first), 'time_mix_k': jnp.asarray(time_mix_k), 'time_mix_v': jnp.asarray(time_mix_v), 'time_mix_r': jnp.asarray(time_mix_r), 'Wk': jax.random.normal(ks[1], (C, C), jnp.float32) * scale, 'Wv': jax.random.normal(ks[2], (C, C), jnp.float32) * scale, 'Wr': jax.random.normal(ks[3], (C, C), jnp.float32) * scale, 'Wo': jax.random.normal(ks[4], (C, C), jnp.float32) * scale}
    _L1_attn_all = _L1_attn_setup()
    _L1_attn_in = {k: v for k, v in _L1_attn_all.items() if k in ('time_decay', 'time_first', 'time_mix_k', 'time_mix_v', 'time_mix_r', 'Wk', 'Wv', 'Wr', 'Wo')}
    del _L1_attn_all

    def _L1_xattn_setup():
        import jax, jax.numpy as jnp
        import numpy as np
        D_MODEL = 128
        N_HEADS = 16
        D_K = D_MODEL // N_HEADS
        key = jax.random.key(seed)
        ks = jax.random.split(key, 12)
        B, S = (4, 256)
        s = 1.0 / np.sqrt(D_MODEL)
        return {'query': jax.random.normal(ks[0], (B, S, D_MODEL), jnp.float32), 'key': jax.random.normal(ks[1], (B, S, D_MODEL), jnp.float32), 'value': jax.random.normal(ks[2], (B, S, D_MODEL), jnp.float32), 'Wq': jax.random.normal(ks[3], (D_MODEL, D_MODEL), jnp.float32) * s, 'bq': jnp.zeros((D_MODEL,), jnp.float32), 'Wk': jax.random.normal(ks[4], (D_MODEL, D_MODEL), jnp.float32) * s, 'bk': jnp.zeros((D_MODEL,), jnp.float32), 'Wv': jax.random.normal(ks[5], (D_MODEL, D_MODEL), jnp.float32) * s, 'bv': jnp.zeros((D_MODEL,), jnp.float32), 'Wo': jax.random.normal(ks[6], (D_MODEL, D_MODEL), jnp.float32) * s, 'bo': jnp.zeros((D_MODEL,), jnp.float32)}
    _L1_xattn_all = _L1_xattn_setup()
    _L1_xattn_in = {k: v for k, v in _L1_xattn_all.items() if k in ('Wq', 'bq', 'Wk', 'bk', 'Wv', 'bv', 'Wo', 'bo')}
    del _L1_xattn_all

    def _L1_ffn_setup():
        import jax, jax.numpy as jnp
        import numpy as np
        D_IN, D_HID = (128, 512)

        def _ternary(key, shape):
            return jax.random.randint(key, shape, -1, 2).astype(jnp.float32)

        def _tlin(x, w, s):
            return jnp.einsum('bsi,oi->bso', x, w) * s
        key = jax.random.key(seed)
        ks = jax.random.split(key, 12)
        inv = lambda fan: 1.0 / np.sqrt(fan).astype(np.float32)
        return {'x': jax.random.normal(ks[0], (4, 256, D_IN), dtype=jnp.float32), 'w1_w': _ternary(ks[1], (D_HID, D_IN)), 'w1_s': jax.random.uniform(ks[2], (D_HID,), dtype=jnp.float32) * inv(D_IN), 'w2_w': _ternary(ks[3], (D_HID, D_IN)), 'w2_s': jax.random.uniform(ks[4], (D_HID,), dtype=jnp.float32) * inv(D_IN), 'h1_w': _ternary(ks[5], (D_HID, D_HID)), 'h1_s': jax.random.uniform(ks[6], (D_HID,), dtype=jnp.float32) * inv(D_HID), 'h2_w': _ternary(ks[7], (D_HID, D_HID)), 'h2_s': jax.random.uniform(ks[8], (D_HID,), dtype=jnp.float32) * inv(D_HID), 'w3_w': _ternary(ks[9], (D_IN, D_HID)), 'w3_s': jax.random.uniform(ks[10], (D_IN,), dtype=jnp.float32) * inv(D_HID)}
    _L1_ffn_all = _L1_ffn_setup()
    _L1_ffn_in = {k: v for k, v in _L1_ffn_all.items() if k in ('w1_w', 'w1_s', 'w2_w', 'w2_s', 'h1_w', 'h1_s', 'h2_w', 'h2_s', 'w3_w', 'w3_s')}
    del _L1_ffn_all
    return {'x': x, 'ctx_1024': ctx_1024, 'L0_attn_w_attn': _L0_attn_in['w_attn'], 'L0_attn_b_attn': _L0_attn_in['b_attn'], 'L0_attn_w_proj': _L0_attn_in['w_proj'], 'L0_attn_b_proj': _L0_attn_in['b_proj'], 'L0_xattn_Wq': _L0_xattn_in['Wq'], 'L0_xattn_Wk': _L0_xattn_in['Wk'], 'L0_xattn_Wv': _L0_xattn_in['Wv'], 'L0_xattn_Wo': _L0_xattn_in['Wo'], 'L0_xattn_lambda_param': _L0_xattn_in['lambda_param'], 'L0_xattn_ln1_g': _L0_xattn_in['ln1_g'], 'L0_xattn_ln1_b': _L0_xattn_in['ln1_b'], 'L0_xattn_ln2_g': _L0_xattn_in['ln2_g'], 'L0_xattn_ln2_b': _L0_xattn_in['ln2_b'], 'L0_xattn_ffn_w1': _L0_xattn_in['ffn_w1'], 'L0_xattn_ffn_b1': _L0_xattn_in['ffn_b1'], 'L0_xattn_ffn_w2': _L0_xattn_in['ffn_w2'], 'L0_xattn_ffn_b2': _L0_xattn_in['ffn_b2'], 'L0_ffn_Wr': _L0_ffn_in['Wr'], 'L0_ffn_br': _L0_ffn_in['br'], 'L0_ffn_W1': _L0_ffn_in['W1'], 'L0_ffn_b1': _L0_ffn_in['b1'], 'L0_ffn_W2': _L0_ffn_in['W2'], 'L0_ffn_b2': _L0_ffn_in['b2'], 'L1_attn_time_decay': _L1_attn_in['time_decay'], 'L1_attn_time_first': _L1_attn_in['time_first'], 'L1_attn_time_mix_k': _L1_attn_in['time_mix_k'], 'L1_attn_time_mix_v': _L1_attn_in['time_mix_v'], 'L1_attn_time_mix_r': _L1_attn_in['time_mix_r'], 'L1_attn_Wk': _L1_attn_in['Wk'], 'L1_attn_Wv': _L1_attn_in['Wv'], 'L1_attn_Wr': _L1_attn_in['Wr'], 'L1_attn_Wo': _L1_attn_in['Wo'], 'L1_xattn_Wq': _L1_xattn_in['Wq'], 'L1_xattn_bq': _L1_xattn_in['bq'], 'L1_xattn_Wk': _L1_xattn_in['Wk'], 'L1_xattn_bk': _L1_xattn_in['bk'], 'L1_xattn_Wv': _L1_xattn_in['Wv'], 'L1_xattn_bv': _L1_xattn_in['bv'], 'L1_xattn_Wo': _L1_xattn_in['Wo'], 'L1_xattn_bo': _L1_xattn_in['bo'], 'L1_ffn_w1_w': _L1_ffn_in['w1_w'], 'L1_ffn_w1_s': _L1_ffn_in['w1_s'], 'L1_ffn_w2_w': _L1_ffn_in['w2_w'], 'L1_ffn_w2_s': _L1_ffn_in['w2_s'], 'L1_ffn_h1_w': _L1_ffn_in['h1_w'], 'L1_ffn_h1_s': _L1_ffn_in['h1_s'], 'L1_ffn_h2_w': _L1_ffn_in['h2_w'], 'L1_ffn_h2_s': _L1_ffn_in['h2_s'], 'L1_ffn_w3_w': _L1_ffn_in['w3_w'], 'L1_ffn_w3_s': _L1_ffn_in['w3_s']}

def reference(x, ctx_1024, L0_attn_w_attn, L0_attn_b_attn, L0_attn_w_proj, L0_attn_b_proj, L0_xattn_Wq, L0_xattn_Wk, L0_xattn_Wv, L0_xattn_Wo, L0_xattn_lambda_param, L0_xattn_ln1_g, L0_xattn_ln1_b, L0_xattn_ln2_g, L0_xattn_ln2_b, L0_xattn_ffn_w1, L0_xattn_ffn_b1, L0_xattn_ffn_w2, L0_xattn_ffn_b2, L0_ffn_Wr, L0_ffn_br, L0_ffn_W1, L0_ffn_b1, L0_ffn_W2, L0_ffn_b2, L1_attn_time_decay, L1_attn_time_first, L1_attn_time_mix_k, L1_attn_time_mix_v, L1_attn_time_mix_r, L1_attn_Wk, L1_attn_Wv, L1_attn_Wr, L1_attn_Wo, L1_xattn_Wq, L1_xattn_bq, L1_xattn_Wk, L1_xattn_bk, L1_xattn_Wv, L1_xattn_bv, L1_xattn_Wo, L1_xattn_bo, L1_ffn_w1_w, L1_ffn_w1_s, L1_ffn_w2_w, L1_ffn_w2_s, L1_ffn_h1_w, L1_ffn_h1_s, L1_ffn_h2_w, L1_ffn_h2_s, L1_ffn_w3_w, L1_ffn_w3_s):
    import jax
    import jax.numpy as jnp

    def _L0_attn_ref(hidden_states, w_attn, b_attn, w_proj, b_proj):
        import jax, jax.numpy as jnp
        import numpy as np
        N_EMBD = 128
        N_HEAD = 16
        SEQ = 256
        BATCH = 2
        NEG = -1000000000.0
        B, S, E = hidden_states.shape
        H = N_HEAD
        D = E // H
        qkv = hidden_states @ w_attn.T + b_attn
        q, k, v = jnp.split(qkv, 3, axis=-1)
        split = lambda t: t.reshape(B, S, H, D).transpose(0, 2, 1, 3)
        q, k, v = (split(q), split(k), split(v))
        w = jnp.einsum('bhnd,bhmd->bhnm', q, k) * jax.lax.rsqrt(float(D))
        mask = jnp.tril(jnp.ones((S, S), dtype=jnp.float32))
        w = jnp.where(mask > 0, w, NEG)
        w = jax.nn.softmax(w, axis=-1)
        attn = jnp.einsum('bhnm,bhmd->bhnd', w, v)
        attn = attn.transpose(0, 2, 1, 3).reshape(B, S, E)
        return attn @ w_proj.T + b_proj

    def _L0_xattn_ref(query, key, value, Wq, Wk, Wv, Wo, lambda_param, ln1_g, ln1_b, ln2_g, ln2_b, ffn_w1, ffn_b1, ffn_w2, ffn_b2):
        import jax, jax.numpy as jnp
        import numpy as np
        import math
        D_MODEL = 128
        NUM_HEADS = 8
        D_HEAD = D_MODEL // NUM_HEADS
        D_FF = 4 * D_MODEL
        LN_EPS = 1e-05

        def _layer_norm(x, g, b):
            mu = jnp.mean(x, axis=-1, keepdims=True)
            var = jnp.mean((x - mu) ** 2, axis=-1, keepdims=True)
            return (x - mu) * jax.lax.rsqrt(var + LN_EPS) * g + b
        B, Sq, _ = query.shape
        Sk = key.shape[1]
        Q = (query @ Wq).reshape(B, Sq, NUM_HEADS, D_HEAD)
        K = (key @ Wk).reshape(B, Sk, NUM_HEADS, D_HEAD)
        V = (value @ Wv).reshape(B, Sk, NUM_HEADS, D_HEAD)
        scale = 1.0 / math.sqrt(D_HEAD)
        scores = jnp.einsum('bqhd,bkhd->bhqk', Q, K) * scale
        attn1 = jax.nn.softmax(scores, axis=-1)
        attn2 = jax.nn.softmax(scores - 1.0, axis=-1)
        lam = jax.nn.sigmoid(lambda_param)
        attn = attn1 - lam * attn2
        attn_out = jnp.einsum('bhqk,bkhd->bqhd', attn, V).reshape(B, Sq, D_MODEL)
        attn_out = attn_out @ Wo
        q_enh = _layer_norm(query + attn_out, ln1_g, ln1_b)
        ffn = jax.nn.relu(q_enh @ ffn_w1 + ffn_b1) @ ffn_w2 + ffn_b2
        return _layer_norm(q_enh + ffn, ln2_g, ln2_b)

    def _L0_ffn_ref(x, Wr, br, W1, b1, W2, b2):
        import jax, jax.numpy as jnp
        import numpy as np
        TOP_K = 2
        k = TOP_K
        scores0 = x[:, 0, :] @ Wr + br
        _, idx = jax.lax.top_k(scores0, k)
        W1g, b1g = (W1[idx], b1[idx])
        W2g, b2g = (W2[idx], b2[idx])
        h = jnp.einsum('bsd,bkde->bkse', x, W1g) + b1g[:, :, None, :]
        h = jax.nn.gelu(h, approximate=False)
        o = jnp.einsum('bkse,bkef->bksf', h, W2g) + b2g[:, :, None, :]
        return jnp.sum(o, axis=1) / k

    def _L1_attn_ref(x, time_decay, time_first, time_mix_k, time_mix_v, time_mix_r, Wk, Wv, Wr, Wo):
        import jax, jax.numpy as jnp
        import numpy as np
        import math
        B, T, C = (8, 256, 128)
        N_LAYER, LAYER_ID = (24, 12)

        def wkv_scan(w_decay, u, k, v):
            w = -jnp.exp(w_decay)
            kt = jnp.swapaxes(k, 0, 1)
            vt = jnp.swapaxes(v, 0, 1)
            Bn, Cn = (k.shape[0], k.shape[2])
            aa0 = jnp.zeros((Bn, Cn), k.dtype)
            bb0 = jnp.zeros((Bn, Cn), k.dtype)
            pp0 = jnp.full((Bn, Cn), -1e+38, k.dtype)

            def step(carry, kv):
                aa, bb, pp = carry
                k_t, v_t = kv
                ww = u + k_t
                q = jnp.maximum(pp, ww)
                e1 = jnp.exp(pp - q)
                e2 = jnp.exp(ww - q)
                y = (e1 * aa + e2 * v_t) / (e1 * bb + e2)
                ww2 = pp + w
                q2 = jnp.maximum(ww2, k_t)
                e1 = jnp.exp(ww2 - q2)
                e2 = jnp.exp(k_t - q2)
                return ((e1 * aa + e2 * v_t, e1 * bb + e2, q2), y)
            _, ys = jax.lax.scan(step, (aa0, bb0, pp0), (kt, vt))
            return jnp.swapaxes(ys, 0, 1)
        xx = jnp.pad(x, ((0, 0), (1, 0), (0, 0)))[:, :-1]
        xk = x * time_mix_k + xx * (1.0 - time_mix_k)
        xv = x * time_mix_v + xx * (1.0 - time_mix_v)
        xr = x * time_mix_r + xx * (1.0 - time_mix_r)
        k = jnp.einsum('btc,oc->bto', xk, Wk)
        v = jnp.einsum('btc,oc->bto', xv, Wv)
        r = jnp.einsum('btc,oc->bto', xr, Wr)
        wkv = wkv_scan(time_decay, time_first, k, v)
        rwkv = jax.nn.sigmoid(r) * wkv
        return jnp.einsum('btc,oc->bto', rwkv, Wo)

    def _L1_xattn_ref(query, key, value, Wq, bq, Wk, bk, Wv, bv, Wo, bo):
        import jax, jax.numpy as jnp
        import numpy as np
        D_MODEL = 128
        N_HEADS = 16
        D_K = D_MODEL // N_HEADS
        B, S, _ = query.shape

        def shape(x):
            return x.reshape(B, -1, N_HEADS, D_K).transpose(0, 2, 1, 3)
        q = shape(query @ Wq + bq)
        k = shape(key @ Wk + bk)
        v = shape(value @ Wv + bv)
        scores = jnp.einsum('bhqd,bhkd->bhqk', q, k) / jnp.sqrt(jnp.float32(D_K))
        p_attn = jax.nn.softmax(scores, axis=-1)
        x = jnp.einsum('bhqk,bhkd->bhqd', p_attn, v)
        x = x.transpose(0, 2, 1, 3).reshape(B, -1, N_HEADS * D_K)
        return x @ Wo + bo

    def _L1_ffn_ref(x, w1_w, w1_s, w2_w, w2_s, h1_w, h1_s, h2_w, h2_s, w3_w, w3_s):
        import jax, jax.numpy as jnp
        import numpy as np
        D_IN, D_HID = (128, 512)

        def _ternary(key, shape):
            return jax.random.randint(key, shape, -1, 2).astype(jnp.float32)

        def _tlin(x, w, s):
            return jnp.einsum('bsi,oi->bso', x, w) * s
        h = jax.nn.silu(_tlin(x, w1_w, w1_s)) * _tlin(x, w2_w, w2_s)
        h = jax.nn.gelu(_tlin(h, h1_w, h1_s), approximate=False)
        h = jax.nn.gelu(_tlin(h, h2_w, h2_s), approximate=False)
        return _tlin(h, w3_w, w3_s)
    x = _layernorm(x + _L0_attn_ref(x, L0_attn_w_attn, L0_attn_b_attn, L0_attn_w_proj, L0_attn_b_proj), axis=-1)
    x = _layernorm(x + _L0_xattn_ref(x, ctx_1024, ctx_1024, L0_xattn_Wq, L0_xattn_Wk, L0_xattn_Wv, L0_xattn_Wo, L0_xattn_lambda_param, L0_xattn_ln1_g, L0_xattn_ln1_b, L0_xattn_ln2_g, L0_xattn_ln2_b, L0_xattn_ffn_w1, L0_xattn_ffn_b1, L0_xattn_ffn_w2, L0_xattn_ffn_b2), axis=-1)
    x = _layernorm(x + _L0_ffn_ref(x, L0_ffn_Wr, L0_ffn_br, L0_ffn_W1, L0_ffn_b1, L0_ffn_W2, L0_ffn_b2), axis=-1)
    x = _layernorm(x + _L1_attn_ref(x, L1_attn_time_decay, L1_attn_time_first, L1_attn_time_mix_k, L1_attn_time_mix_v, L1_attn_time_mix_r, L1_attn_Wk, L1_attn_Wv, L1_attn_Wr, L1_attn_Wo), axis=-1)
    x = _layernorm(x + _L1_xattn_ref(x, ctx_1024, ctx_1024, L1_xattn_Wq, L1_xattn_bq, L1_xattn_Wk, L1_xattn_bk, L1_xattn_Wv, L1_xattn_bv, L1_xattn_Wo, L1_xattn_bo), axis=-1)
    x = _layernorm(x + _L1_ffn_ref(x, L1_ffn_w1_w, L1_ffn_w1_s, L1_ffn_w2_w, L1_ffn_w2_s, L1_ffn_h1_w, L1_ffn_h1_s, L1_ffn_h2_w, L1_ffn_h2_s, L1_ffn_w3_w, L1_ffn_w3_s), axis=-1)
    return x

_drawn_inputs = setup_inputs


def setup_inputs(seed=0):
    import zlib

    import numpy as np

    out = dict(_drawn_inputs(seed))
    spreads = {'L0_attn_b_attn': (0.0, 0.389),
     'L0_attn_b_proj': (0.0, 0.1),
     'L0_xattn_ln1_g': (1.0, 0.2),
     'L0_xattn_ln1_b': (0.0, 0.1),
     'L0_xattn_ln2_g': (1.0, 0.2),
     'L0_xattn_ln2_b': (0.0, 0.1),
     'L0_xattn_ffn_b1': (0.0, 0.292),
     'L0_xattn_ffn_b2': (0.0, 0.1),
     'L0_ffn_br': (0.0, 0.1),
     'L0_ffn_b1': (0.0, 0.1),
     'L0_ffn_b2': (0.0, 0.1),
     'L1_xattn_bq': (0.0, 0.376),
     'L1_xattn_bk': (0.0, 0.8),
     'L1_xattn_bv': (0.0, 0.1),
     'L1_xattn_bo': (0.0, 0.1)}
    factors = {'L0_attn_w_proj': 2.988,
     'L1_ffn_w1_w': 8.0,
     'L1_ffn_w1_s': 8.0,
     'L1_ffn_w2_w': 8.0,
     'L1_ffn_w2_s': 8.0,
     'L1_ffn_h1_w': 8.0,
     'L1_ffn_h1_s': 8.0,
     'L1_ffn_h2_w': 8.0,
     'L1_ffn_h2_s': 8.0,
     'L1_ffn_w3_w': 8.0,
     'L1_ffn_w3_s': 8.0}
    for name, (base, spread) in spreads.items():
        noise = np.random.default_rng([zlib.crc32(name.encode()), seed]).standard_normal(out[name].shape)
        drawn = base * np.exp(spread * noise) if base else spread * noise
        out[name] = jnp.asarray(drawn.astype(out[name].dtype))
    for name, factor in factors.items():
        out[name] = (out[name] * factor).astype(out[name].dtype)
    return out
```

```python
from contextlib import ExitStack

import concourse.bass as bass
from concourse import mybir

F32 = mybir.dt.float32
BF16 = mybir.dt.bfloat16
U32 = mybir.dt.uint32
ALU = mybir.AluOpType
ACT = mybir.ActivationFunctionType
AX = mybir.AxisListType

P = 128
NB = 2
T = 512
TT = T // P
NKEY = 77
NE = 8
TOPK = 2
NF = 4
EPS = 1e-5
VW = 32
H0, D0 = 16, 8
HX = (8, 16)
DX = (16, 8)
QPART = (0, 0, 1, 1, 0, 2)
KPART = (0, 1, 0, 1, 2, 0)
NS = len(QPART)
AUG0 = NS * D0
AUGX = (NS * DX[0], 64)
ONES = 1.0 + 0x3F80 / 2.0 ** 23
G = 4
NG0 = H0 // G
FIRST = {"q": 1, "val": 1, "split": 3, "stack": 16 * NS, "msc": TT * HX[0] // G, "mx": TT * HX[0] // G, "mt": 1,
         "mval": 1, "msplit": 3, "maug": 48, "sc": HX[0], "exp": HX[0], "pv": HX[0], "o": HX[0] // G,
         "den": HX[0] // G, "div": HX[0] // G, "out": 1}
LN_EXP = "natural_log_exp_and_others"
NEG = -1e38

MAX_UNITS = [(0, 0, 4), (1, 0, 2), (1, 2, 2)] + [(i, h, 1) for i in (2, 3) for h in range(G)]
NM = len(MAX_UNITS)
EXP_UNITS = [
    [(0, 0, 0), (1, 0, 512)], [(2, 0, 0), (3, 0, 512)],
    [(0, 1, 0), (0, 3, 384), (1, 1, 512), (1, 3, 896)], [(2, 1, 0), (2, 3, 384), (3, 1, 512), (3, 3, 896)],
    [(0, 2, 0), (1, 2, 256), (2, 2, 512), (3, 2, 768)],
]
NX = len(EXP_UNITS)
DIAGONALS = [[(0, 512, 2)], [(0, 512, 2)], [(0, 512, 2), (384, 512, 2)], [(0, 512, 2), (384, 512, 2)], [(0, 256, 4)]]
LAG = 1.45


def causal_items():
    items = []
    for n in range(NB * NG0):
        items += [(n + j / NM, "max", n, j) for j in range(NM)]
        items.append((n + 1 + 1.5 / NM, "rowmax", n, 0))
        parts = [("score", n, 0), ("score", n, 1), ("values", n - 1, 4), ("score", n, 2), ("score", n, 3),
                 ("denominator", n - 1, 0), ("values", n, 0), ("score", n, 4), ("values", n, 2)]
        items += [(n + LAG + k / len(parts), *part) for k, part in enumerate(parts) if part[1] >= 0]
    last = NB * NG0 - 1
    items.append((last + LAG + 1, "values", last, 4))
    items.append((last + LAG + 1.1, "denominator", last, 0))
    for b in range(NB):
        items.append((NG0 * (b + 1) + LAG + 0.9 + 0.3 * (b == 1), "project", b, 0))
    return [i[1:] for i in sorted(items, key=lambda i: i[0])]


def later_steps():
    out = ["norm_mean0", "norm_var0"]
    for L in range(2):
        cross = [f"cross_query{L}"]
        cross += [(f"cross_max{L}", i, g) for i in range(TT) for g in range(HX[L] // G)]
        cross += [f"cross_rowmax{L}"]
        for h in range(HX[L] + 2):
            cross.append((f"cross_exp{L}", h))
        cross.append(f"cross_out{L}")
        if L == 0:
            out += cross
            out += ["norm_mean1", "norm_var1", "ffn_up", "ffn_down", "norm_mean2", "norm_var2", "norm_mean3",
                    "norm_var3", "route", "expert_up", "expert_down", "norm_mean4", "norm_var4", "mix_in",
                    "mix_scan", "mix_divide", "mix_out", "norm_mean5", "norm_var5"]
        else:
            out += cross
            out += ["norm_mean6", "norm_var6", "gate", "hidden1", "hidden2", "down", "norm_mean7", "norm_var7"]
    return [(s, b) if isinstance(s, str) else (s[0], b, *s[1:]) for s in out for b in range(NB)]


def decoder(nc, dram, out):
    ctx = ExitStack()
    with ctx:
        def sb(name, shape, dt=F32):
            return ctx.enter_context(nc.sbuf_tensor(name, shape, dt))

        def sem(name):
            return ctx.enter_context(nc.semaphore(name))

        def sems(name):
            return [sem(f"{name}_{b}") for b in range(NB)]

        w = {}
        for name, (shape, _) in LOADS.items():
            if name in ("h1", "h2", "x"):
                continue
            w[name] = sb("w_" + name, shape)
        center, mean, ident, sel8, sel16 = (w["const"][:, P * i:P * (i + 1)] for i in range(5))
        sel = {8: sel8, 16: sel16}
        ones = w["const"][0:1, 5 * P:6 * P]
        ident_b = sb("ident_b", [P, P], BF16)
        mask_b = sb("mask_b", [P, P], BF16)
        col = {name: w["cols"][:, i:i + n] for name, i, n in COLS}

        def pair(name, shape, dt=F32):
            return [sb(f"{name}{b}", shape, dt) for b in range(NB)]

        xs = pair("xs", [P, T + 1])
        qe = pair("qe", [P, T])
        z = pair("z", [P, T])
        sq = pair("sq", [P, T])
        rstd = pair("rstd", [P, T])
        qstack = pair("qstack", [P, H0, T], BF16)
        kstack = pair("kstack", [P, H0, T], BF16)
        work = pair("work", [P, 1792])
        wide = pair("wide", [P, 4 * T])
        kx = [sb(f"kx{L}", [P, HX[L], NB * NKEY], BF16) for L in range(2)]
        vx = [sb(f"vx{L}", [NKEY, NB, HX[L], VW]) for L in range(2)]
        v0 = sb("v0", [P, NB, TT, H0, VW])
        probs = sb("probs", [P, 4, 1024])
        mx = pair("mx", [P, TT * H0])
        mt = pair("mt", [64, 2, P])
        mp = pair("mp", [64, 3, P], BF16)
        wmix = [sb(f"wmix{i}", [P, 2, P]) for i in range(3)]
        omm = sb("omm", [P, 3])
        decay = sb("decay", [P, 2])
        keep = sb("keep", [P, 3])
        eps = sb("eps", [P, 1])
        b2s = pair("b2s", [P, 2])
        xb = [z[b] for b in range(NB)]
        route = pair("route", [1, 16])
        choice = pair("choice", [1, 8], U32)
        wh = [v0[:, i, :, :, :].rearrange("p a h c -> p (a h c)").rearrange("p (k n) -> p k n", k=NF)
              for i in range(2)]
        qx = [kstack[b][:, 0:8, :] for b in range(NB)]
        scratch = [kstack[b][:, :, :].rearrange("p h t -> p (h t)").bitcast(F32).rearrange("p (j t) -> p j t", t=T)
                   for b in range(NB)]
        w4 = [wide[b][:, :].rearrange("p (j t) -> p j t", t=T) for b in range(NB)]

        def state(b):
            return xs[b][:, 1:T + 1]

        def split_tiles(area, n):
            parts = area[:, 2 * n:2 * n + 3 * n // 2].bitcast(BF16).rearrange("p (i t) -> p i t", i=3)
            return area[:, 0:n], area[:, n:2 * n], parts

        q_split = [split_tiles(work[b], T) for b in range(NB)]
        k_split = [split_tiles(wide[b], T) for b in range(NB)]
        kx_split = [split_tiles(probs[:, L, :], NB * NKEY) for L in range(2)]

        psum = ctx.enter_context(nc.psum_tensor("psum", [P, 8, 512], F32))

        def bank(i):
            return psum[:, i, :]

        def own(b, i):
            return psum[:, 4 * b + i, :]

        s_load = {name: sem("load_" + name) for name in LOAD_GROUPS}

        def loaded(engine, name):
            group = next(g for g, names in LOAD_GROUPS.items() if name in names)
            n = len(LOAD_GROUPS[group]) if group != "x" else NB
            engine.wait_ge(s_load[group], 16 * n)

        s_zero = sem("zeroed")
        s_vzero = sem("vzero")
        s_qk = sem("qk_proj")
        s_qk_val = sem("qk_value")
        s_qk_split = sem("qk_split")
        s_stack = [sem(f"stack{u}") for u in range(4)]
        s_v0 = sem("v0_proj")
        s_v0_out = sem("v0_out")
        s_kx = sem("kx_proj")
        s_kx_val = sem("kx_value")
        s_kx_split = sem("kx_split")
        s_kx_stack = sem("kx_stack")
        s_vx = sem("vx_proj")
        s_vx_out = sem("vx_out")
        s_wmix = sem("wmix")
        s_small = sem("small")
        s_param = sem("param")
        s_msc = sem("max_scores")
        s_mx = sem("max_done")
        s_mt = sem("rowmax_turned")
        s_mval = sem("rowmax_value")
        s_msplit = sem("rowmax_split")
        s_maug = sem("rowmax_rows")
        s_sc = sem("exp_scores")
        s_exp = sem("exp_done")
        s_mask = sem("masked")
        s_pv = sem("values_done")
        s_o = sem("out_copied")
        s_den = sem("denominators")
        s_rec = sem("reciprocal")
        s_div = sem("divided")
        s_proj = sems("projected")
        s_wh = sem("load_wh")
        s_z, s_cent, s_sq, s_var, s_rstd, s_aff, s_x = (
            sems(n) for n in ("residual", "centered", "squared", "variance", "rstd", "gained", "state"))
        x_q, x_val, x_split, x_stack, x_msc, x_mx, x_mt, x_mval, x_msplit, x_maug, x_sc, x_exp, x_pv, x_o, \
            x_den, x_div, x_out = (sems("x_" + n) for n in (
                "query", "value", "split", "stack", "max_scores", "max_done", "rowmax", "mval", "msplit", "maug",
                "scores", "exp", "values", "copied", "den", "div", "out"))
        s_ln = sems("log_variance")
        x_rec = sems("x_reciprocal")
        s_up, s_relu, s_down = (sems(n) for n in ("ffn_up", "ffn_relu", "ffn_down"))
        s_rt, s_rchain, s_choice, s_pick, s_b2s, s_eup, s_egelu, s_edown = (
            sems(n) for n in ("route_scores", "route_chain", "choice", "picked", "expert_bias", "expert_up",
                              "expert_gelu", "expert_down"))
        s_rk, s_rcp, s_rscan, s_rpool, s_rexp, s_rout = (
            sems(n) for n in ("mix_proj", "mix_copied", "mix_dve", "mix_pool", "mix_exp", "mix_out"))
        s_ga, s_gs, s_gb, s_gh, s_h1, s_g1, s_h2, s_g2, s_dn = (
            sems(n) for n in ("gate_a", "gate_silu", "gate_b", "gated", "hid1", "gelu1", "hid2", "gelu2", "down"))
        s_store = sem("stored")

        items = causal_items()
        steps = later_steps()
        block = ctx.enter_context(nc.Block())

        @block.sync
        def _(sp):
            def load(name):
                group = next(g for g, names in LOAD_GROUPS.items() if name in names)
                sp.dma_start(w[name][:], dram[name]).then_inc(s_load[group], 16)

            for name in ("x", "qk", "cols", "const"):
                if name == "x":
                    for b in range(NB):
                        sp.dma_start(state(b), dram["x"][:, T * b:T * (b + 1)]).then_inc(s_load["x"], 16)
                else:
                    load(name)
            for name in LOADS:
                if name not in ("x", "qk", "cols", "const", "h1", "h2"):
                    load(name)

            def stack(dst, parts, which, d, done):
                for s in range(NS):
                    sp.dma_start(dst[d * s:d * (s + 1)], parts[:, which[s], :]).then_inc(done, 16)

            for u in range(2 * NB):
                b, is_key = u // 2, u % 2
                if u % 2 == 0:
                    sp.wait_ge(s_vzero, b + 1)
                else:
                    sp.wait_ge(s_zero, 6 * b + 1)
                sp.wait_ge(s_qk_split, 3 * (u + 1))
                if is_key:
                    stack(kstack[b], k_split[b][2], KPART, D0, s_stack[u])
                else:
                    stack(qstack[b], q_split[b][2], QPART, D0, s_stack[u])
            for L in range(2):
                sp.wait_ge(s_zero, 6)
                sp.wait_ge(s_kx_split, 3 * (L + 1))
                stack(kx[L], kx_split[L][2], KPART, DX[L], s_kx_stack)

            for kind, n, _ in items:
                if kind == "rowmax":
                    b, g = n // NG0, n % NG0
                    sp.wait_ge(s_msplit, 3 * (n + 1))
                    for i in range(3):
                        dst = qstack[b][AUG0 + i:AUG0 + i + 1, G * g:G * (g + 1), :]
                        sp.dma_start(dst, mp[n % 2][0:G * TT, i, :]) \
                            .then_inc(s_maug, 16)
            sp.wait_ge(s_pv, NX * NB * NG0)
            for i in range(2):
                sp.dma_start(wh[i], dram[f"h{i + 1}"]).then_inc(s_wh, 16)

            for step, b, *_ in steps:
                for L in range(2):
                    if step == f"cross_query{L}":
                        sp.wait_ge(x_split[b], L * FIRST["split"] + 3)
                        stack(qx[b] if L == 0 else qstack[b], q_split[b][2], QPART, DX[L], x_stack[b])
                    if step == f"cross_rowmax{L}":
                        sp.wait_ge(x_msplit[b], L * FIRST["msplit"] + 3)
                        q = qx[b] if L == 0 else qstack[b]
                        for i in range(3):
                            dst = q[AUGX[L] + i:AUGX[L] + i + 1, :, :]
                            sp.dma_start(dst, mp[b][0:HX[L] * TT, i, :]).then_inc(x_maug[b], 16)
                if step == "norm_var7":
                    sp.wait_ge(s_x[b], 7)
                    sp.dma_start(out[:, T * b:T * (b + 1)], state(b)).then_inc(s_store, 16)
            sp.wait_ge(s_store, 16 * NB)

        @block.tensor
        def _(pe):
            loaded(pe, "x")
            loaded(pe, "qk")
            for u in range(2 * NB):
                pe.matmul(bank(u), w["qk"][:, P * (u % 2):P * (u % 2 + 1)], state(u // 2),
                          start=True, stop=True).then_inc(s_qk, 1)
            loaded(pe, "const")
            loaded(pe, "v0")
            for b in range(NB):
                for k in range(TT):
                    o = psum[:, 4 + b, P * k:P * (k + 1)]
                    pe.matmul(o, state(b)[:, P * k:P * (k + 1)], w["v0"][:, 0:P], start=True, stop=False)
                    mm = pe.matmul(o, ones, w["v0"][0:1, P:2 * P], start=False, stop=True)
                mm.then_inc(s_v0, 1)
            loaded(pe, "xkv")
            loaded(pe, "ctx")
            for L in range(2):
                pe.matmul(psum[:, 6 + L, 0:NB * NKEY], w["xkv"][:, 2 * P * L:2 * P * L + P], w["ctx"][:, :],
                          start=True, stop=True).then_inc(s_kx, 1)
            pe.wait_ge(s_v0_out, 1)
            loaded(pe, "xbv")
            for L in range(2):
                for b in range(NB):
                    o = psum[0:NKEY, 4, P * (2 * L + b):P * (2 * L + b + 1)]
                    pe.matmul(o, w["ctx"][:, NKEY * b:NKEY * (b + 1)], w["xkv"][:, 2 * P * L + P:2 * P * (L + 1)],
                              start=True, stop=L == 0)
                    if L == 1:
                        mm = pe.matmul(o, ones[:, 0:NKEY], w["xbv"][0:1, :], start=False, stop=True)
            mm.then_inc(s_vx, 1)

            def max_bank(n, j):
                e = (NM + 1) * n + j
                m, i = divmod(e - 2, NM + 1)
                if e >= 2 and m < NB * NG0:
                    if i == 2:
                        if m >= 1:
                            pe.wait_ge(s_mval, m)
                    else:
                        pe.wait_ge(s_mx, NM * m + (i if i < 2 else i - 1) + 1)
                return 4 + e % 2

            for kind, n, j in items:
                b, g = n // NG0, n % NG0
                if kind == "max":
                    i, h0, nh = MAX_UNITS[j]
                    if n == 0 and j == 0:
                        pe.wait_ge(s_vx_out, 4)
                        pe.wait_ge(s_v0_out, 2)
                    if g == 0 and j == 0:
                        pe.wait_ge(s_stack[2 * b], 16 * NS)
                        pe.wait_ge(s_stack[2 * b + 1], 16 * NS)
                        pe.wait_ge(s_zero, 5 * b + 3)
                    o = bank(max_bank(n, j if j < 2 else j + 1))
                    width = P * (i + 1)
                    for k in range(nh):
                        h = G * g + h0 + k
                        pe.matmul(o[:, width * k:width * (k + 1)], qstack[b][:, h, P * i:P * (i + 1)],
                                  kstack[b][:, h, 0:width], start=True, stop=True, skip_group_check=True)
                        mm = pe.matmul(o[:, width * (k + 1) - P:width * (k + 1)], ident_b[:, :], mask_b[:, :],
                                       start=False, stop=True, skip_group_check=True)
                    mm.then_inc(s_msc, 1)
                if kind == "rowmax":
                    o = bank(max_bank(n + 1, 2))
                    pe.wait_ge(s_mx, NM * (n + 1))
                    pe.transpose(o[0:G * TT, 0:P], mx[n % 2][:, 0:G * TT], ident).then_inc(s_mt, 1)
                if kind == "score":
                    v = NX * n + j
                    if j == 0:
                        pe.wait_ge(s_maug, 48 * (n + 1))
                    if v >= 2:
                        pe.wait_ge(s_exp, v - 1)
                    if v == 0:
                        pe.wait_ge(s_qk_val, 4)
                    for h, k, c in EXP_UNITS[j]:
                        at = 2 * (v % 2) + c // 512
                        c = c % 512
                        width = T - P * k
                        mm = pe.matmul(psum[:, at, c:c + width], kstack[b][:, G * g + h, P * k:P * (k + 1)],
                                       qstack[b][:, G * g + h, P * k:T], start=True, stop=True,
                                       skip_group_check=True)
                    mm.then_inc(s_sc, 1)
                if kind == "values":
                    units = [j] if j == 4 else [j, j + 1]
                    pe.wait_ge(s_mask, NX * n + units[-1] + 1)
                    if j == 0 and n >= 1:
                        pe.wait_ge(s_o, n)
                    if n == 0 and j == 0:
                        pe.wait_ge(s_kx_val, 2)
                    blocks = [(u, h, k, c) for u in units for h, k, c in EXP_UNITS[u]]
                    blocks.sort(key=lambda x: x[2])
                    for u, h, k, c in blocks:
                        width = T - P * k
                        mm = pe.matmul(psum[VW * h:VW * (h + 1), 6, P * k:T], v0[:, b, k, G * g + h, :],
                                       probs[:, (NX * n + u) % 4, c:c + width], start=k == 0, stop=k == 2,
                                       skip_group_check=True, tile_position=(0, VW * h))
                    mm.then_inc(s_pv, len(units))
                if kind == "denominator":
                    pe.wait_ge(s_o, n + 1)
                    if n >= 1:
                        pe.wait_ge(s_div, n)
                    if n == NG0:
                        pe.wait_ge(s_z[0], 1)
                    if n == 0:
                        pe.wait_ge(s_kx_val, 2)
                    pe.matmul(bank(7), sel8, sq[b][:, :], start=True, stop=True).then_inc(s_den, 1)
                if kind == "project":
                    b = n
                    if b == 0:
                        loaded(pe, "o0")
                    pe.wait_ge(s_div, NG0 * (b + 1))
                    for k in range(NG0):
                        mm = pe.matmul(bank(7), w["o0"][:, P * k:P * (k + 1)], w4[b][:, k, :],
                                       start=k == 0, stop=k == NG0 - 1)
                    mm.then_inc(s_proj[b], 1)

            for step, b, *at in steps:
                if step.startswith("norm_mean"):
                    pe.wait_ge(s_z[b], int(step[-1]) + 1)
                    pe.matmul(own(b, 0), center, z[b][:, :], start=True, stop=True).then_inc(s_cent[b], 1)
                if step.startswith("norm_var"):
                    pe.wait_ge(s_sq[b], int(step[-1]) + 1)
                    pe.matmul(own(b, 1), mean, sq[b][:, :], start=True, stop=True).then_inc(s_var[b], 1)
                for L in range(2):
                    q = qx[b] if L == 0 else qstack[b]
                    if step == f"cross_query{L}":
                        loaded(pe, "xq")
                        pe.wait_ge(s_x[b], 1 if L == 0 else 5)
                        pe.matmul(own(b, 0), w["xq"][:, P * L:P * (L + 1)], state(b),
                                  start=True, stop=True).then_inc(x_q[b], 1)
                    if step == f"cross_max{L}":
                        i, g = at
                        u = i * (HX[L] // G) + g
                        if u == 0:
                            pe.wait_ge(x_stack[b], L * FIRST["stack"] + 16 * NS)
                            pe.wait_ge(s_kx_stack, 2 * 16 * NS)
                        if u >= 2:
                            pe.wait_ge(x_mx[b], L * FIRST["mx"] + u - 1)
                        for k in range(G):
                            h = G * g + k
                            mm = pe.matmul(own(b, u % 2)[:, NKEY * k:NKEY * (k + 1)], q[:, h, P * i:P * (i + 1)],
                                           kx[L][:, h, NKEY * b:NKEY * (b + 1)], start=True, stop=True)
                        mm.then_inc(x_msc[b], 1)
                    if step == f"cross_rowmax{L}":
                        n = TT * HX[L]
                        pe.wait_ge(x_mx[b], L * FIRST["mx"] + TT * HX[L] // G)
                        pe.transpose(own(b, 2)[0:n, 0:P], mx[b][:, 0:n], ident).then_inc(x_mt[b], 1)
                    if step == f"cross_exp{L}":
                        h, = at
                        if h == 0:
                            pe.wait_ge(x_maug[b], L * FIRST["maug"] + 48)
                        if h < HX[L]:
                            if h >= 2:
                                pe.wait_ge(x_exp[b], L * FIRST["exp"] + h - 1)
                            pe.matmul(own(b, h % 2)[0:NKEY, :], kx[L][:, h, NKEY * b:NKEY * (b + 1)], q[:, h, :],
                                      start=True, stop=True).then_inc(x_sc[b], 1)
                        if h >= 2 and (h - 2) % G == G - 1:
                            g = (h - 2) // G
                            pv = h - 2
                        pv = h - 1
                        if 0 <= pv < HX[L]:
                            k = pv % G
                            pe.wait_ge(x_exp[b], L * FIRST["exp"] + pv + 1)
                            if k == 0 and pv:
                                pe.wait_ge(x_o[b], L * FIRST["o"] + pv // G)
                            pe.matmul(own(b, 2)[VW * k:VW * (k + 1), :], vx[L][:, b, pv, :],
                                      probs[0:NKEY, 2 * b + (pv % G) // 2, T * (pv % 2):T * (pv % 2 + 1)],
                                      start=True, stop=True, skip_group_check=True,
                                      tile_position=(0, VW * k)).then_inc(x_pv[b], 1)
                        if h >= 2 and (h - 2) % G == G - 1:
                            g = (h - 2) // G
                            pe.wait_ge(x_o[b], L * FIRST["o"] + g + 1)
                            if g:
                                pe.wait_ge(x_div[b], L * FIRST["div"] + g)
                            pe.matmul(own(b, 3), sel[DX[L]], sq[b][:, :], start=True, stop=True) \
                                .then_inc(x_den[b], 1)
                    if step == f"cross_out{L}":
                        ng = HX[L] // G
                        loaded(pe, "xo")
                        pe.wait_ge(x_div[b], L * FIRST["div"] + ng)
                        for k in range(ng):
                            c = P * (2 * L + k)
                            mm = pe.matmul(own(b, 0), w["xo"][:, c:c + P], w4[b][:, k, :],
                                           start=k == 0, stop=k == ng - 1)
                        mm.then_inc(x_out[b], 1)
                if step == "ffn_up":
                    loaded(pe, "ffn")
                    pe.wait_ge(s_x[b], 2)
                    for j in range(NF):
                        pe.matmul(own(b, j), w["ffn"][:, P * j:P * (j + 1)], qe[b][:, :],
                                  start=True, stop=True).then_inc(s_up[b], 1)
                if step == "ffn_down":
                    for j in range(NF):
                        pe.wait_ge(s_relu[b], max(j + 1, 1))
                        mm = pe.matmul(own(b, 0), w["ffn"][:, P * (NF + j):P * (NF + j + 1)], w4[b][:, j, :],
                                       start=j == 0, stop=j == NF - 1)
                    mm.then_inc(s_down[b], 1)
                if step == "route":
                    loaded(pe, "route")
                    pe.wait_ge(s_x[b], 3)
                    pe.matmul(own(b, 2)[0:1, 0:NE], xs[b][:, 1:2], w["route"][:, 0:NE],
                              start=True, stop=True).then_inc(s_rt[b], 1)
                if step == "expert_up":
                    for k in range(TOPK):
                        pe.wait_ge(s_pick[b], k + 1)
                        pe.matmul(own(b, k), work[b][:, MOE * k:MOE * k + P], state(b),
                                  start=True, stop=True).then_inc(s_eup[b], 1)
                if step == "expert_down":
                    for k in range(TOPK):
                        pe.wait_ge(s_egelu[b], k + 1)
                        mm = pe.matmul(own(b, 2), work[b][:, MOE * k + P:MOE * k + 2 * P], w4[b][:, k, :],
                                       start=k == 0, stop=k == TOPK - 1)
                    mm.then_inc(s_edown[b], 1)
                if step == "mix_in":
                    pe.wait_ge(s_wmix, 6)
                    pe.wait_ge(s_x[b], 4)
                    for i in range(3):
                        pe.matmul(own(b, i), wmix[i][:, 0, :], state(b), start=True, stop=False)
                        pe.matmul(own(b, i), wmix[i][:, 1, :], xs[b][:, 0:T], start=False, stop=True) \
                            .then_inc(s_rk[b], 1)
                if step == "mix_out":
                    pe.wait_ge(s_rscan[b], MIX_DVE)
                    pe.matmul(own(b, 3), w["mix"][:, 3 * P:4 * P], scratch[b][:, 7, :],
                              start=True, stop=True).then_inc(s_rout[b], 1)
                if step == "gate":
                    loaded(pe, "gate")
                    pe.wait_ge(s_x[b], 6)
                    for j in range(NF):
                        if j >= 2:
                            pe.wait_ge(s_gs[b], j - 1)
                        pe.matmul(own(b, 2 * j % 4), w["gate"][:, P * j:P * (j + 1)], state(b),
                                  start=True, stop=True).then_inc(s_ga[b], 1)
                        if j >= 2:
                            pe.wait_ge(s_gh[b], j - 1)
                        pe.matmul(own(b, (2 * j + 1) % 4), w["gate"][:, P * (NF + j):P * (NF + j + 1)], state(b),
                                  start=True, stop=True).then_inc(s_gb[b], 1)
                for i, (name, src, ready, done, free) in enumerate((
                        ("hidden1", 0, s_gh, s_h1, s_gh), ("hidden2", 4, s_g1, s_h2, s_g1))):
                    if step == name:
                        pe.wait_ge(s_wh, 32)
                        for j in range(NF):
                            if j == 0:
                                pe.wait_ge(ready[b], NF)
                            for k in range(NF):
                                mm = pe.matmul(own(b, j), wh[i][:, k, P * j:P * (j + 1)],
                                               scratch[b][:, src + k, :], start=k == 0, stop=k == NF - 1)
                            mm.then_inc(done[b], 1)
                if step == "down":
                    pe.wait_ge(s_g2[b], NF)
                    for k in range(NF):
                        mm = pe.matmul(own(b, 0), w["gate"][:, P * (2 * NF + k):P * (2 * NF + k + 1)],
                                       w4[b][:, k, :], start=k == 0, stop=k == NF - 1)
                    mm.then_inc(s_dn[b], 1)

        @block.scalar
        def _(act):
            def value_and_first(src, dst, first, bias, scale=1.0):
                if bias is None:
                    act.activation(dst, src, ACT.Copy, scale=scale)
                    return act.activation(first, src, ACT.Copy, scale=scale)
                act.activation(dst, src, ACT.Identity, bias=bias)
                return act.activation(first, src, ACT.Identity, bias=bias)

            def reciprocal(src, dst, chain, done):
                act.activation(dst, src, ACT.Ln).then_inc(chain, 1)
                act.wait_ge(chain, done + 1)
                act.activation(dst, dst, ACT.Exp, scale=-1.0).then_inc(chain, 1)

            act.preload_act_table_set(LN_EXP)
            loaded(act, "cols")
            act.activation(decay[:, 0:1], col["decay"], ACT.Exp).then_inc(s_small, 1)
            act.activation(keep[:, 0:1], col["lambda"], ACT.Exp, scale=-1.0).then_inc(s_small, 1)
            for u in range(2 * NB):
                act.wait_ge(s_qk, u + 1)
                value, _, parts = (q_split, k_split)[u % 2][u // 2]
                value_and_first(bank(u), value, parts[:, 0, :], col["bq" if u % 2 == 0 else "bk"]) \
                    .then_inc(s_qk_val, 1)
            for L in range(2):
                act.wait_ge(s_kx, L + 1)
                value, _, parts = kx_split[L]
                value_and_first(psum[:, 6 + L, 0:NB * NKEY], value, parts[:, 0, :],
                                None if L == 0 else col["xbk"]).then_inc(s_kx_val, 1)

            for kind, n, j in items:
                b = n // NG0
                if kind == "rowmax":
                    act.wait_ge(s_mt, n + 1)
                    if n >= 2:
                        act.wait_ge(s_maug, 48 * (n - 1))
                    o = bank(4 + ((NM + 1) * (n + 1) + 2) % 2)[0:G * TT, 0:P]
                    value_and_first(o, mt[n % 2][0:G * TT, 0, :], mp[n % 2][0:G * TT, 0, :], None, -1.0) \
                        .then_inc(s_mval, 1)
                if kind == "score":
                    v = NX * n + j
                    act.wait_ge(s_sc, v + 1)
                    if v == 0:
                        act.wait_ge(s_kx_stack, 2 * 16 * NS)
                    if v >= 4:
                        act.wait_ge(s_pv, v - 3)
                    act.activation(probs[:, v % 4, :], psum[:, 2 * (v % 2):2 * (v % 2) + 2, :]
                                   .rearrange("p a c -> p (a c)"), ACT.Exp, scale=float(D0) ** -0.5) \
                        .then_inc(s_exp, 1)
                if kind == "denominator":
                    act.wait_ge(s_den, n + 1)
                    if n >= 1:
                        act.wait_ge(s_div, n)
                    reciprocal(bank(7), rstd[b][:, :], s_rec, 2 * n)
                if kind == "values" and j == 4:
                    act.wait_ge(s_pv, NX * (n + 1))
                    if n >= 1:
                        act.wait_ge(s_div, n)
                    act.copy(sq[b][:, :], bank(6)).then_inc(s_o, 1)

            for step, b, *at in steps:
                if step.startswith("norm_mean"):
                    act.wait_ge(s_cent[b], int(step[-1]) + 1)
                    act.activation(sq[b][:, :], own(b, 0), ACT.Square).then_inc(s_sq[b], 1)
                if step.startswith("norm_var"):
                    n = int(step[-1])
                    if b == 0:
                        act.preload_act_table_set(LN_EXP)
                    act.wait_ge(s_var[b], n + 1)
                    if n == 0:
                        act.wait_ge(s_vzero, 2)
                    act.activation(rstd[b][:, :], own(b, 1), ACT.Ln, bias=eps[:, 0:1]).then_inc(s_ln[b], 1)
                    act.wait_ge(s_ln[b], n + 1)
                    act.activation(rstd[b][:, :], rstd[b][:, :], ACT.Exp, scale=-0.5).then_inc(s_rstd[b], 1)
                for L in range(2):
                    if step == f"cross_query{L}":
                        act.wait_ge(x_q[b], L * FIRST["q"] + 1)
                        value, _, parts = q_split[b]
                        value_and_first(own(b, 0), value, parts[:, 0, :], None if L == 0 else col["xbq"]) \
                            .then_inc(x_val[b], 1)
                    if step == f"cross_rowmax{L}":
                        n = TT * HX[L]
                        act.wait_ge(x_mt[b], L * FIRST["mt"] + 1)
                        value_and_first(own(b, 2)[0:n, 0:P], mt[b][0:n, 0, :], mp[b][0:n, 0, :], None, -1.0) \
                            .then_inc(x_mval[b], 1)
                    if step == f"cross_exp{L}":
                        h, = at
                        if h < HX[L]:
                            act.wait_ge(x_sc[b], L * FIRST["sc"] + h + 1)
                            if h >= G:
                                act.wait_ge(x_pv[b], L * FIRST["pv"] + h - G + 1)
                            act.activation(probs[0:NKEY, 2 * b + (h % G) // 2, T * (h % 2):T * (h % 2 + 1)],
                                           own(b, h % 2)[0:NKEY, :], ACT.Exp, scale=float(DX[L]) ** -0.5) \
                                .then_inc(x_exp[b], 1)
                        if h >= 2 and (h - 2) % G == G - 1:
                            g = (h - 2) // G
                            act.wait_ge(x_den[b], L * FIRST["den"] + g + 1)
                            if g:
                                act.wait_ge(x_div[b], L * FIRST["div"] + g)
                            reciprocal(own(b, 3), rstd[b][:, :], x_rec[b], 2 * (L * FIRST["den"] + g))
                        if h >= 1 and (h - 1) % G == G - 1:
                            g = (h - 1) // G
                            act.wait_ge(x_pv[b], L * FIRST["pv"] + G * (g + 1))
                            if g:
                                act.wait_ge(x_div[b], L * FIRST["div"] + g)
                            act.copy(sq[b][:, :], own(b, 2)).then_inc(x_o[b], 1)
                if step == "ffn_up":
                    for j in range(NF):
                        act.wait_ge(s_up[b], j + 1)
                        act.activation(w4[b][:, j, :], own(b, j), ACT.Relu, bias=col["ffn_b1"][:, j:j + 1]) \
                            .then_inc(s_relu[b], 1)
                if step == "expert_up":
                    for k in range(TOPK):
                        act.wait_ge(s_eup[b], k + 1)
                        act.activation(w4[b][:, k, :], own(b, k), ACT.Gelu,
                                       bias=work[b][:, MOE * k + 2 * P:MOE * k + 2 * P + 1]).then_inc(s_egelu[b], 1)
                if step == "mix_in":
                    for i in range(3):
                        act.wait_ge(s_rk[b], i + 1)
                        if i < 2:
                            act.copy(scratch[b][:, i, :], own(b, i)).then_inc(s_rcp[b], 1)
                        else:
                            act.activation(scratch[b][:, 6, :], own(b, i), ACT.Sigmoid) \
                                .then_inc(s_rcp[b], 1)
                if step == "mix_scan":
                    s = scratch[b]
                    act.wait_ge(s_rscan[b], 5)
                    if b == 0:
                        act.preload_act_table_set(LN_EXP)
                    act.activation(s[:, 2:4, :], s[:, 2:4, :], ACT.Exp).then_inc(s_rexp[b], 1)
                    act.wait_ge(s_rpool[b], 1)
                    act.wait_ge(s_rscan[b], 6)
                    act.activation(s[:, 4:6, :], s[:, 4:6, :], ACT.Exp).then_inc(s_rexp[b], 1)
                if step == "mix_divide":
                    s = scratch[b]
                    act.wait_ge(s_rscan[b], 11)
                    reciprocal(s[:, 2, :], s[:, 3, :], s_rexp[b], 2)
                if step == "gate":
                    for j in range(NF):
                        act.wait_ge(s_ga[b], j + 1)
                        act.activation(w4[b][:, j, :], own(b, 2 * j % 4), ACT.Silu,
                                       scale=col["w1_s"][:, j:j + 1]).then_inc(s_gs[b], 1)
                for name, dst, ready, scale, done in (
                        ("hidden1", [scratch[b][:, 4 + j, :] for j in range(NF)], s_h1, "h1_s", s_g1),
                        ("hidden2", [w4[b][:, j, :] for j in range(NF)], s_h2, "h2_s", s_g2)):
                    if step == name:
                        for j in range(NF):
                            act.wait_ge(ready[b], j + 1)
                            act.activation(dst[j], own(b, j), ACT.Gelu, scale=col[scale][:, j:j + 1]) \
                                .then_inc(done[b], 1)

        @block.vector
        def _(dve):
            def split_rest(value, rest, parts, chain, done):
                dve.tensor_tensor(rest, value, parts[:, 0, :], ALU.subtract).then_inc(chain, 1)
                dve.wait_ge(chain, done + 1)
                dve.tensor_copy(parts[:, 1, :], rest).then_inc(chain, 1)
                dve.wait_ge(chain, done + 2)
                dve.tensor_tensor(parts[:, 2, :], rest, parts[:, 1, :], ALU.subtract).then_inc(chain, 1)

            for b in range(NB):
                if b == 1:
                    dve.memset(eps[:, :], EPS)
                dve.memset(qstack[b][:, :, :].rearrange("p h t -> p (h t)").bitcast(F32), 0.0).then_inc(s_vzero, 1)
                if b == 0:
                    for u in range(2):
                        dve.wait_ge(s_qk_val, u + 1)
                        split_rest(*(q_split, k_split)[u][0], s_qk_split, 3 * u)
            for u in range(2, 4):
                dve.wait_ge(s_qk_val, u + 1)
                split_rest(*(q_split, k_split)[u % 2][1], s_qk_split, 3 * u)
            dve.wait_ge(s_zero, 12)
            for b in range(NB):
                dve.wait_ge(s_v0, b + 1)
                dve.tensor_copy(v0[:, b, :, :, 0:D0].rearrange("p k h d -> p (k h) d"),
                                bank(4 + b).rearrange("p (k d) -> p k d", d=D0)).then_inc(s_v0_out, 1)
            for L in range(2):
                dve.wait_ge(s_kx_val, L + 1)
                split_rest(*kx_split[L], s_kx_split, 3 * L)
            dve.wait_ge(s_vx, 1)
            for L in range(2):
                for b in range(NB):
                    o = psum[0:NKEY, 4, P * (2 * L + b):P * (2 * L + b + 1)]
                    dve.tensor_copy(vx[L][:, b, :, 0:DX[L]], o.rearrange("p (h d) -> p h d", d=DX[L])) \
                        .then_inc(s_vx_out, 1)
            dve.wait_ge(s_small, 2)
            dve.tensor_scalar(keep[:, 1:2], keep[:, 0:1], 1.0, None, ALU.add).then_inc(s_param, 1)
            dve.wait_ge(s_param, 1)
            dve.reciprocal(keep[:, 0:1], keep[:, 1:2]).then_inc(s_param, 1)
            dve.wait_ge(s_param, 2)
            dve.tensor_scalar(keep[:, 2:3], keep[:, 0:1], -1.0, 1.0, ALU.mult, ALU.add).then_inc(s_param, 1)
            dve.tensor_scalar(decay[:, 1:2], decay[:, 0:1], -1.0, None, ALU.mult).then_inc(s_param, 1)
            dve.tensor_scalar(omm[:, :], col["mix"], -1.0, 1.0, ALU.mult, ALU.add).then_inc(s_param, 1)
            for b in range(NB):
                dve.memset(xs[b][:, 0:1], 0.0).then_inc(s_param, 1)

            for kind, n, j in items:
                b, g = n // NG0, n % NG0
                if kind == "max":
                    i, h0, nh = MAX_UNITS[j]
                    if n >= 2 and j == 0:
                        dve.wait_ge(s_mt, n - 1)
                    dve.wait_ge(s_msc, NM * n + j + 1)
                    e = (NM + 1) * n + (j if j < 2 else j + 1)
                    width = P * (i + 1)
                    src = bank(4 + e % 2)[:, 0:nh * width].rearrange("p (h k) -> p h k", h=nh)
                    dve.tensor_reduce(mx[n % 2][:, TT * h0 + i:TT * (h0 + nh - 1) + i + 1:TT], src, AX.X, ALU.max) \
                        .then_inc(s_mx, 1)
                if kind == "rowmax":
                    dve.wait_ge(s_mval, n + 1)
                    split_rest(mt[n % 2][0:G * TT, 0, :], mt[n % 2][0:G * TT, 1, :], mp[n % 2][0:G * TT],
                               s_msplit, 3 * n)
                if kind == "denominator":
                    dve.wait_ge(s_rec, 2 * (n + 1))
                    dve.tensor_tensor(w4[b][:, g, :], sq[b][:, :], rstd[b][:, :], ALU.mult).then_inc(s_div, 1)
                if kind == "project":
                    b = n
                    dve.wait_ge(s_proj[b], 1)
                    dve.scalar_tensor_tensor(out=z[b][:, :], in0=bank(7), scalar=col["bo"], in1=state(b),
                                             op0=ALU.add, op1=ALU.add).then_inc(s_z[b], 1)

            for step, b, *at in steps:
                if step.startswith("norm_var"):
                    n = int(step[-1])
                    dve.wait_ge(s_rstd[b], n + 1)
                    if n in (1, 2):
                        dst = qe[b] if n == 1 else z[b]
                        dve.scalar_tensor_tensor(out=dst[:, :], in0=own(b, 0), scalar=col[f"ln{n}_g"],
                                                 in1=rstd[b][:, :], op0=ALU.mult, op1=ALU.mult) \
                            .then_inc(s_aff[b], 1)
                        dve.wait_ge(s_aff[b], n)
                        if n == 1:
                            dve.tensor_scalar(qe[b][:, :], qe[b][:, :], col["ln1_b"], None, ALU.add) \
                                .then_inc(s_x[b], 1)
                        else:
                            dve.scalar_tensor_tensor(out=z[b][:, :], in0=z[b][:, :], scalar=col["ln2_b"],
                                                     in1=state(b), op0=ALU.add, op1=ALU.add) \
                                .then_inc(s_z[b], 1)
                    else:
                        dve.tensor_tensor(state(b), own(b, 0), rstd[b][:, :], ALU.mult).then_inc(s_x[b], 1)
                for L in range(2):
                    if step == f"cross_query{L}":
                        dve.wait_ge(x_val[b], L * FIRST["val"] + 1)
                        split_rest(*q_split[b], x_split[b], L * FIRST["split"])
                    if step == f"cross_max{L}":
                        i, g = at
                        u = i * (HX[L] // G) + g
                        dve.wait_ge(x_msc[b], L * FIRST["msc"] + u + 1)
                        src = own(b, u % 2)[:, 0:G * NKEY].rearrange("p (h k) -> p h k", h=G)
                        dve.tensor_reduce(mx[b][:, TT * G * g + i:TT * (G * (g + 1) - 1) + i + 1:TT], src, AX.X, ALU.max) \
                            .then_inc(x_mx[b], 1)
                    if step == f"cross_rowmax{L}":
                        n = TT * HX[L]
                        dve.wait_ge(x_mval[b], L * FIRST["mval"] + 1)
                        split_rest(mt[b][0:n, 0, :], mt[b][0:n, 1, :], mp[b][0:n], x_msplit[b], L * FIRST["msplit"])
                    if step == f"cross_exp{L}":
                        h, = at
                        if h >= 2 and (h - 2) % G == G - 1:
                            g = (h - 2) // G
                            dve.wait_ge(x_rec[b], 2 * (L * FIRST["den"] + g + 1))
                            if L == 0:
                                dve.scalar_tensor_tensor(out=w4[b][:, g, :], in0=sq[b][:, :], scalar=keep[:, 2:3],
                                                         in1=rstd[b][:, :], op0=ALU.mult, op1=ALU.mult) \
                                    .then_inc(x_div[b], 1)
                            else:
                                dve.tensor_tensor(w4[b][:, g, :], sq[b][:, :], rstd[b][:, :], ALU.mult) \
                                    .then_inc(x_div[b], 1)
                    if step == f"cross_out{L}":
                        dve.wait_ge(x_out[b], L * FIRST["out"] + 1)
                        if L == 0:
                            dve.tensor_tensor(z[b][:, :], own(b, 0), state(b), ALU.add).then_inc(s_z[b], 1)
                        else:
                            dve.scalar_tensor_tensor(out=z[b][:, :], in0=own(b, 0), scalar=col["xbo"],
                                                     in1=state(b), op0=ALU.add, op1=ALU.add).then_inc(s_z[b], 1)
                if step == "ffn_down":
                    dve.wait_ge(s_down[b], 1)
                    dve.scalar_tensor_tensor(out=z[b][:, :], in0=own(b, 0), scalar=col["ffn_b2"],
                                             in1=qe[b][:, :], op0=ALU.add, op1=ALU.add).then_inc(s_z[b], 1)
                if step == "route":
                    r = route[b]
                    dve.wait_ge(s_rt[b], 1)
                    dve.tensor_tensor(r[:, 0:NE], own(b, 2)[0:1, 0:NE], w["route"][0:1, NE:2 * NE], ALU.add) \
                        .then_inc(s_rchain[b], 1)
                    dve.wait_ge(s_rchain[b], 1)
                    dve.max(r[:, NE:2 * NE], r[:, 0:NE]).then_inc(s_rchain[b], 1)
                    dve.wait_ge(s_rchain[b], 2)
                    dve.max_index(choice[b][:, :], r[:, NE:2 * NE], r[:, 0:NE]).then_inc(s_choice[b], 1)
                if step == "expert_down":
                    dve.wait_ge(s_edown[b], 1)
                    dve.wait_ge(s_b2s[b], 3)
                    dve.scalar_tensor_tensor(out=z[b][:, :], in0=own(b, 2), scalar=1.0 / TOPK, in1=qe[b][:, :],
                                             op0=ALU.mult, op1=ALU.add).then_inc(s_z[b], 1)
                if step == "mix_in":
                    s, (pp, aa, bb) = scratch[b], carried(wide[b])
                    for t, v in ((pp, NEG), (aa, 0.0), (bb, 0.0)):
                        ins = dve.memset(t[:, 0:1], v)
                    ins.then_inc(s_rscan[b], 1)
                    dve.wait_ge(s_rscan[b], 1)
                    dve.wait_ge(s_rcp[b], 1)
                    dve.tensor_tensor_scan(pp[:, 1:T + 1], decay[:, 1:2].broadcast_to([P, T]), s[:, 0, :], NEG,
                                           ALU.add, ALU.max).then_inc(s_rscan[b], 1)
                    dve.wait_ge(s_rscan[b], 2)
                    dve.scalar_tensor_tensor(out=s[:, 7, :], in0=s[:, 0, :], scalar=col["first"], in1=pp[:, 0:T],
                                             op0=ALU.add, op1=ALU.max).then_inc(s_rscan[b], 1)
                    dve.scalar_tensor_tensor(out=s[:, 2, :], in0=pp[:, 0:T], scalar=decay[:, 1:2],
                                             in1=pp[:, 1:T + 1], op0=ALU.add, op1=ALU.subtract) \
                        .then_inc(s_rscan[b], 1)
                    dve.wait_ge(s_rscan[b], 4)
                    dve.tensor_tensor(s[:, 3, :], s[:, 0, :], pp[:, 1:T + 1], ALU.subtract).then_inc(s_rscan[b], 1)
                    dve.scalar_tensor_tensor(out=s[:, 5, :], in0=s[:, 0, :], scalar=col["first"], in1=s[:, 7, :],
                                             op0=ALU.add, op1=ALU.subtract).then_inc(s_rscan[b], 1)
                if step == "mix_scan":
                    s, (pp, aa, bb) = scratch[b], carried(wide[b])
                    dve.wait_ge(s_rexp[b], 1)
                    dve.tensor_tensor_scan(bb[:, 1:T + 1], s[:, 2, :], s[:, 3, :], 0.0, ALU.mult, ALU.add) \
                        .then_inc(s_rscan[b], 1)
                    dve.wait_ge(s_rpool[b], 2)
                    dve.tensor_tensor_scan(aa[:, 1:T + 1], s[:, 2, :], s[:, 7, :], 0.0, ALU.mult, ALU.add) \
                        .then_inc(s_rscan[b], 1)
                    dve.wait_ge(s_rscan[b], 8)
                    dve.wait_ge(s_rexp[b], 2)
                    dve.tensor_tensor(s[:, 2, :], s[:, 4, :], bb[:, 0:T], ALU.mult).then_inc(s_rscan[b], 1)
                    dve.tensor_tensor(s[:, 0, :], s[:, 4, :], aa[:, 0:T], ALU.mult).then_inc(s_rscan[b], 1)
                    dve.wait_ge(s_rscan[b], 9)
                    dve.tensor_tensor(s[:, 2, :], s[:, 2, :], s[:, 5, :], ALU.add).then_inc(s_rscan[b], 1)
                    dve.wait_ge(s_rscan[b], 10)
                    dve.wait_ge(s_rpool[b], 3)
                    dve.wait_ge(s_rcp[b], 3)
                    dve.tensor_tensor(s[:, 0, :], s[:, 0, :], s[:, 1, :], ALU.add).then_inc(s_rscan[b], 1)
                    dve.wait_ge(s_rscan[b], 12)
                    dve.tensor_tensor(s[:, 0, :], s[:, 0, :], s[:, 6, :], ALU.mult).then_inc(s_rscan[b], 1)
                if step == "mix_divide":
                    s = scratch[b]
                    dve.wait_ge(s_rexp[b], 4)
                    dve.wait_ge(s_rscan[b], 13)
                    dve.tensor_tensor(s[:, 7, :], s[:, 0, :], s[:, 3, :], ALU.mult).then_inc(s_rscan[b], 1)
                if step == "mix_out":
                    dve.wait_ge(s_rout[b], 1)
                    dve.tensor_tensor(z[b][:, :], own(b, 3), state(b), ALU.add).then_inc(s_z[b], 1)
                if step == "gate":
                    for j in range(NF):
                        dve.wait_ge(s_gb[b], j + 1)
                        dve.wait_ge(s_gs[b], j + 1)
                        dve.scalar_tensor_tensor(out=scratch[b][:, j, :], in0=own(b, (2 * j + 1) % 4),
                                                 scalar=col["w2_s"][:, j:j + 1], in1=w4[b][:, j, :],
                                                 op0=ALU.mult, op1=ALU.mult).then_inc(s_gh[b], 1)
                if step == "down":
                    dve.wait_ge(s_dn[b], 1)
                    dve.scalar_tensor_tensor(out=z[b][:, :], in0=own(b, 0), scalar=col["w3_s"], in1=state(b),
                                             op0=ALU.mult, op1=ALU.add).then_inc(s_z[b], 1)

        @block.gpsimd
        def _(pool):
            def fill(stack, first, end, value):
                return pool.memset(stack[first:end, :, :].rearrange("p h t -> p (h t)").bitcast(F32), value)

            fill(kstack[0], 32, 64, ONES).then_inc(s_zero, 1)
            pool.wait_ge(s_zero, 1)
            fill(kstack[0], 64, P, 0.0).then_inc(s_zero, 1)
            loaded(pool, "const")
            pool.wait_ge(s_zero, 2)
            pool.tensor_copy(ident_b[:, :], ident)
            pool.tensor_copy(mask_b[:, :], w["const"][:, 6 * P:7 * P]).then_inc(s_zero, 1)
            pool.wait_ge(s_zero, 3)
            fill(kx[0], 96, P, ONES).then_inc(s_zero, 1)
            pool.wait_ge(s_zero, 4)
            fill(kx[1], 32, 64, 0.0).then_inc(s_zero, 1)
            pool.wait_ge(s_zero, 5)
            fill(kx[1], 64, P, ONES).then_inc(s_zero, 1)
            pool.wait_ge(s_zero, 6)
            fill(kstack[1], 32, 64, ONES).then_inc(s_zero, 1)
            pool.wait_ge(s_zero, 7)
            fill(kstack[1], 64, P, 0.0).then_inc(s_zero, 1)
            pool.wait_ge(s_zero, 8)
            pool.memset(v0[:, :, :, :, :].rearrange("p b k h c -> p (b k h c)"), 0.0).then_inc(s_zero, 1)
            pool.wait_ge(s_zero, 9)
            pool.memset(v0[:, :, :, :, D0:D0 + 1].rearrange("p b k h c -> p (b k h) c"), 1.0).then_inc(s_zero, 1)
            pool.wait_ge(s_zero, 10)
            for L in range(2):
                last = pool.memset(vx[L][:, :, :, :], 0.0)
            last.then_inc(s_zero, 1)
            pool.wait_ge(s_zero, 11)
            for L in range(2):
                last = pool.memset(vx[L][:, :, :, DX[L]:DX[L] + 1], 1.0)
            last.then_inc(s_zero, 1)
            pool.wait_ge(s_zero, 12)

            for kind, n, j in items:
                if kind == "score":
                    v = NX * n + j
                    pool.wait_ge(s_exp, v + 1)
                    for c, step, m in DIAGONALS[j]:
                        last = diagonal(pool, probs[:, v % 4, :], c, step, m)
                    last.then_inc(s_mask, 1)

            loaded(pool, "mix")
            pool.wait_ge(s_param, 5)
            for i in range(3):
                wi = w["mix"][:, P * i:P * (i + 1)]
                pool.tensor_scalar(wmix[i][:, 0, :], wi, col["mix"][:, i:i + 1], None, ALU.mult).then_inc(s_wmix, 1)
                pool.tensor_scalar(wmix[i][:, 1, :], wi, omm[:, i:i + 1], None, ALU.mult).then_inc(s_wmix, 1)
            loaded(pool, "moe")

            for step, b, *at in steps:
                if step == "route":
                    pool.wait_ge(s_choice[b], 1)
                    for k in range(TOPK):
                        e = pool.value_load(choice[b][0:1, k:k + 1], min_val=0, max_val=NE - 1)
                        pool.tensor_copy(work[b][:, MOE * k:MOE * (k + 1)],
                                         w["moe"][:, bass.ds(e * MOE, MOE)]).then_inc(s_pick[b], 1)
                    pool.wait_ge(s_pick[b], TOPK)
                    pool.tensor_tensor(b2s[b][:, 0:1], work[b][:, MOE - 1:MOE], work[b][:, 2 * MOE - 1:2 * MOE],
                                       ALU.add).then_inc(s_b2s[b], 1)
                    pool.wait_ge(s_b2s[b], 1)
                    pool.tensor_scalar(b2s[b][:, 1:2], b2s[b][:, 0:1], 1.0 / TOPK, None, ALU.mult) \
                        .then_inc(s_b2s[b], 1)
                    pool.wait_ge(s_b2s[b], 2)
                    pool.tensor_scalar(qe[b][:, :], state(b), b2s[b][:, 1:2], None, ALU.add).then_inc(s_b2s[b], 1)
                if step == "mix_in":
                    s, (pp, _, _) = scratch[b], carried(wide[b])
                    pool.wait_ge(s_rscan[b], 3)
                    pool.tensor_tensor(s[:, 4, :], pp[:, 0:T], s[:, 7, :], ALU.subtract).then_inc(s_rpool[b], 1)
                if step == "mix_scan":
                    s = scratch[b]
                    pool.wait_ge(s_rexp[b], 1)
                    pool.wait_ge(s_rscan[b], 6)
                    pool.wait_ge(s_rpool[b], 1)
                    pool.wait_ge(s_rcp[b], 2)
                    pool.tensor_tensor(s[:, 7, :], s[:, 3, :], s[:, 1, :], ALU.mult).then_inc(s_rpool[b], 1)
                    pool.wait_ge(s_rpool[b], 2)
                    pool.wait_ge(s_rexp[b], 2)
                    pool.tensor_tensor(s[:, 1, :], s[:, 5, :], s[:, 1, :], ALU.mult).then_inc(s_rpool[b], 1)


MIX_DVE = 14
MOE = 2 * P + 2


def carried(area):
    return [area[:, (T + 1) * i:(T + 1) * (i + 1)] for i in range(3)]


def diagonal(pool, probs, c, step, m):
    size = step * m
    base = 0 if c == 0 else c
    view = probs.rearrange("p (m s) -> p m s", s=step)[:, 0:m, base:base + P]
    assert size <= 1024
    return pool.affine_select(out=view, in_=view, compare_op=ALU.is_ge, fill=0.0, base=0,
                              pattern=[[0, m], [1, P]], channel_multiplier=-1)


_COLS = [("bq", 1), ("bk", 1), ("bo", 1), ("ln1_g", 1), ("ln1_b", 1), ("ln2_g", 1), ("ln2_b", 1), ("ffn_b1", NF),
         ("ffn_b2", 1), ("lambda", 1), ("decay", 1), ("first", 1), ("mix", 3), ("xbq", 1), ("xbk", 1), ("xbo", 1),
         ("w1_s", NF), ("w2_s", NF), ("h1_s", NF), ("h2_s", NF), ("w3_s", 1)]
COLS, _at = [], 0
for _name, _n in _COLS:
    COLS.append((_name, _at, _n))
    _at += _n
NCOL = _at

LOADS = {
    "x": ([P, NB * T], F32), "qk": ([P, 2 * P], F32), "cols": ([P, NCOL], F32), "const": ([P, 7 * P], F32),
    "v0": ([P, 2 * P], F32), "ctx": ([P, NB * NKEY], F32), "xkv": ([P, 4 * P], F32), "xbv": ([1, P], F32),
    "o0": ([P, NG0 * P], F32), "xq": ([P, 2 * P], F32), "xo": ([P, 6 * P], F32), "ffn": ([P, 2 * NF * P], F32),
    "route": ([P, 2 * NE], F32), "moe": ([P, NE * MOE], F32), "mix": ([P, 4 * P], F32),
    "gate": ([P, 3 * NF * P], F32), "h1": ([P, NF, NF * P], F32), "h2": ([P, NF, NF * P], F32),
}
LOAD_GROUPS = {"x": ["x"], "qk": ["qk"], "cols": ["cols"], "const": ["const"],
               "context": ["v0", "ctx", "xkv", "xbv"], "project": ["o0", "xq", "xo"],
               "ffn": ["ffn", "route", "moe"], "mix": ["mix", "gate"]}


def laid_out(i):
    import numpy as np

    i = {k: np.asarray(v) for k, v in i.items()}

    def by_feature(a, heads):
        return a.reshape(*a.shape[:-1], heads, -1).swapaxes(-1, -2).reshape(a.shape)

    def column(a, n=1):
        return np.broadcast_to(a, (P,)).reshape(P, 1) if a.ndim == 0 else a.reshape(n, P).T

    def padded(wo, d):
        g = wo.reshape(-1, G, d, P)
        out = np.zeros((g.shape[0], G, VW, P), np.float32)
        out[:, :, :d] = g
        return out.reshape(-1, P, P).transpose(1, 0, 2).reshape(P, -1)

    def in_rows(a):
        return a.reshape(-1, P, a.shape[-1]).transpose(1, 0, 2).reshape(P, -1)

    out = {}
    out["x"] = i["x"].transpose(2, 0, 1).reshape(P, NB * T)
    wq, wk, wv = np.split(i["L0_attn_w_attn"].T, 3, axis=1)
    bq, bk, bv = np.split(i["L0_attn_b_attn"], 3)
    out["qk"] = np.concatenate([by_feature(wq, H0), by_feature(wk, H0)], 1)
    row = np.zeros((P, P), np.float32)
    row[0] = bv
    out["v0"] = np.concatenate([wv, row], 1)
    out["ctx"] = i["ctx_1024"].transpose(2, 0, 1).reshape(P, NB * NKEY)
    out["xkv"] = np.concatenate([by_feature(i["L0_xattn_Wk"], HX[0]), i["L0_xattn_Wv"],
                                 by_feature(i["L1_xattn_Wk"], HX[1]), i["L1_xattn_Wv"]], 1)
    out["xbv"] = i["L1_xattn_bv"].reshape(1, P)
    out["o0"] = padded(i["L0_attn_w_proj"].T, D0)
    out["xq"] = np.concatenate([by_feature(i["L0_xattn_Wq"], HX[0]), by_feature(i["L1_xattn_Wq"], HX[1])], 1)
    out["xo"] = np.concatenate([padded(i["L0_xattn_Wo"], DX[0]), padded(i["L1_xattn_Wo"], DX[1])], 1)
    out["ffn"] = np.concatenate([i["L0_xattn_ffn_w1"], in_rows(i["L0_xattn_ffn_w2"])], 1)
    br = np.zeros((P, NE), np.float32)
    br[0] = i["L0_ffn_br"]
    out["route"] = np.concatenate([i["L0_ffn_Wr"], br], 1)
    out["moe"] = np.concatenate([i["L0_ffn_W1"], i["L0_ffn_W2"], i["L0_ffn_b1"][:, :, None],
                                 i["L0_ffn_b2"][:, :, None]], 2).transpose(1, 0, 2).reshape(P, -1)
    out["mix"] = np.concatenate([i[f"L1_attn_W{k}"].T for k in "kvro"], 1)
    out["gate"] = np.concatenate([i["L1_ffn_w1_w"].T, i["L1_ffn_w2_w"].T, in_rows(i["L1_ffn_w3_w"].T)], 1)
    for k in ("h1", "h2"):
        out[k] = in_rows(i[f"L1_ffn_{k}_w"].T).reshape(P, NF, NF * P)
    mix = np.stack([i[f"L1_attn_time_mix_{k}"].reshape(P) for k in "kvr"], 1)
    cols = {
        "bq": by_feature(bq, H0), "bk": by_feature(bk, H0), "bo": i["L0_attn_b_proj"],
        "ln1_g": i["L0_xattn_ln1_g"], "ln1_b": i["L0_xattn_ln1_b"], "ln2_g": i["L0_xattn_ln2_g"],
        "ln2_b": i["L0_xattn_ln2_b"], "ffn_b1": i["L0_xattn_ffn_b1"], "ffn_b2": i["L0_xattn_ffn_b2"],
        "lambda": i["L0_xattn_lambda_param"], "decay": i["L1_attn_time_decay"], "first": i["L1_attn_time_first"],
        "xbq": by_feature(i["L1_xattn_bq"], HX[1]), "xbk": by_feature(i["L1_xattn_bk"], HX[1]),
        "xbo": i["L1_xattn_bo"], "w1_s": i["L1_ffn_w1_s"], "w2_s": i["L1_ffn_w2_s"], "h1_s": i["L1_ffn_h1_s"],
        "h2_s": i["L1_ffn_h2_s"], "w3_s": i["L1_ffn_w3_s"],
    }
    out["cols"] = np.concatenate([mix if n == "mix" else column(cols[n], k) for n, _, k in COLS], 1)

    eye = np.eye(P, dtype=np.float32)
    quad = np.kron(np.eye(G, dtype=np.float32), np.ones((VW, VW), np.float32))
    p = np.arange(P)
    const = [eye - 1.0 / P, np.full((P, P), 1.0 / P), eye]
    const += [quad * (p % VW == d)[:, None] for d in (8, 16)]
    const += [np.ones((P, P)), np.where(p[None, :] > p[:, None], -1e30, 0.0)]
    out["const"] = np.concatenate(const, 1).astype(np.float32)
    return out


def kernel(**inputs):
    import numpy as np
    import concourse.bacc as bacc
    from concourse.bass_utils import run_bass_kernel_spmd

    nc = bacc.Bacc("TRN2", target_bir_lowering=False, num_devices=1)
    arrays, dram = {}, {}
    for name, a in laid_out(inputs).items():
        a = np.ascontiguousarray(a)
        arrays[f"in_{name}"] = a
        dram[name] = nc.dram_tensor(f"in_{name}", a.shape, mybir.dt.from_np(a.dtype), kind="ExternalInput").ap()
    out = nc.dram_tensor("out", [P, NB * T], F32, kind="ExternalOutput").ap()
    decoder(nc, dram, out)
    r = run_bass_kernel_spmd(nc, [arrays], core_ids=[0])
    return r.results[0]["out"].reshape(P, NB, T).transpose(1, 2, 0)
```

```python
from contextlib import ExitStack

import concourse.bass as bass
from concourse import mybir

F32 = mybir.dt.float32
BF16 = mybir.dt.bfloat16
U32 = mybir.dt.uint32
ALU = mybir.AluOpType
ACT = mybir.ActivationFunctionType
AX = mybir.AxisListType

P = 128
NB = 2
T = 512
TT = T // P
NKEY = 77
NE = 8
TOPK = 2
NF = 4
EPS = 1e-5
VW = 32
H0, D0 = 16, 8
HX = (8, 16)
DX = (16, 8)
QPART = (0, 0, 1, 1, 0, 2)
KPART = (0, 1, 0, 1, 2, 0)
NS = len(QPART)
AUG0 = NS * D0
AUGX = (NS * DX[0], 64)
ONES = 1.0 + 0x3F80 / 2.0 ** 23
G = 4
NG0 = H0 // G
FIRST = {"q": 1, "val": 1, "split": 3, "stack": 16 * NS, "msc": TT * HX[0] // G, "mx": TT * HX[0] // G, "mt": 1,
         "mval": 1, "msplit": 3, "maug": 48, "sc": HX[0], "exp": HX[0], "pv": HX[0] // G,
         "den": HX[0] // G, "div": HX[0] // G, "out": 1}
LN_EXP = "natural_log_exp_and_others"
RING_BANKS = (4, 5)
OFFSET = 0.3
NEG = -1e38

MAX_UNITS = [(0, 0, 4), (1, 0, 2), (1, 2, 2)] + [(i, h, 1) for i in (2, 3) for h in range(G)]
NM = len(MAX_UNITS)
EXP_UNITS = [[(h, 0, 0)] for h in range(G)] + [[(h, 3, 0), (h, 1, 128)] for h in range(G)] \
    + [[(0, 2, 0), (1, 2, 256)], [(2, 2, 0), (3, 2, 256)]]
NX = len(EXP_UNITS)
DIAGONALS = [(T, 1)] * G + [(P, 2)] * G + [(256, 2)] * 2
VALUE_UNITS = {"values0": range(0, 4), "values1": range(4, 8), "values2": range(8, 10)}
NPROB = 8
LAG = 1.95


def causal_items():
    items = []
    for n in range(NB * NG0):
        items += [(n + j / NM, "max", n, j) for j in range(NM)]
        items.append((n + 1 + 1.5 / NM, "rowmax", n, 0))
        parts = [("score", n, 0), ("score", n, 1), ("values1", n - 1, 0), ("score", n, 2), ("score", n, 3),
                 ("values2", n - 1, 0), ("score", n, 4), ("denominator", n - 1, 0), ("score", n, 5),
                 ("score", n, 6), ("values0", n, 0), ("score", n, 7), ("divide", n - 1, 0), ("score", n, 8),
                 ("score", n, 9)]
        items += [(n + LAG + k / len(parts), *part) for k, part in enumerate(parts) if part[1] >= 0]
    last = NB * NG0 - 1
    items += [(last + LAG + 1, "values1", last, 0), (last + LAG + 1.05, "values2", last, 0)]
    items += [(last + LAG + 1.1, "denominator", last, 0), (last + LAG + 1.12, "divide", last, 0)]
    for b in range(NB):
        items.append((NG0 * (b + 1) + LAG + 0.95 + 0.3 * (b == 1), "project", b, 0))
    return [i[1:] for i in sorted(items, key=lambda i: i[0])]


def later_steps():
    def norm(n):
        return [((f"norm_mean{n}",), 2.0), ((f"norm_var{n}",), 3.2)]

    def cross(L):
        groups = HX[L] // G
        out = [((f"cross_query{L}",), 11.0)]
        out += [((f"cross_max{L}", i, g), 0.5) for i in range(TT) for g in range(groups)]
        out += [((f"cross_rowmax{L}",), 7.0)]
        for g in range(groups + 1):
            if g < groups:
                out += [((f"cross_score{L}", G * g + k), 0.6) for k in (0, 1)]
            if g:
                out.append(((f"cross_values{L}", g - 1), 0.8))
            if g < groups:
                out += [((f"cross_score{L}", G * g + k), 0.6) for k in (2, 3)]
            if g:
                out += [((f"cross_den{L}", g - 1), 0.4), ((f"cross_div{L}", g - 1), 0.4)]
        return out + [((f"cross_out{L}",), 4.0)]

    chain = norm(0) + cross(0) + norm(1) + [(("ffn_up",), 3.5), (("ffn_down",), 4.5)] + norm(2) + norm(3)
    chain += [(("route",), 3.5), (("expert_up",), 3.0), (("expert_down",), 3.0)] + norm(4)
    chain += [(("mix_in",), 7.0), (("mix_scan",), 7.0), (("mix_divide",), 2.0), (("mix_out",), 2.0)] + norm(5)
    chain += cross(1) + norm(6) + [(("gate",), 8.0), (("hidden1",), 15.0), (("hidden2",), 15.0), (("down",), 4.5)]
    chain += norm(7)
    timed = []
    for b in range(NB):
        at = OFFSET * b
        for (step, *args), takes in chain:
            timed.append((at, b, (step, b, *args)))
            at += takes
    return [step for _, _, step in sorted(timed, key=lambda x: x[:2])]


def decoder(nc, dram, out):
    ctx = ExitStack()
    with ctx:
        def sb(name, shape, dt=F32):
            return ctx.enter_context(nc.sbuf_tensor(name, shape, dt))

        def sem(name):
            return ctx.enter_context(nc.semaphore(name))

        def sems(name):
            return [sem(f"{name}_{b}") for b in range(NB)]

        w = {}
        for name, (shape, _) in LOADS.items():
            if name in ("h1", "h2", "x"):
                continue
            w[name] = sb("w_" + name, shape)
        center, mean, ident = (w["const"][:, P * i:P * (i + 1)] for i in range(3))
        ones = w["const"][0:1, 3 * P:4 * P]
        ident_b = sb("ident_b", [P, P], BF16)
        mask_b = sb("mask_b", [P, P], BF16)
        col = {name: w["cols"][:, i:i + n] for name, i, n in COLS}

        def pair(name, shape, dt=F32):
            return [sb(f"{name}{b}", shape, dt) for b in range(NB)]

        xs = pair("xs", [P, T + 1])
        qe = pair("qe", [P, T])
        z = pair("z", [P, T])
        sq = pair("sq", [P, T])
        rstd = pair("rstd", [P, T])
        qstack = pair("qstack", [P, H0, T], BF16)
        kstack = pair("kstack", [P, H0, T], BF16)
        work = pair("work", [P, 1792])
        wide = pair("wide", [P, 4 * T])
        kx = [sb(f"kx{L}", [P, HX[L], NB * NKEY], BF16) for L in range(2)]
        vx = [sb(f"vx{L}", [NKEY, NB, HX[L], VW]) for L in range(2)]
        v0 = sb("v0", [P, NB, TT, H0, VW])
        probs = sb("probs", [P, NPROB, T])
        mx = pair("mx", [P, TT * H0])
        mt = pair("mt", [64, 2, P])
        mp = pair("mp", [64, 3, P], BF16)
        wmix = [sb(f"wmix{i}", [P, 2, P]) for i in range(3)]
        omm = sb("omm", [P, 3])
        decay = sb("decay", [P, 2])
        keep = sb("keep", [P, 3])
        eps = sb("eps", [P, 1])
        b2s = pair("b2s", [P, 2])
        xb = [z[b] for b in range(NB)]
        route = pair("route", [1, 16])
        choice = pair("choice", [1, 8], U32)
        wh = [v0[:, i, :, :, :].rearrange("p a h c -> p (a h c)").rearrange("p (k n) -> p k n", k=NF)
              for i in range(2)]
        qx = [kstack[b][:, 0:8, :] for b in range(NB)]
        scratch = [kstack[b][:, :, :].rearrange("p h t -> p (h t)").bitcast(F32).rearrange("p (j t) -> p j t", t=T)
                   for b in range(NB)]
        w4 = [wide[b][:, :].rearrange("p (j t) -> p j t", t=T) for b in range(NB)]

        def state(b):
            return xs[b][:, 1:T + 1]

        def split_tiles(area, n):
            parts = area[:, 2 * n:2 * n + 3 * n // 2].bitcast(BF16).rearrange("p (i t) -> p i t", i=3)
            return area[:, 0:n], area[:, n:2 * n], parts

        q_split = [split_tiles(work[b], T) for b in range(NB)]
        k_split = [split_tiles(wide[b], T) for b in range(NB)]
        kx_split = [(z[L][:, 0:NB * NKEY], z[L][:, NB * NKEY:2 * NB * NKEY],
                     qe[L][:, 0:3 * NB * NKEY // 2].bitcast(BF16).rearrange("p (i t) -> p i t", i=3))
                    for L in range(2)]

        psum = ctx.enter_context(nc.psum_tensor("psum", [P, 8, 512], F32))

        def bank(i):
            return psum[:, i, :]

        def den_tile(b, g):
            return (rstd, sq)[g % 2][b][:, :]

        def cross_probs(b, h):
            at = probs[:, G * b + h % G, :] if h % (2 * G) < G else scratch[b][:, G + h % G, :]
            return at[0:NKEY, :]

        def own(b, i):
            return psum[:, 4 * b + i, :]

        s_load = {name: sem("load_" + name) for name in LOAD_GROUPS}

        def loaded(engine, name):
            group = next(g for g, names in LOAD_GROUPS.items() if name in names)
            n = len(LOAD_GROUPS[group]) if group != "x" else NB
            engine.wait_ge(s_load[group], 16 * n)

        s_zero = sem("zeroed")
        s_vzero = sem("vzero")
        s_qk = sem("qk_proj")
        s_qk_val = sem("qk_value")
        s_qk_split = sem("qk_split")
        s_stack = [sem(f"stack{u}") for u in range(4)]
        s_v0 = sem("v0_proj")
        s_v0_out = sem("v0_out")
        s_kx = sem("kx_proj")
        s_kx_val = sem("kx_value")
        s_kx_split = sem("kx_split")
        s_kx_stack = sem("kx_stack")
        s_vx = sem("vx_proj")
        s_vx_out = sem("vx_out")
        s_wmix = sem("wmix")
        s_small = sem("small")
        s_param = sem("param")
        s_msc = sem("max_scores")
        s_mx = sem("max_done")
        s_mt = sem("rowmax_turned")
        s_mval = sem("rowmax_value")
        s_msplit = sem("rowmax_split")
        s_maug = sem("rowmax_rows")
        s_sc = sem("exp_scores")
        s_exp = sem("exp_done")
        s_mask = sem("masked")
        s_pv = sem("values_done")
        s_den = sem("denominators")
        s_rec = sem("reciprocal")
        s_div = sem("divided")
        s_proj = sems("projected")
        s_wh = sem("load_wh")
        s_z, s_cent, s_sq, s_var, s_rstd, s_aff, s_x = (
            sems(n) for n in ("residual", "centered", "squared", "variance", "rstd", "gained", "state"))
        x_q, x_val, x_split, x_stack, x_msc, x_mx, x_mt, x_mval, x_msplit, x_maug, x_sc, x_exp, x_pv, \
            x_den, x_div, x_out = (sems("x_" + n) for n in (
                "query", "value", "split", "stack", "max_scores", "max_done", "rowmax", "mval", "msplit", "maug",
                "scores", "exp", "values", "den", "div", "out"))
        s_ln = sems("log_variance")
        x_rec = sems("x_reciprocal")
        s_up, s_relu, s_down = (sems(n) for n in ("ffn_up", "ffn_relu", "ffn_down"))
        s_rt, s_rchain, s_choice, s_pick, s_b2s, s_eup, s_egelu, s_edown = (
            sems(n) for n in ("route_scores", "route_chain", "choice", "picked", "expert_bias", "expert_up",
                              "expert_gelu", "expert_down"))
        s_rk, s_rcp, s_rscan, s_rpool, s_rexp, s_rout = (
            sems(n) for n in ("mix_proj", "mix_copied", "mix_dve", "mix_pool", "mix_exp", "mix_out"))
        s_ga, s_gs, s_gb, s_gh, s_h1, s_g1, s_h2, s_g2, s_dn = (
            sems(n) for n in ("gate_a", "gate_silu", "gate_b", "gated", "hid1", "gelu1", "hid2", "gelu2", "down"))
        s_store = sem("stored")

        items = causal_items()
        ring = [i for i in items if i[0] in ("max", "rowmax", "project")]

        def ring_bank(kind, n, j=0):
            return bank(RING_BANKS[ring.index((kind, n, j)) % len(RING_BANKS)])

        steps = later_steps()
        block = ctx.enter_context(nc.Block())

        @block.sync
        def _(sp):
            def load(name):
                group = next(g for g, names in LOAD_GROUPS.items() if name in names)
                sp.dma_start(w[name][:], dram[name]).then_inc(s_load[group], 16)

            for name in ("x", "qk", "cols", "const"):
                if name == "x":
                    for b in range(NB):
                        sp.dma_start(state(b), dram["x"][:, T * b:T * (b + 1)]).then_inc(s_load["x"], 16)
                else:
                    load(name)
            for name in LOADS:
                if name not in ("x", "qk", "cols", "const", "h1", "h2"):
                    load(name)

            def stack(dst, parts, which, d, done, split, n, value, m):
                for part in range(3):
                    if part == 0:
                        sp.wait_ge(value, m)
                    else:
                        sp.wait_ge(split, n + part + 1)
                    for s in range(NS):
                        if which[s] == part:
                            sp.dma_start(dst[d * s:d * (s + 1)], parts[:, part, :]).then_inc(done, 16)

            for u in range(2 * NB):
                b, is_key = u // 2, u % 2
                if u % 2 == 0:
                    sp.wait_ge(s_vzero, b + 1)
                else:
                    sp.wait_ge(s_zero, 8 * b + 1)
                if is_key:
                    stack(kstack[b], k_split[b][2], KPART, D0, s_stack[u], s_qk_split, 3 * u, s_qk_val, u + 1)
                else:
                    stack(qstack[b], q_split[b][2], QPART, D0, s_stack[u], s_qk_split, 3 * u, s_qk_val, u + 1)
            for kind, n, _ in items:
                if kind == "rowmax":
                    if n == 1:
                        for L in range(2):
                            sp.wait_ge(s_zero, 8)
                            stack(kx[L], kx_split[L][2], KPART, DX[L], s_kx_stack, s_kx_split, 3 * L, s_kx_val,
                                  L + 1)
                    b, g = n // NG0, n % NG0
                    sp.wait_ge(s_msplit, 3 * (n + 1))
                    for i in range(3):
                        dst = qstack[b][AUG0 + i:AUG0 + i + 1, G * g:G * (g + 1), :]
                        sp.dma_start(dst, mp[n % 2][0:G * TT, i, :]) \
                            .then_inc(s_maug, 16)
            sp.wait_ge(s_pv, NX * NB * NG0)
            for i in range(2):
                sp.dma_start(wh[i], dram[f"h{i + 1}"]).then_inc(s_wh, 16)

            for step, b, *_ in steps:
                for L in range(2):
                    if step == f"cross_query{L}":
                        stack(qx[b] if L == 0 else qstack[b], q_split[b][2], QPART, DX[L], x_stack[b],
                              x_split[b], L * FIRST["split"], x_val[b], L + 1)
                    if step == f"cross_rowmax{L}":
                        q = qx[b] if L == 0 else qstack[b]
                        for i in range(3):
                            if i == 0:
                                sp.wait_ge(x_mval[b], L + 1)
                            else:
                                sp.wait_ge(x_msplit[b], L * FIRST["msplit"] + i + 1)
                            dst = q[AUGX[L] + i:AUGX[L] + i + 1, :, :]
                            sp.dma_start(dst, mp[b][0:HX[L] * TT, i, :]).then_inc(x_maug[b], 16)
                if step == "norm_var7":
                    sp.wait_ge(s_x[b], 7)
                    sp.dma_start(out[:, T * b:T * (b + 1)], state(b)).then_inc(s_store, 16)
            sp.wait_ge(s_store, 16 * NB)

        @block.tensor
        def _(pe):
            loaded(pe, "x")
            loaded(pe, "qk")
            for u in range(2 * NB):
                pe.matmul(bank(u), w["qk"][:, P * (u % 2):P * (u % 2 + 1)], state(u // 2),
                          start=True, stop=True).then_inc(s_qk, 1)
            loaded(pe, "const")
            loaded(pe, "v0")
            for L in range(2):
                pe.matmul(psum[:, 6, 256 * L:256 * L + NB * NKEY], w["xkv"][:, 2 * P * L:2 * P * L + P],
                          w["ctx"][:, :], start=True, stop=True, skip_group_check=True).then_inc(s_kx, 1)
            for b in range(NB):
                pe.wait_ge(s_qk_val, b + 1)
                for k in range(TT):
                    o = psum[:, b, P * k:P * (k + 1)]
                    pe.matmul(o, state(b)[:, P * k:P * (k + 1)], w["v0"][:, 0:P], start=True, stop=False)
                    mm = pe.matmul(o, ones, w["v0"][0:1, P:2 * P], start=False, stop=True)
                mm.then_inc(s_v0, 1)
            pe.wait_ge(s_qk_val, 3)
            for L in range(2):
                for b in range(NB):
                    o = psum[0:NKEY, 2, P * (2 * L + b):P * (2 * L + b + 1)]
                    pe.matmul(o, w["ctx"][:, NKEY * b:NKEY * (b + 1)], w["xkv"][:, 2 * P * L + P:2 * P * (L + 1)],
                              start=True, stop=L == 0)
                    if L == 1:
                        mm = pe.matmul(o, ones[:, 0:NKEY], w["xbv"][0:1, :], start=False, stop=True)
            mm.then_inc(s_vx, 1)

            def turn(kind, n, j=0):
                at = ring.index((kind, n, j))
                if at >= len(RING_BANKS):
                    kind, n, j = ring[at - len(RING_BANKS)]
                    if kind == "max":
                        pe.wait_ge(s_mx, NM * n + j + 1)
                    if kind == "rowmax":
                        pe.wait_ge(s_mval, n + 1)
                    if kind == "project":
                        pe.wait_ge(s_z[n], 1)
                return bank(RING_BANKS[at % len(RING_BANKS)])

            for kind, n, j in items:
                b, g = n // NG0, n % NG0
                if kind == "max":
                    i, h0, nh = MAX_UNITS[j]
                    if g == 0 and j == 0:
                        pe.wait_ge(s_stack[2 * b], 16 * NS)
                        pe.wait_ge(s_stack[2 * b + 1], 16 * NS)
                        pe.wait_ge(s_zero, 7 * b + 3)
                    o = turn(kind, n, j)
                    width = P * (i + 1)
                    for k in range(nh):
                        h = G * g + h0 + k
                        pe.matmul(o[:, width * k:width * (k + 1)], qstack[b][:, h, P * i:P * (i + 1)],
                                  kstack[b][:, h, 0:width], start=True, stop=True, skip_group_check=True)
                        mm = pe.matmul(o[:, width * (k + 1) - P:width * (k + 1)], ident_b[:, :], mask_b[:, :],
                                       start=False, stop=True, skip_group_check=True)
                    mm.then_inc(s_msc, 1)
                if kind == "rowmax":
                    o = turn(kind, n)
                    pe.wait_ge(s_mx, NM * (n + 1))
                    pe.transpose(o[0:G * TT, 0:P], mx[n % 2][:, 0:G * TT], ident).then_inc(s_mt, 1)
                if kind == "score":
                    v = NX * n + j
                    if j == 0:
                        pe.wait_ge(s_maug, 48 * (n + 1))
                    if v >= 4:
                        pe.wait_ge(s_exp, v - 3)
                    else:
                        pe.wait_ge(s_qk_val, 4)
                        pe.wait_ge(s_v0_out, 2)
                        pe.wait_ge(s_vx_out, 4)
                    for h, k, c in EXP_UNITS[j]:
                        width = T - P * k
                        mm = pe.matmul(bank(v % 4)[:, c:c + width], kstack[b][:, G * g + h, P * k:P * (k + 1)],
                                       qstack[b][:, G * g + h, P * k:T], start=True, stop=True,
                                       skip_group_check=True)
                    mm.then_inc(s_sc, 1)
                if kind in VALUE_UNITS:
                    units = VALUE_UNITS[kind]
                    pe.wait_ge(s_mask, NX * n + units[-1] + 1)
                    if units[0] == 0 and n >= 2:
                        pe.wait_ge(s_div, n - 1)
                    if n == 0 and units[0] == 0:
                        pe.wait_ge(s_kx_val, 2)
                    blocks = [(k, h, u, c) for u in units for h, k, c in EXP_UNITS[u]]
                    for k, h, u, c in sorted(blocks):
                        width = T - P * k
                        mm = pe.matmul(psum[VW * h:VW * (h + 1), 6 + n % 2, P * k:T], v0[:, b, k, G * g + h, :],
                                       probs[:, (NX * n + u) % NPROB, c:c + width], start=k == 0, stop=k == 2,
                                       skip_group_check=True, tile_position=(0, VW * h))
                    mm.then_inc(s_pv, len(units))
                if kind == "project":
                    b = n
                    if b == 0:
                        loaded(pe, "o0")
                    pe.wait_ge(s_div, NG0 * (b + 1))
                    o = turn(kind, n)
                    for k in range(NG0):
                        mm = pe.matmul(o, w["o0"][:, P * k:P * (k + 1)], w4[b][:, k, :],
                                       start=k == 0, stop=k == NG0 - 1)
                    mm.then_inc(s_proj[b], 1)

            for step, b, *at in steps:
                if step.startswith("norm_mean"):
                    pe.wait_ge(s_z[b], int(step[-1]) + 1)
                    pe.matmul(own(b, 0), center, z[b][:, :], start=True, stop=True).then_inc(s_cent[b], 1)
                if step.startswith("norm_var"):
                    pe.wait_ge(s_sq[b], int(step[-1]) + 1)
                    pe.matmul(own(b, 1), mean, sq[b][:, :], start=True, stop=True).then_inc(s_var[b], 1)
                for L in range(2):
                    q = qx[b] if L == 0 else qstack[b]
                    if step == f"cross_query{L}":
                        loaded(pe, "xq")
                        pe.wait_ge(s_x[b], 1 if L == 0 else 5)
                        pe.matmul(own(b, 0), w["xq"][:, P * L:P * (L + 1)], state(b),
                                  start=True, stop=True).then_inc(x_q[b], 1)
                    if step == f"cross_max{L}":
                        i, g = at
                        u = i * (HX[L] // G) + g
                        if u == 0:
                            pe.wait_ge(x_stack[b], L * FIRST["stack"] + 16 * NS)
                            pe.wait_ge(s_kx_stack, 2 * 16 * NS)
                        if u >= 4:
                            pe.wait_ge(x_mx[b], L * FIRST["mx"] + u - 3)
                        for k in range(G):
                            h = G * g + k
                            mm = pe.matmul(own(b, u % 4)[:, NKEY * k:NKEY * (k + 1)], q[:, h, P * i:P * (i + 1)],
                                           kx[L][:, h, NKEY * b:NKEY * (b + 1)], start=True, stop=True)
                        mm.then_inc(x_msc[b], 1)
                    if step == f"cross_rowmax{L}":
                        n = TT * HX[L]
                        pe.wait_ge(x_mx[b], L * FIRST["mx"] + TT * HX[L] // G)
                        pe.transpose(own(b, 2)[0:n, 0:P], mx[b][:, 0:n], ident).then_inc(x_mt[b], 1)
                    if step == f"cross_score{L}":
                        h, = at
                        if h == 0:
                            pe.wait_ge(x_maug[b], L * FIRST["maug"] + 48)
                        if h >= 2:
                            pe.wait_ge(x_exp[b], L * FIRST["exp"] + h - 1)
                        pe.matmul(own(b, h % 2)[0:NKEY, :], kx[L][:, h, NKEY * b:NKEY * (b + 1)], q[:, h, :],
                                  start=True, stop=True).then_inc(x_sc[b], 1)
                    if step == f"cross_values{L}":
                        g, = at
                        pe.wait_ge(x_exp[b], L * FIRST["exp"] + G * (g + 1))
                        if g >= 2:
                            pe.wait_ge(x_div[b], L * FIRST["div"] + g - 1)
                        for k in range(G):
                            h = G * g + k
                            mm = pe.matmul(own(b, 2 + g % 2)[VW * k:VW * (k + 1), :], vx[L][:, b, h, :],
                                           cross_probs(b, h), start=True, stop=True, skip_group_check=True,
                                           tile_position=(0, VW * k))
                        mm.then_inc(x_pv[b], 1)
                    if step == f"cross_out{L}":
                        ng = HX[L] // G
                        loaded(pe, "xo")
                        pe.wait_ge(x_div[b], L * FIRST["div"] + ng)
                        for k in range(ng):
                            c = P * (2 * L + k)
                            mm = pe.matmul(own(b, 0), w["xo"][:, c:c + P], w4[b][:, k, :],
                                           start=k == 0, stop=k == ng - 1)
                        mm.then_inc(x_out[b], 1)
                if step == "ffn_up":
                    loaded(pe, "ffn")
                    pe.wait_ge(s_x[b], 2)
                    for j in range(NF):
                        pe.matmul(own(b, j), w["ffn"][:, P * j:P * (j + 1)], qe[b][:, :],
                                  start=True, stop=True).then_inc(s_up[b], 1)
                if step == "ffn_down":
                    for j in range(NF):
                        pe.wait_ge(s_relu[b], max(j + 1, 1))
                        mm = pe.matmul(own(b, 0), w["ffn"][:, P * (NF + j):P * (NF + j + 1)], w4[b][:, j, :],
                                       start=j == 0, stop=j == NF - 1)
                    mm.then_inc(s_down[b], 1)
                if step == "route":
                    loaded(pe, "route")
                    pe.wait_ge(s_x[b], 3)
                    pe.matmul(own(b, 2)[0:1, 0:NE], xs[b][:, 1:2], w["route"][:, 0:NE],
                              start=True, stop=True).then_inc(s_rt[b], 1)
                if step == "expert_up":
                    for k in range(TOPK):
                        pe.wait_ge(s_pick[b], k + 1)
                        pe.matmul(own(b, k), work[b][:, MOE * k:MOE * k + P], state(b),
                                  start=True, stop=True).then_inc(s_eup[b], 1)
                if step == "expert_down":
                    for k in range(TOPK):
                        pe.wait_ge(s_egelu[b], k + 1)
                        mm = pe.matmul(own(b, 2), work[b][:, MOE * k + P:MOE * k + 2 * P], w4[b][:, k, :],
                                       start=k == 0, stop=k == TOPK - 1)
                    mm.then_inc(s_edown[b], 1)
                if step == "mix_in":
                    pe.wait_ge(s_wmix, 6)
                    pe.wait_ge(s_x[b], 4)
                    for i in range(3):
                        pe.matmul(own(b, i), wmix[i][:, 0, :], state(b), start=True, stop=False)
                        pe.matmul(own(b, i), wmix[i][:, 1, :], xs[b][:, 0:T], start=False, stop=True) \
                            .then_inc(s_rk[b], 1)
                if step == "mix_out":
                    pe.wait_ge(s_rscan[b], MIX_DVE)
                    pe.matmul(own(b, 3), w["mix"][:, 3 * P:4 * P], scratch[b][:, 7, :],
                              start=True, stop=True).then_inc(s_rout[b], 1)
                if step == "gate":
                    loaded(pe, "gate")
                    pe.wait_ge(s_x[b], 6)
                    for j in range(NF):
                        if j >= 2:
                            pe.wait_ge(s_gs[b], j - 1)
                        pe.matmul(own(b, 2 * j % 4), w["gate"][:, P * j:P * (j + 1)], state(b),
                                  start=True, stop=True).then_inc(s_ga[b], 1)
                        if j >= 2:
                            pe.wait_ge(s_gh[b], j - 1)
                        pe.matmul(own(b, (2 * j + 1) % 4), w["gate"][:, P * (NF + j):P * (NF + j + 1)], state(b),
                                  start=True, stop=True).then_inc(s_gb[b], 1)
                for i, (name, src, ready, done, free) in enumerate((
                        ("hidden1", 0, s_gh, s_h1, s_gh), ("hidden2", 4, s_g1, s_h2, s_g1))):
                    if step == name:
                        pe.wait_ge(s_wh, 32)
                        for j in range(NF):
                            if j == 0:
                                pe.wait_ge(ready[b], NF)
                            for k in range(NF):
                                mm = pe.matmul(own(b, j), wh[i][:, k, P * j:P * (j + 1)],
                                               scratch[b][:, src + k, :], start=k == 0, stop=k == NF - 1)
                            mm.then_inc(done[b], 1)
                if step == "down":
                    pe.wait_ge(s_g2[b], NF)
                    for k in range(NF):
                        mm = pe.matmul(own(b, 0), w["gate"][:, P * (2 * NF + k):P * (2 * NF + k + 1)],
                                       w4[b][:, k, :], start=k == 0, stop=k == NF - 1)
                    mm.then_inc(s_dn[b], 1)

        @block.scalar
        def _(act):
            def value_and_first(src, dst, first, bias, scale=1.0):
                if bias is None:
                    act.activation(dst, src, ACT.Copy, scale=scale)
                    return act.activation(first, src, ACT.Copy, scale=scale)
                act.activation(dst, src, ACT.Identity, bias=bias)
                return act.activation(first, src, ACT.Identity, bias=bias)

            def reciprocal(tile, chain, done):
                act.activation(tile, tile, ACT.Ln).then_inc(chain, 1)
                act.wait_ge(chain, done + 1)
                act.activation(tile, tile, ACT.Exp, scale=-1.0).then_inc(chain, 1)

            held = [None]

            def tables(name):
                if held[0] != name:
                    act.preload_act_table_set(name)
                    held[0] = name

            tables(LN_EXP)
            loaded(act, "cols")
            act.activation(decay[:, 0:1], col["decay"], ACT.Exp).then_inc(s_small, 1)
            act.activation(keep[:, 0:1], col["lambda"], ACT.Exp, scale=-1.0).then_inc(s_small, 1)
            for u in range(2 * NB):
                act.wait_ge(s_qk, u + 1)
                value, _, parts = (q_split, k_split)[u % 2][u // 2]
                value_and_first(bank(u), value, parts[:, 0, :], col["bq" if u % 2 == 0 else "bk"]) \
                    .then_inc(s_qk_val, 1)
            for L in range(2):
                act.wait_ge(s_kx, 2)
                value, _, parts = kx_split[L]
                value_and_first(psum[:, 6, 256 * L:256 * L + NB * NKEY], value, parts[:, 0, :],
                                None if L == 0 else col["xbk"]).then_inc(s_kx_val, 1)

            for kind, n, j in items:
                b = n // NG0
                if kind == "rowmax":
                    act.wait_ge(s_mt, n + 1)
                    if n >= 2:
                        act.wait_ge(s_maug, 48 * (n - 1))
                    o = ring_bank(kind, n)[0:G * TT, 0:P]
                    value_and_first(o, mt[n % 2][0:G * TT, 0, :], mp[n % 2][0:G * TT, 0, :], None, -1.0) \
                        .then_inc(s_mval, 1)
                if kind == "score":
                    v = NX * n + j
                    act.wait_ge(s_sc, v + 1)
                    if v >= NPROB:
                        act.wait_ge(s_pv, v - NPROB + 1)
                    act.activation(probs[:, v % NPROB, :], bank(v % 4), ACT.Exp, scale=float(D0) ** -0.5) \
                        .then_inc(s_exp, 1)
                if kind == "denominator":
                    act.wait_ge(s_den, n + 1)
                    reciprocal(den_tile(b, n), s_rec, 2 * n)

            for step, b, *at in steps:
                if step.startswith("norm_mean"):
                    act.wait_ge(s_cent[b], int(step[-1]) + 1)
                    act.activation(sq[b][:, :], own(b, 0), ACT.Square).then_inc(s_sq[b], 1)
                if step.startswith(("norm_var", "mix_scan", "mix_divide", "cross_score", "cross_den")):
                    tables(LN_EXP)
                if step.startswith("norm_var"):
                    n = int(step[-1])
                    act.wait_ge(s_var[b], n + 1)
                    if n == 0:
                        act.wait_ge(s_vzero, 2)
                    act.activation(rstd[b][:, :], own(b, 1), ACT.Ln, bias=eps[:, 0:1]).then_inc(s_ln[b], 1)
                    act.wait_ge(s_ln[b], n + 1)
                    act.activation(rstd[b][:, :], rstd[b][:, :], ACT.Exp, scale=-0.5).then_inc(s_rstd[b], 1)
                for L in range(2):
                    if step == f"cross_query{L}":
                        act.wait_ge(x_q[b], L * FIRST["q"] + 1)
                        value, _, parts = q_split[b]
                        value_and_first(own(b, 0), value, parts[:, 0, :], None if L == 0 else col["xbq"]) \
                            .then_inc(x_val[b], 1)
                    if step == f"cross_rowmax{L}":
                        n = TT * HX[L]
                        act.wait_ge(x_mt[b], L * FIRST["mt"] + 1)
                        value_and_first(own(b, 2)[0:n, 0:P], mt[b][0:n, 0, :], mp[b][0:n, 0, :], None, -1.0) \
                            .then_inc(x_mval[b], 1)
                    if step == f"cross_score{L}":
                        h, = at
                        act.wait_ge(x_sc[b], L * FIRST["sc"] + h + 1)
                        if h >= 2 * G:
                            act.wait_ge(x_pv[b], L * FIRST["pv"] + h // G - 1)
                        act.activation(cross_probs(b, h), own(b, h % 2)[0:NKEY, :], ACT.Exp,
                                       scale=float(DX[L]) ** -0.5).then_inc(x_exp[b], 1)
                    if step == f"cross_den{L}":
                        g, = at
                        act.wait_ge(x_den[b], L * FIRST["den"] + g + 1)
                        reciprocal(den_tile(b, g), x_rec[b], 2 * (L * FIRST["den"] + g))
                if step == "ffn_up":
                    for j in range(NF):
                        act.wait_ge(s_up[b], j + 1)
                        act.activation(w4[b][:, j, :], own(b, j), ACT.Relu, bias=col["ffn_b1"][:, j:j + 1]) \
                            .then_inc(s_relu[b], 1)
                if step == "expert_up":
                    tables("gelu_and_others")
                    for k in range(TOPK):
                        act.wait_ge(s_eup[b], k + 1)
                        act.activation(w4[b][:, k, :], own(b, k), ACT.Gelu,
                                       bias=work[b][:, MOE * k + 2 * P:MOE * k + 2 * P + 1]).then_inc(s_egelu[b], 1)
                if step == "mix_in":
                    for i in range(3):
                        act.wait_ge(s_rk[b], i + 1)
                        if i < 2:
                            act.copy(scratch[b][:, i, :], own(b, i)).then_inc(s_rcp[b], 1)
                        else:
                            tables("sigmoid_and_others")
                            act.activation(scratch[b][:, 6, :], own(b, i), ACT.Sigmoid) \
                                .then_inc(s_rcp[b], 1)
                if step == "mix_scan":
                    s = scratch[b]
                    act.wait_ge(s_rscan[b], 5)
                    act.activation(s[:, 2:4, :], s[:, 2:4, :], ACT.Exp).then_inc(s_rexp[b], 1)
                    act.wait_ge(s_rpool[b], 1)
                    act.wait_ge(s_rscan[b], 6)
                    act.activation(s[:, 4:6, :], s[:, 4:6, :], ACT.Exp).then_inc(s_rexp[b], 1)
                if step == "mix_divide":
                    s = scratch[b]
                    act.wait_ge(s_rscan[b], 11)
                    reciprocal(s[:, 2, :], s_rexp[b], 2)
                if step == "gate":
                    tables("silu_and_others")
                    for j in range(NF):
                        act.wait_ge(s_ga[b], j + 1)
                        act.activation(w4[b][:, j, :], own(b, 2 * j % 4), ACT.Silu,
                                       scale=col["w1_s"][:, j:j + 1]).then_inc(s_gs[b], 1)
                for name, dst, ready, scale, done in (
                        ("hidden1", [scratch[b][:, 4 + j, :] for j in range(NF)], s_h1, "h1_s", s_g1),
                        ("hidden2", [w4[b][:, j, :] for j in range(NF)], s_h2, "h2_s", s_g2)):
                    if step == name:
                        tables("gelu_and_others")
                        for j in range(NF):
                            act.wait_ge(ready[b], j + 1)
                            act.activation(dst[j], own(b, j), ACT.Gelu, scale=col[scale][:, j:j + 1]) \
                                .then_inc(done[b], 1)

        @block.vector
        def _(dve):
            def split_rest(value, rest, parts, chain, done):
                dve.tensor_tensor(rest, value, parts[:, 0, :], ALU.subtract).then_inc(chain, 1)
                dve.wait_ge(chain, done + 1)
                dve.tensor_copy(parts[:, 1, :], rest).then_inc(chain, 1)
                dve.wait_ge(chain, done + 2)
                dve.tensor_tensor(parts[:, 2, :], rest, parts[:, 1, :], ALU.subtract).then_inc(chain, 1)

            for b in range(NB):
                if b == 1:
                    dve.memset(eps[:, :], EPS)
                dve.memset(qstack[b][:, :, :].rearrange("p h t -> p (h t)").bitcast(F32), 0.0).then_inc(s_vzero, 1)
                if b == 0:
                    for u in range(2):
                        dve.wait_ge(s_qk_val, u + 1)
                        split_rest(*(q_split, k_split)[u][0], s_qk_split, 3 * u)
            for u in range(2, 4):
                dve.wait_ge(s_qk_val, u + 1)
                split_rest(*(q_split, k_split)[u % 2][1], s_qk_split, 3 * u)
            dve.wait_ge(s_zero, 5)
            for b in range(NB):
                dve.wait_ge(s_v0, b + 1)
                dve.tensor_copy(v0[:, b, :, :, 0:D0].rearrange("p k h d -> p (k h) d"),
                                bank(b).rearrange("p (k d) -> p k d", d=D0)).then_inc(s_v0_out, 1)
            dve.wait_ge(s_small, 2)
            dve.tensor_scalar(keep[:, 1:2], keep[:, 0:1], 1.0, None, ALU.add).then_inc(s_param, 1)
            dve.wait_ge(s_param, 1)
            dve.reciprocal(keep[:, 0:1], keep[:, 1:2]).then_inc(s_param, 1)
            dve.wait_ge(s_param, 2)
            dve.tensor_scalar(keep[:, 2:3], keep[:, 0:1], -1.0, 1.0, ALU.mult, ALU.add).then_inc(s_param, 1)
            dve.tensor_scalar(decay[:, 1:2], decay[:, 0:1], -1.0, None, ALU.mult).then_inc(s_param, 1)
            dve.tensor_scalar(omm[:, :], col["mix"], -1.0, 1.0, ALU.mult, ALU.add).then_inc(s_param, 1)
            for b in range(NB):
                dve.memset(xs[b][:, 0:1], 0.0).then_inc(s_param, 1)

            for kind, n, j in items:
                b, g = n // NG0, n % NG0
                if kind == "max":
                    i, h0, nh = MAX_UNITS[j]
                    if n == 1 and j == 0:
                        for L in range(2):
                            dve.wait_ge(s_kx_val, L + 1)
                            split_rest(*kx_split[L], s_kx_split, 3 * L)
                        dve.wait_ge(s_vx, 1)
                        dve.wait_ge(s_zero, 12)
                        for L in range(2):
                            for c in range(NB):
                                o = psum[0:NKEY, 2, P * (2 * L + c):P * (2 * L + c + 1)]
                                dve.tensor_copy(vx[L][:, c, :, 0:DX[L]], o.rearrange("p (h d) -> p h d", d=DX[L])) \
                                    .then_inc(s_vx_out, 1)
                    if n >= 2 and j == 0:
                        dve.wait_ge(s_mt, n - 1)
                    dve.wait_ge(s_msc, NM * n + j + 1)
                    width = P * (i + 1)
                    src = ring_bank(kind, n, j)[:, 0:nh * width].rearrange("p (h k) -> p h k", h=nh)
                    dve.tensor_reduce(mx[n % 2][:, TT * h0 + i:TT * (h0 + nh - 1) + i + 1:TT], src, AX.X, ALU.max) \
                        .then_inc(s_mx, 1)
                if kind == "rowmax":
                    dve.wait_ge(s_mval, n + 1)
                    split_rest(mt[n % 2][0:G * TT, 0, :], mt[n % 2][0:G * TT, 1, :], mp[n % 2][0:G * TT],
                               s_msplit, 3 * n)
                if kind == "denominator":
                    dve.wait_ge(s_pv, NX * (n + 1))
                    dve.stream_shuffle(den_tile(b, n), bank(6 + n % 2), [D0] * VW).then_inc(s_den, 1)
                if kind == "divide":
                    dve.wait_ge(s_rec, 2 * (n + 1))
                    dve.tensor_tensor(w4[b][:, g, :], bank(6 + n % 2), den_tile(b, n), ALU.mult) \
                        .then_inc(s_div, 1)
                if kind == "project":
                    b = n
                    dve.wait_ge(s_proj[b], 1)
                    dve.scalar_tensor_tensor(out=z[b][:, :], in0=ring_bank(kind, n), scalar=col["bo"], in1=state(b),
                                             op0=ALU.add, op1=ALU.add).then_inc(s_z[b], 1)

            for step, b, *at in steps:
                if step.startswith("norm_var"):
                    n = int(step[-1])
                    dve.wait_ge(s_rstd[b], n + 1)
                    if n in (1, 2):
                        dst = qe[b] if n == 1 else z[b]
                        dve.scalar_tensor_tensor(out=dst[:, :], in0=own(b, 0), scalar=col[f"ln{n}_g"],
                                                 in1=rstd[b][:, :], op0=ALU.mult, op1=ALU.mult) \
                            .then_inc(s_aff[b], 1)
                        dve.wait_ge(s_aff[b], n)
                        if n == 1:
                            dve.tensor_scalar(qe[b][:, :], qe[b][:, :], col["ln1_b"], None, ALU.add) \
                                .then_inc(s_x[b], 1)
                        else:
                            dve.scalar_tensor_tensor(out=z[b][:, :], in0=z[b][:, :], scalar=col["ln2_b"],
                                                     in1=state(b), op0=ALU.add, op1=ALU.add) \
                                .then_inc(s_z[b], 1)
                    else:
                        dve.tensor_tensor(state(b), own(b, 0), rstd[b][:, :], ALU.mult).then_inc(s_x[b], 1)
                for L in range(2):
                    if step == f"cross_query{L}":
                        dve.wait_ge(x_val[b], L * FIRST["val"] + 1)
                        split_rest(*q_split[b], x_split[b], L * FIRST["split"])
                    if step == f"cross_max{L}":
                        i, g = at
                        u = i * (HX[L] // G) + g
                        dve.wait_ge(x_msc[b], L * FIRST["msc"] + u + 1)
                        src = own(b, u % 4)[:, 0:G * NKEY].rearrange("p (h k) -> p h k", h=G)
                        dve.tensor_reduce(mx[b][:, TT * G * g + i:TT * (G * (g + 1) - 1) + i + 1:TT], src, AX.X, ALU.max) \
                            .then_inc(x_mx[b], 1)
                    if step == f"cross_rowmax{L}":
                        n = TT * HX[L]
                        dve.wait_ge(x_mval[b], L * FIRST["mval"] + 1)
                        split_rest(mt[b][0:n, 0, :], mt[b][0:n, 1, :], mp[b][0:n], x_msplit[b], L * FIRST["msplit"])
                    if step == f"cross_den{L}":
                        g, = at
                        dve.wait_ge(x_pv[b], L * FIRST["pv"] + g + 1)
                        dve.stream_shuffle(den_tile(b, g), own(b, 2 + g % 2), [DX[L]] * VW).then_inc(x_den[b], 1)
                    if step == f"cross_div{L}":
                        g, = at
                        dve.wait_ge(x_rec[b], 2 * (L * FIRST["den"] + g + 1))
                        if L == 0:
                            dve.scalar_tensor_tensor(out=w4[b][:, g, :], in0=own(b, 2 + g % 2),
                                                     scalar=keep[:, 2:3], in1=den_tile(b, g),
                                                     op0=ALU.mult, op1=ALU.mult).then_inc(x_div[b], 1)
                        else:
                            dve.tensor_tensor(w4[b][:, g, :], own(b, 2 + g % 2), den_tile(b, g), ALU.mult) \
                                .then_inc(x_div[b], 1)
                    if step == f"cross_out{L}":
                        dve.wait_ge(x_out[b], L * FIRST["out"] + 1)
                        if L == 0:
                            dve.tensor_tensor(z[b][:, :], own(b, 0), state(b), ALU.add).then_inc(s_z[b], 1)
                        else:
                            dve.scalar_tensor_tensor(out=z[b][:, :], in0=own(b, 0), scalar=col["xbo"],
                                                     in1=state(b), op0=ALU.add, op1=ALU.add).then_inc(s_z[b], 1)
                if step == "ffn_down":
                    dve.wait_ge(s_down[b], 1)
                    dve.scalar_tensor_tensor(out=z[b][:, :], in0=own(b, 0), scalar=col["ffn_b2"],
                                             in1=qe[b][:, :], op0=ALU.add, op1=ALU.add).then_inc(s_z[b], 1)
                if step == "route":
                    r = route[b]
                    dve.wait_ge(s_rt[b], 1)
                    dve.tensor_tensor(r[:, 0:NE], own(b, 2)[0:1, 0:NE], w["route"][0:1, NE:2 * NE], ALU.add) \
                        .then_inc(s_rchain[b], 1)
                    dve.wait_ge(s_rchain[b], 1)
                    dve.max(r[:, NE:2 * NE], r[:, 0:NE]).then_inc(s_rchain[b], 1)
                    dve.wait_ge(s_rchain[b], 2)
                    dve.max_index(choice[b][:, :], r[:, NE:2 * NE], r[:, 0:NE]).then_inc(s_choice[b], 1)
                if step == "expert_down":
                    dve.wait_ge(s_edown[b], 1)
                    dve.wait_ge(s_b2s[b], 3)
                    dve.scalar_tensor_tensor(out=z[b][:, :], in0=own(b, 2), scalar=1.0 / TOPK, in1=qe[b][:, :],
                                             op0=ALU.mult, op1=ALU.add).then_inc(s_z[b], 1)
                if step == "mix_in":
                    s, (pp, aa, bb) = scratch[b], carried(wide[b])
                    for t, v in ((pp, NEG), (aa, 0.0), (bb, 0.0)):
                        ins = dve.memset(t[:, 0:1], v)
                    ins.then_inc(s_rscan[b], 1)
                    dve.wait_ge(s_rscan[b], 1)
                    dve.wait_ge(s_rcp[b], 1)
                    dve.tensor_tensor_scan(pp[:, 1:T + 1], decay[:, 1:2].broadcast_to([P, T]), s[:, 0, :], NEG,
                                           ALU.add, ALU.max).then_inc(s_rscan[b], 1)
                    dve.wait_ge(s_rscan[b], 2)
                    dve.scalar_tensor_tensor(out=s[:, 7, :], in0=s[:, 0, :], scalar=col["first"], in1=pp[:, 0:T],
                                             op0=ALU.add, op1=ALU.max).then_inc(s_rscan[b], 1)
                    dve.scalar_tensor_tensor(out=s[:, 2, :], in0=pp[:, 0:T], scalar=decay[:, 1:2],
                                             in1=pp[:, 1:T + 1], op0=ALU.add, op1=ALU.subtract) \
                        .then_inc(s_rscan[b], 1)
                    dve.wait_ge(s_rscan[b], 4)
                    dve.tensor_tensor(s[:, 3, :], s[:, 0, :], pp[:, 1:T + 1], ALU.subtract).then_inc(s_rscan[b], 1)
                    dve.scalar_tensor_tensor(out=s[:, 5, :], in0=s[:, 0, :], scalar=col["first"], in1=s[:, 7, :],
                                             op0=ALU.add, op1=ALU.subtract).then_inc(s_rscan[b], 1)
                if step == "mix_scan":
                    s, (pp, aa, bb) = scratch[b], carried(wide[b])
                    dve.wait_ge(s_rexp[b], 1)
                    dve.tensor_tensor_scan(bb[:, 1:T + 1], s[:, 2, :], s[:, 3, :], 0.0, ALU.mult, ALU.add) \
                        .then_inc(s_rscan[b], 1)
                    dve.wait_ge(s_rpool[b], 2)
                    dve.tensor_tensor_scan(aa[:, 1:T + 1], s[:, 2, :], s[:, 7, :], 0.0, ALU.mult, ALU.add) \
                        .then_inc(s_rscan[b], 1)
                    dve.wait_ge(s_rscan[b], 8)
                    dve.wait_ge(s_rexp[b], 2)
                    dve.tensor_tensor(s[:, 2, :], s[:, 4, :], bb[:, 0:T], ALU.mult).then_inc(s_rscan[b], 1)
                    dve.tensor_tensor(s[:, 0, :], s[:, 4, :], aa[:, 0:T], ALU.mult).then_inc(s_rscan[b], 1)
                    dve.wait_ge(s_rscan[b], 9)
                    dve.tensor_tensor(s[:, 2, :], s[:, 2, :], s[:, 5, :], ALU.add).then_inc(s_rscan[b], 1)
                    dve.wait_ge(s_rscan[b], 10)
                    dve.wait_ge(s_rpool[b], 3)
                    dve.wait_ge(s_rcp[b], 3)
                    dve.tensor_tensor(s[:, 0, :], s[:, 0, :], s[:, 1, :], ALU.add).then_inc(s_rscan[b], 1)
                    dve.wait_ge(s_rscan[b], 12)
                    dve.tensor_tensor(s[:, 0, :], s[:, 0, :], s[:, 6, :], ALU.mult).then_inc(s_rscan[b], 1)
                if step == "mix_divide":
                    s = scratch[b]
                    dve.wait_ge(s_rexp[b], 4)
                    dve.wait_ge(s_rscan[b], 13)
                    dve.tensor_tensor(s[:, 7, :], s[:, 0, :], s[:, 2, :], ALU.mult).then_inc(s_rscan[b], 1)
                if step == "mix_out":
                    dve.wait_ge(s_rout[b], 1)
                    dve.tensor_tensor(z[b][:, :], own(b, 3), state(b), ALU.add).then_inc(s_z[b], 1)
                if step == "gate":
                    for j in range(NF):
                        dve.wait_ge(s_gb[b], j + 1)
                        dve.wait_ge(s_gs[b], j + 1)
                        dve.scalar_tensor_tensor(out=scratch[b][:, j, :], in0=own(b, (2 * j + 1) % 4),
                                                 scalar=col["w2_s"][:, j:j + 1], in1=w4[b][:, j, :],
                                                 op0=ALU.mult, op1=ALU.mult).then_inc(s_gh[b], 1)
                if step == "down":
                    dve.wait_ge(s_dn[b], 1)
                    dve.scalar_tensor_tensor(out=z[b][:, :], in0=own(b, 0), scalar=col["w3_s"], in1=state(b),
                                             op0=ALU.mult, op1=ALU.add).then_inc(s_z[b], 1)

        @block.gpsimd
        def _(pool):
            def fill(stack, first, end, value):
                return pool.memset(stack[first:end, :, :].rearrange("p h t -> p (h t)").bitcast(F32), value)

            fill(kstack[0], 32, 64, ONES).then_inc(s_zero, 1)
            pool.wait_ge(s_zero, 1)
            fill(kstack[0], 64, P, 0.0).then_inc(s_zero, 1)
            loaded(pool, "const")
            pool.wait_ge(s_zero, 2)
            pool.tensor_copy(ident_b[:, :], ident)
            pool.tensor_copy(mask_b[:, :], w["const"][:, 4 * P:5 * P]).then_inc(s_zero, 1)
            pool.wait_ge(s_zero, 3)
            pool.memset(v0[:, :, :, :, :].rearrange("p b k h c -> p (b k h c)"), 0.0).then_inc(s_zero, 1)
            pool.wait_ge(s_zero, 4)
            pool.memset(v0[:, :, :, :, D0:D0 + 1].rearrange("p b k h c -> p (b k h) c"), 1.0).then_inc(s_zero, 1)
            pool.wait_ge(s_zero, 5)
            fill(kx[0], 96, P, ONES).then_inc(s_zero, 1)
            pool.wait_ge(s_zero, 6)
            fill(kx[1], 32, 64, 0.0).then_inc(s_zero, 1)
            pool.wait_ge(s_zero, 7)
            fill(kx[1], 64, P, ONES).then_inc(s_zero, 1)
            pool.wait_ge(s_zero, 8)
            fill(kstack[1], 32, 64, ONES).then_inc(s_zero, 1)
            pool.wait_ge(s_zero, 9)
            fill(kstack[1], 64, P, 0.0).then_inc(s_zero, 1)
            pool.wait_ge(s_zero, 10)
            for L in range(2):
                last = pool.memset(vx[L][:, :, :, :], 0.0)
            last.then_inc(s_zero, 1)
            pool.wait_ge(s_zero, 11)
            for L in range(2):
                last = pool.memset(vx[L][:, :, :, DX[L]:DX[L] + 1], 1.0)
            last.then_inc(s_zero, 1)
            pool.wait_ge(s_zero, 12)

            for kind, n, j in items:
                if kind == "score":
                    v = NX * n + j
                    pool.wait_ge(s_exp, v + 1)
                    step, m = DIAGONALS[j]
                    view = probs[:, v % NPROB, 0:step * m].rearrange("p (m s) -> p m s", s=step)[:, :, 0:P]
                    pool.affine_select(out=view, in_=view, compare_op=ALU.is_ge, fill=0.0, base=0,
                                       pattern=[[0, m], [1, P]], channel_multiplier=-1).then_inc(s_mask, 1)

            loaded(pool, "mix")
            pool.wait_ge(s_param, 5)
            for i in range(3):
                wi = w["mix"][:, P * i:P * (i + 1)]
                pool.tensor_scalar(wmix[i][:, 0, :], wi, col["mix"][:, i:i + 1], None, ALU.mult).then_inc(s_wmix, 1)
                pool.tensor_scalar(wmix[i][:, 1, :], wi, omm[:, i:i + 1], None, ALU.mult).then_inc(s_wmix, 1)
            loaded(pool, "moe")

            for step, b, *at in steps:
                if step == "route":
                    pool.wait_ge(s_choice[b], 1)
                    for k in range(TOPK):
                        e = pool.value_load(choice[b][0:1, k:k + 1], min_val=0, max_val=NE - 1)
                        pool.tensor_copy(work[b][:, MOE * k:MOE * (k + 1)],
                                         w["moe"][:, bass.ds(e * MOE, MOE)]).then_inc(s_pick[b], 1)
                    pool.wait_ge(s_pick[b], TOPK)
                    pool.tensor_tensor(b2s[b][:, 0:1], work[b][:, MOE - 1:MOE], work[b][:, 2 * MOE - 1:2 * MOE],
                                       ALU.add).then_inc(s_b2s[b], 1)
                    pool.wait_ge(s_b2s[b], 1)
                    pool.tensor_scalar(b2s[b][:, 1:2], b2s[b][:, 0:1], 1.0 / TOPK, None, ALU.mult) \
                        .then_inc(s_b2s[b], 1)
                    pool.wait_ge(s_b2s[b], 2)
                    pool.tensor_scalar(qe[b][:, :], state(b), b2s[b][:, 1:2], None, ALU.add).then_inc(s_b2s[b], 1)
                if step == "mix_in":
                    s, (pp, _, _) = scratch[b], carried(wide[b])
                    pool.wait_ge(s_rscan[b], 3)
                    pool.tensor_tensor(s[:, 4, :], pp[:, 0:T], s[:, 7, :], ALU.subtract).then_inc(s_rpool[b], 1)
                if step == "mix_scan":
                    s = scratch[b]
                    pool.wait_ge(s_rexp[b], 1)
                    pool.wait_ge(s_rscan[b], 6)
                    pool.wait_ge(s_rpool[b], 1)
                    pool.wait_ge(s_rcp[b], 2)
                    pool.tensor_tensor(s[:, 7, :], s[:, 3, :], s[:, 1, :], ALU.mult).then_inc(s_rpool[b], 1)
                    pool.wait_ge(s_rpool[b], 2)
                    pool.wait_ge(s_rexp[b], 2)
                    pool.tensor_tensor(s[:, 1, :], s[:, 5, :], s[:, 1, :], ALU.mult).then_inc(s_rpool[b], 1)


MIX_DVE = 14
MOE = 2 * P + 2


def carried(area):
    return [area[:, (T + 1) * i:(T + 1) * (i + 1)] for i in range(3)]


_COLS = [("bq", 1), ("bk", 1), ("bo", 1), ("ln1_g", 1), ("ln1_b", 1), ("ln2_g", 1), ("ln2_b", 1), ("ffn_b1", NF),
         ("ffn_b2", 1), ("lambda", 1), ("decay", 1), ("first", 1), ("mix", 3), ("xbq", 1), ("xbk", 1), ("xbo", 1),
         ("w1_s", NF), ("w2_s", NF), ("h1_s", NF), ("h2_s", NF), ("w3_s", 1)]
COLS, _at = [], 0
for _name, _n in _COLS:
    COLS.append((_name, _at, _n))
    _at += _n
NCOL = _at

LOADS = {
    "x": ([P, NB * T], F32), "qk": ([P, 2 * P], F32), "cols": ([P, NCOL], F32), "const": ([P, 5 * P], F32),
    "v0": ([P, 2 * P], F32), "ctx": ([P, NB * NKEY], F32), "xkv": ([P, 4 * P], F32), "xbv": ([1, P], F32),
    "o0": ([P, NG0 * P], F32), "xq": ([P, 2 * P], F32), "xo": ([P, 6 * P], F32), "ffn": ([P, 2 * NF * P], F32),
    "route": ([P, 2 * NE], F32), "moe": ([P, NE * MOE], F32), "mix": ([P, 4 * P], F32),
    "gate": ([P, 3 * NF * P], F32), "h1": ([P, NF, NF * P], F32), "h2": ([P, NF, NF * P], F32),
}
LOAD_GROUPS = {"x": ["x"], "qk": ["qk"], "cols": ["cols"], "const": ["const"],
               "context": ["v0", "ctx", "xkv", "xbv"], "project": ["o0", "xq", "xo"],
               "ffn": ["ffn", "route", "moe"], "mix": ["mix", "gate"]}


def laid_out(i):
    import numpy as np

    i = {k: np.asarray(v) for k, v in i.items()}

    def by_feature(a, heads):
        return a.reshape(*a.shape[:-1], heads, -1).swapaxes(-1, -2).reshape(a.shape)

    def column(a, n=1):
        return np.broadcast_to(a, (P,)).reshape(P, 1) if a.ndim == 0 else a.reshape(n, P).T

    def padded(wo, d):
        g = wo.reshape(-1, G, d, P)
        out = np.zeros((g.shape[0], G, VW, P), np.float32)
        out[:, :, :d] = g
        return out.reshape(-1, P, P).transpose(1, 0, 2).reshape(P, -1)

    def in_rows(a):
        return a.reshape(-1, P, a.shape[-1]).transpose(1, 0, 2).reshape(P, -1)

    out = {}
    out["x"] = i["x"].transpose(2, 0, 1).reshape(P, NB * T)
    wq, wk, wv = np.split(i["L0_attn_w_attn"].T, 3, axis=1)
    bq, bk, bv = np.split(i["L0_attn_b_attn"], 3)
    out["qk"] = np.concatenate([by_feature(wq, H0), by_feature(wk, H0)], 1)
    row = np.zeros((P, P), np.float32)
    row[0] = bv
    out["v0"] = np.concatenate([wv, row], 1)
    out["ctx"] = i["ctx_1024"].transpose(2, 0, 1).reshape(P, NB * NKEY)
    out["xkv"] = np.concatenate([by_feature(i["L0_xattn_Wk"], HX[0]), i["L0_xattn_Wv"],
                                 by_feature(i["L1_xattn_Wk"], HX[1]), i["L1_xattn_Wv"]], 1)
    out["xbv"] = i["L1_xattn_bv"].reshape(1, P)
    out["o0"] = padded(i["L0_attn_w_proj"].T, D0)
    out["xq"] = np.concatenate([by_feature(i["L0_xattn_Wq"], HX[0]), by_feature(i["L1_xattn_Wq"], HX[1])], 1)
    out["xo"] = np.concatenate([padded(i["L0_xattn_Wo"], DX[0]), padded(i["L1_xattn_Wo"], DX[1])], 1)
    out["ffn"] = np.concatenate([i["L0_xattn_ffn_w1"], in_rows(i["L0_xattn_ffn_w2"])], 1)
    br = np.zeros((P, NE), np.float32)
    br[0] = i["L0_ffn_br"]
    out["route"] = np.concatenate([i["L0_ffn_Wr"], br], 1)
    out["moe"] = np.concatenate([i["L0_ffn_W1"], i["L0_ffn_W2"], i["L0_ffn_b1"][:, :, None],
                                 i["L0_ffn_b2"][:, :, None]], 2).transpose(1, 0, 2).reshape(P, -1)
    out["mix"] = np.concatenate([i[f"L1_attn_W{k}"].T for k in "kvro"], 1)
    out["gate"] = np.concatenate([i["L1_ffn_w1_w"].T, i["L1_ffn_w2_w"].T, in_rows(i["L1_ffn_w3_w"].T)], 1)
    for k in ("h1", "h2"):
        out[k] = in_rows(i[f"L1_ffn_{k}_w"].T).reshape(P, NF, NF * P)
    mix = np.stack([i[f"L1_attn_time_mix_{k}"].reshape(P) for k in "kvr"], 1)
    cols = {
        "bq": by_feature(bq, H0), "bk": by_feature(bk, H0), "bo": i["L0_attn_b_proj"],
        "ln1_g": i["L0_xattn_ln1_g"], "ln1_b": i["L0_xattn_ln1_b"], "ln2_g": i["L0_xattn_ln2_g"],
        "ln2_b": i["L0_xattn_ln2_b"], "ffn_b1": i["L0_xattn_ffn_b1"], "ffn_b2": i["L0_xattn_ffn_b2"],
        "lambda": i["L0_xattn_lambda_param"], "decay": i["L1_attn_time_decay"], "first": i["L1_attn_time_first"],
        "xbq": by_feature(i["L1_xattn_bq"], HX[1]), "xbk": by_feature(i["L1_xattn_bk"], HX[1]),
        "xbo": i["L1_xattn_bo"], "w1_s": i["L1_ffn_w1_s"], "w2_s": i["L1_ffn_w2_s"], "h1_s": i["L1_ffn_h1_s"],
        "h2_s": i["L1_ffn_h2_s"], "w3_s": i["L1_ffn_w3_s"],
    }
    out["cols"] = np.concatenate([mix if n == "mix" else column(cols[n], k) for n, _, k in COLS], 1)

    eye = np.eye(P, dtype=np.float32)
    p = np.arange(P)
    const = [eye - 1.0 / P, np.full((P, P), 1.0 / P), eye]
    const += [np.ones((P, P)), np.where(p[None, :] > p[:, None], -1e30, 0.0)]
    out["const"] = np.concatenate(const, 1).astype(np.float32)
    return out


def kernel(**inputs):
    import numpy as np
    import concourse.bacc as bacc
    from concourse.bass_utils import run_bass_kernel_spmd

    nc = bacc.Bacc("TRN2", target_bir_lowering=False, num_devices=1)
    arrays, dram = {}, {}
    for name, a in laid_out(inputs).items():
        a = np.ascontiguousarray(a)
        arrays[f"in_{name}"] = a
        dram[name] = nc.dram_tensor(f"in_{name}", a.shape, mybir.dt.from_np(a.dtype), kind="ExternalInput").ap()
    out = nc.dram_tensor("out", [P, NB * T], F32, kind="ExternalOutput").ap()
    decoder(nc, dram, out)
    r = run_bass_kernel_spmd(nc, [arrays], core_ids=[0])
    return r.results[0]["out"].reshape(P, NB, T).transpose(1, 2, 0)
```

```python
from contextlib import ExitStack

import concourse.bass as bass
from concourse import mybir

F32 = mybir.dt.float32
BF16 = mybir.dt.bfloat16
F32R = mybir.dt.float32r
U32 = mybir.dt.uint32
ALU = mybir.AluOpType
ACT = mybir.ActivationFunctionType
AX = mybir.AxisListType

P = 128
NB = 2
T = 512
TT = T // P
NKEY = 77
NE = 8
TOPK = 2
NF = 4
EPS = 1e-5
VW = 32
H0, D0 = 16, 8
HX = (8, 16)
DX = (16, 8)
QPART = (0, 0, 1, 1, 0, 2)
KPART = (0, 1, 0, 1, 2, 0)
NS = len(QPART)
AUG0 = NS * D0
AUGX = (NS * DX[0], 64)
ONES = 1.0 + 0x3F80 / 2.0 ** 23
G = 4
NG0 = H0 // G
FIRST = {"q": 1, "val": 1, "split": 3, "stack": 16 * NS, "msc": TT * HX[0] // G, "mx": TT * HX[0] // G, "mt": 1,
         "mval": 1, "msplit": 3, "maug": 48, "sc": HX[0], "exp": HX[0], "pv": HX[0] // G,
         "den": HX[0] // G, "div": HX[0] // G, "out": 1}
LN_EXP = "natural_log_exp_and_others"
SCORE_BANKS = ((0, 1, 2, 6), (3, 6))
RING_BANKS = ((4, 5), (4, 5))
OUT_BANKS = ((3, 7), (7, 7))
OWN_BANKS = (3, 4)
NEG = -1e38

MAX_UNITS = [(0, 0, 4), (1, 0, 2), (1, 2, 2)] + [(i, h, 1) for i in (2, 3) for h in range(G)]
NM = len(MAX_UNITS)
EXP_UNITS = [[(h, 0, 0)] for h in range(G)] + [[(h, 3, 0), (h, 1, 128)] for h in range(G)] \
    + [[(0, 2, 0), (1, 2, 256)], [(2, 2, 0), (3, 2, 256)]]
NX = len(EXP_UNITS)
DIAGONALS = [(T, 1)] * G + [(P, 2)] * G + [(256, 2)] * 2
VALUE_UNITS = {"values0": range(0, 4), "values1": range(4, 8), "values2": range(8, 10)}
NPROB = 8
LAG = 1.85
TURNS = {
    "tensor":
        "c163 a1 c8 a1 c3 a1 c18 a1 c2 a2 c3 a2 c1 a1 c1 a2 c2 a1 c11 a2 c2 a1 c3 a8 c1 a3 b2 a1 b1 a2 b1 "
        "a1 b4 a1 b3 a1 b1 a1 b2 a1 b2 a1 b4 a1 b6 a3 b1 a1 b2 a3 b2 a1 b1 a1 b1 a1 b1 a1 b1 a1 b1 a6 b1 a4 "
        "b2 a3 b1 a3 b3 a11 b1 a2 b1 a7 b1 a8 b1 a1 b4 a1 b5 a1 b8 a4 b2 a2 b2 a1 b1 a1 b6 a1 b1 a1 b2 a1 "
        "b1 a1 b3 a1 b1 a1 b2 a1 b4 a2 b3 a8 b1 a4 b1 a3 b1 a9 b2 a1 b1 a2 b4 a1 b20 a1 b17 a1 b3",
    "scalar":
        "c167 a2 c14 a9 c21 a1 c13 a5 c3 a10 b11 a5 b1 a1 b2 a1 b2 a2 b8 a2 b3 a2 b2 a2 b2 a2 b1 a1 b1 a1 "
        "b1 a17 b6 a1 b2 a7 b2 a9 b1 a10 b1 a3 b17 a2 b1 a8 b26 a5 b3 a20 b2 a10 b3 a2 b25 a1 b17 a1 b2",
    "vector":
        "a1 b1 c172 a1 c16 a1 c17 a8 c3 a10 c8 a1 c1 a2 c1 a2 b1 a2 b1 a2 b5 a2 b13 a3 b1 a2 b3 a2 b3 a2 b2 "
        "a2 b2 a2 b2 a2 b1 a1 b2 a7 b2 a8 b1 a10 b3 a1 b2 a16 b1 a2 b1 a2 b16 a1 b10 a8 b18 a5 b1 a15 b2 a5 "
        "b1 a10 b3 a1 b5 a2 b38 a1 b1",
    "gpsimd":
        "c22 b3 a35 c196 b32 a107 b107",
    "sync":
        "c13 a2 b2 c174 a9 c31 a35 b44 a95 b95 a1 b1",
}


def causal_items(engine):
    items = []
    for n in range(NB * NG0):
        items += [(n + j / NM, "max", n, j) for j in range(NM)]
        items.append((n + 1 + (2.1 if engine == "vector" else 1.5) / NM, "rowmax", n, 0))
        parts = [("score", n, 0), ("score", n, 1), ("values1", n - 1, 0), ("score", n, 2), ("score", n, 3),
                 ("values2", n - 1, 0), ("score", n, 4), ("denominator", n - 1, 0), ("score", n, 5),
                 ("score", n, 6), ("divide", n - 1, 0), ("values0", n, 0), ("score", n, 7), ("score", n, 8),
                 ("score", n, 9)]
        items += [(n + LAG + k / len(parts), *part) for k, part in enumerate(parts) if part[1] >= 0]
    last = NB * NG0 - 1
    items += [(last + LAG + 1, "values1", last, 0), (last + LAG + 1.05, "values2", last, 0)]
    items += [(last + LAG + 1.1, "denominator", last, 0), (last + LAG + 1.12, "divide", last, 0)]
    for b in range(NB):
        items.append((NG0 * (b + 1) + LAG + 0.95 + 0.3 * b + (0.2 if engine == "vector" else 0), "project", b, 0))
    return [tuple(i) for _, *i in sorted(items, key=lambda i: i[0])]


def later_steps():
    def norm(n):
        return [(f"norm_mean{n}",), (f"norm_var{n}",)]

    def cross(L):
        groups = HX[L] // G
        out = [(f"cross_query{L}",)] + [(f"cross_max{L}", i, g) for i in range(TT) for g in range(groups)]
        out += [(f"cross_rowmax{L}",)]
        for g in range(groups + 1):
            if g < groups:
                out += [(f"cross_score{L}", G * g + k) for k in (0, 1)]
            if g:
                out.append((f"cross_values{L}", g - 1))
            if g < groups:
                out += [(f"cross_score{L}", G * g + k) for k in (2, 3)]
            if g:
                out += [(f"cross_den{L}", g - 1), (f"cross_div{L}", g - 1)]
        return out + [(f"cross_out{L}",)]

    chain = norm(0) + cross(0) + norm(1) + [("ffn_up",), ("ffn_down",)] + norm(2) + norm(3)
    chain += [("route",), ("expert_up",), ("expert_down",)] + norm(4)
    chain += [("mix_in",), ("mix_scan",), ("mix_divide",), ("mix_out",)] + norm(5)
    chain += cross(1) + norm(6) + [("gate", j) for j in range(NF)]
    chain += [(step, j, k) for step in ("hidden1", "hidden2") for j in range(NF) for k in range(NF + 1)]
    chain += [("down",)] + norm(7)
    return chain


def order(engine):
    streams = {"c": [(kind, n, j, "", n if kind == "project" else n // NG0, ()) for kind, n, j in causal_items(engine)]}
    for b, name in enumerate("ab"):
        streams[name] = [("", 0, 0, step, b, tuple(args)) for step, *args in later_steps()]
    following = {name: iter(stream) for name, stream in streams.items()}
    return [next(following[turn[0]]) for turn in TURNS[engine].split() for _ in range(int(turn[1:]))]


def decoder(nc, dram, out):
    ctx, over = ExitStack(), ExitStack()
    with ctx:
        def sb(name, shape, dt=F32):
            return ctx.enter_context(nc.sbuf_tensor(name, shape, dt))

        area, places = {}, []

        def below(name, shape, dt=F32):
            area[name] = over.enter_context(nc.sbuf_tensor(name, shape, dt))
            size = 1
            for n in shape[1:]:
                size *= n
            places.append((name, size * (2 if dt == BF16 else 4) // 4))

        for name in ("gate", "qk", "v0", "xkv", "o0"):
            below("w_" + name, LOADS[name][0])
        below("v0", [P, NB, TT, H0, VW])
        below("probs", [P, NPROB, T])
        for b in range(NB):
            below(f"z{b}", [P, T])
            below(f"sq{b}", [P, T])
            below(f"qstack{b}", [P, H0, T], BF16)
            below(f"kstack{b}", [P, H0, T], BF16)
            below(f"wide{b}", [P, 4 * T])
        over.close()
        fp32r = {name: sb(name + "_r", [P, size], F32R) for name, size in places}

        def sem(name):
            return ctx.enter_context(nc.semaphore(name))

        def sems(name):
            return [sem(f"{name}_{b}") for b in range(NB)]

        w = {}
        for name, (shape, _) in LOADS.items():
            if name in ("h1", "h2", "x"):
                continue
            w[name] = area.get("w_" + name) or sb("w_" + name, shape)
        center, mean, ident = (w["const"][:, P * i:P * (i + 1)] for i in range(3))
        ones = w["const"][0:1, 3 * P:4 * P]
        ident_b = sb("ident_b", [P, P], BF16)
        mask_b = sb("mask_b", [P, P], BF16)
        col = {name: w["cols"][:, i:i + n] for name, i, n in COLS}

        def pair(name, shape, dt=F32):
            return [sb(f"{name}{b}", shape, dt) for b in range(NB)]

        xs = pair("xs", [P, T + 1])
        qe = pair("qe", [P, T])
        z = [area[f"z{b}"] for b in range(NB)]
        sq = [area[f"sq{b}"] for b in range(NB)]
        rstd = pair("rstd", [P, T])
        qstack = [area[f"qstack{b}"] for b in range(NB)]
        kstack = [area[f"kstack{b}"] for b in range(NB)]
        work = pair("work", [P, 1792])
        wide = [area[f"wide{b}"] for b in range(NB)]
        kx = [sb(f"kx{L}", [P, HX[L], NB * NKEY], BF16) for L in range(2)]
        vx = [sb(f"vx{L}", [NKEY, NB, HX[L], VW]) for L in range(2)]
        v0, probs = area["v0"], area["probs"]
        mx = pair("mx", [P, TT * H0])
        mt = pair("mt", [64, 2, P])
        mp = pair("mp", [64, 3, P], BF16)
        wmix = [sb(f"wmix{i}", [P, 2, P]) for i in range(3)]
        omm = sb("omm", [P, 3])
        decay = sb("decay", [P, 2])
        keep = sb("keep", [P, 3])
        eps = sb("eps", [P, 1])
        b2s = pair("b2s", [P, 2])
        route = pair("route", [1, 16])
        choice = pair("choice", [1, 8], U32)
        def matrices(area):
            return [area[:, 4 * T * i:4 * T * (i + 1)].rearrange("p (k n) -> p k n", k=NF) for i in range(2)]

        wh = matrices(v0[:, :, :, :, :].rearrange("p b a h c -> p (b a h c)"))
        wh_rest = matrices(fp32r["v0"])
        wh_first = matrices(fp32r["probs"])
        wg_rest = [fp32r["w_gate"][:, P * i:P * (i + 1)] for i in range(3 * NF)]
        wg_first = [fp32r["w_" + name][:, P * i:P * (i + 1)]
                    for name, n in (("qk", 2), ("v0", 2), ("xkv", 4), ("o0", 4)) for i in range(n)]
        qx = [kstack[b][:, 0:8, :] for b in range(NB)]
        scratch = [kstack[b][:, :, :].rearrange("p h t -> p (h t)").bitcast(F32).rearrange("p (j t) -> p j t", t=T)
                   for b in range(NB)]
        w4 = [wide[b][:, :].rearrange("p (j t) -> p j t", t=T) for b in range(NB)]

        def tiles(b, *names):
            return [fp32r[f"{name}{b}"][:, T * j:T * (j + 1)] for name in names
                    for j in range(fp32r[f"{name}{b}"].shape[1] // T)]

        inner = []
        for b in range(NB):
            values = [scratch[b][:, j, :] for j in range(2 * NF)] + [w4[b][:, j, :] for j in range(NF)]
            firsts = tiles(b, "qstack") + tiles(b, "kstack")[0:NF]
            inner.append([[(values[i], firsts[i], rest) for i, rest in enumerate(tiles(b, "kstack", "wide"))][n:n + NF]
                          for n in (0, NF, 2 * NF)])

        xmx = [qe[b][:, 0:64] for b in range(NB)]
        xmt = [qe[b][0:64, 64:320].rearrange("p (i t) -> p i t", i=2) for b in range(NB)]
        xmp = [qe[b][0:64, 320:512].bitcast(BF16).rearrange("p (i t) -> p i t", i=3) for b in range(NB)]

        def state(b):
            return xs[b][:, 1:T + 1]

        def split_tiles(area, n):
            parts = area[:, 2 * n:2 * n + 3 * n // 2].bitcast(BF16).rearrange("p (i t) -> p i t", i=3)
            return area[:, 0:n], area[:, n:2 * n], parts

        q_split = [split_tiles(work[b], T) for b in range(NB)]
        k_split = [split_tiles(wide[b], T) for b in range(NB)]
        kx_split = [(z[L][:, 0:NB * NKEY], z[L][:, NB * NKEY:2 * NB * NKEY],
                     qe[L][:, 0:3 * NB * NKEY // 2].bitcast(BF16).rearrange("p (i t) -> p i t", i=3))
                    for L in range(2)]

        psum = ctx.enter_context(nc.psum_tensor("psum", [P, 8, 512], F32))

        def bank(i):
            return psum[:, i, :]

        def den_tile(b, g):
            return (rstd, sq)[g % 2][b][:, :]

        def cross_probs(L, b, h):
            free = [scratch[b][:, G + i, :] for i in range(G)] + [w4[b][:, 2, :], w4[b][:, 3, :]] \
                + [work[b][:, 0:T], work[b][:, T:2 * T]]
            at = free[h] if L == 0 else scratch[b][:, h % (2 * G), :]
            return at[0:NKEY, :]

        def own(b, i):
            return psum[:, 4 * b + i, :]

        s_load = {name: sem("load_" + name) for name in LOAD_GROUPS}

        def loaded(engine, name):
            group = next(g for g, names in LOAD_GROUPS.items() if name in names)
            n = len(LOAD_GROUPS[group]) if group != "x" else NB
            engine.wait_ge(s_load[group], 16 * n)

        s_zero = sem("zeroed")
        s_vzero = sem("vzero")
        s_qk = sem("qk_proj")
        s_qk_val = sem("qk_value")
        s_qk_split = sem("qk_split")
        s_stack = [sem(f"stack{u}") for u in range(4)]
        s_v0 = sem("v0_proj")
        s_v0_out = sem("v0_out")
        s_kx = sem("kx_proj")
        s_kx_val = sem("kx_value")
        s_kx_split = sem("kx_split")
        s_kx_stack = sem("kx_stack")
        s_vx = sem("vx_proj")
        s_vx_out = sem("vx_out")
        s_wmix = sem("wmix")
        s_small = sem("small")
        s_param = sem("param")
        s_msc = sem("max_scores")
        s_mx = sem("max_done")
        s_mt = sem("rowmax_turned")
        s_mval = sem("rowmax_value")
        s_msplit = sem("rowmax_split")
        s_maug = sem("rowmax_rows")
        s_sc = sem("exp_scores")
        s_exp = sem("exp_done")
        s_mask = sem("masked")
        s_pv = sem("values_done")
        s_den = sem("denominators")
        s_rec = sem("reciprocal")
        s_div = sem("divided")
        s_proj = sems("projected")
        s_wh = sem("load_wh")
        s_z, s_cent, s_sq, s_var, s_rstd, s_aff, s_x = (
            sems(n) for n in ("residual", "centered", "squared", "variance", "rstd", "gained", "state"))
        x_q, x_val, x_split, x_stack, x_msc, x_mx, x_mt, x_mval, x_msplit, x_maug, x_sc, x_exp, x_pv, \
            x_den, x_div, x_out = (sems("x_" + n) for n in (
                "query", "value", "split", "stack", "max_scores", "max_done", "rowmax", "mval", "msplit", "maug",
                "scores", "exp", "values", "den", "div", "out"))
        s_ln = sems("log_variance")
        x_rec = sems("x_reciprocal")
        s_up, s_relu, s_down = (sems(n) for n in ("ffn_up", "ffn_relu", "ffn_down"))
        s_rt, s_rchain, s_choice, s_pick, s_b2s, s_eup, s_egelu, s_edown = (
            sems(n) for n in ("route_scores", "route_chain", "choice", "picked", "expert_bias", "expert_up",
                              "expert_gelu", "expert_down"))
        s_rk, s_rcp, s_rscan, s_rpool, s_rexp, s_rout = (
            sems(n) for n in ("mix_proj", "mix_copied", "mix_dve", "mix_pool", "mix_exp", "mix_out"))
        s_ga, s_gs, s_gb, s_gh, s_h1, s_g1, s_h2, s_g2, s_dn = (
            sems(n) for n in ("gate_a", "gate_silu", "gate_b", "gated", "hid1", "gelu1", "hid2", "gelu2", "down"))
        s_first, s_rest = sems("first_part"), sems("rest")
        s_wfirst, s_wrest = sem("weight_first"), sem("weight_rest")
        s_store = sem("stored")

        course = order("tensor")
        users = {i: [] for i in range(8)}
        ring = [part[0:3] for part in course if part[0] in ("max", "rowmax")]
        for kind, n, j, _, b, _ in course:
            if kind == "score":
                users[SCORE_BANKS[b][(NX * n + j) % len(SCORE_BANKS[b])]].append((kind, n, j))
            if (kind, n, j) in ring:
                users[RING_BANKS[b][ring.index((kind, n, j)) % len(RING_BANKS[b])]].append((kind, n, j))

        def item_bank(kind, n, j=0):
            return bank(next(i for i in users if (kind, n, j) in users[i]))

        def out_bank(n):
            return OUT_BANKS[n // NG0][n % 2]

        block = ctx.enter_context(nc.Block())

        @block.sync
        def _(sp):
            def load(name):
                group = next(g for g, names in LOAD_GROUPS.items() if name in names)
                sp.dma_start(w[name][:], dram[name]).then_inc(s_load[group], 16)

            for name in ("x", "qk", "cols", "const"):
                if name == "x":
                    for b in range(NB):
                        sp.dma_start(state(b), dram["x"][:, T * b:T * (b + 1)]).then_inc(s_load["x"], 16)
                else:
                    load(name)
            for name in LOAD_GROUPS["context"]:
                load(name)

            def stack(dst, parts, which, d, done, split, n, value, m):
                for part in range(3):
                    if part == 0:
                        sp.wait_ge(value, m)
                    else:
                        sp.wait_ge(split, n + part + 1)
                    for s in range(NS):
                        if which[s] == part:
                            sp.dma_start(dst[d * s:d * (s + 1)], parts[:, part, :]).then_inc(done, 16)

            def stacks(b):
                if b == 0:
                    sp.wait_ge(s_vzero, 1)
                else:
                    sp.wait_ge(s_zero, 13)
                stack(qstack[b], q_split[b][2], QPART, D0, s_stack[2 * b], s_qk_split, 6 * b, s_qk_val, 2 * b + 1)
                sp.wait_ge(s_zero, 8 * b + 1)
                stack(kstack[b], k_split[b][2], KPART, D0, s_stack[2 * b + 1], s_qk_split, 6 * b + 3, s_qk_val,
                      2 * b + 2)

            stacks(0)
            for group in ("project", "ffn", "mix"):
                for name in LOAD_GROUPS[group]:
                    load(name)
            for kind, n, j, step, b, at in order("sync"):
                nb = OWN_BANKS[b]
                if kind == "rowmax":
                    g = n % NG0
                    sp.wait_ge(s_msplit, 3 * (n + 1))
                    for i in range(3):
                        dst = qstack[b][AUG0 + i:AUG0 + i + 1, G * g:G * (g + 1), :]
                        sp.dma_start(dst, mp[n % 2][0:G * TT, i, :]).then_inc(s_maug, 16)
                    if n == 1:
                        stacks(1)
                    if n == 3:
                        for L in range(2):
                            sp.wait_ge(s_zero, 8)
                            stack(kx[L], kx_split[L][2], KPART, DX[L], s_kx_stack, s_kx_split, 3 * L, s_kx_val,
                                  L + 1)
                if step == "cross_query0" and b == 1:
                    sp.wait_ge(s_pv, NX * NB * NG0)
                    for i in range(2):
                        sp.dma_start(wh[i], dram[f"h{i + 1}"]).then_inc(s_wh, 16)
                for L in range(2):
                    if step == f"cross_query{L}":
                        stack(qx[b] if L == 0 else qstack[b], q_split[b][2], QPART, DX[L], x_stack[b],
                              x_split[b], L * FIRST["split"], x_val[b], L + 1)
                    if step == f"cross_rowmax{L}":
                        q = qx[b] if L == 0 else qstack[b]
                        for i in range(3):
                            if i == 0:
                                sp.wait_ge(x_mval[b], L + 1)
                            else:
                                sp.wait_ge(x_msplit[b], L * FIRST["msplit"] + i + 1)
                            dst = q[AUGX[L] + i:AUGX[L] + i + 1, :, :]
                            sp.dma_start(dst, xmp[b][0:HX[L] * TT, i, :]).then_inc(x_maug[b], 16)
                if step == "norm_var7":
                    sp.wait_ge(s_x[b], 7)
                    sp.dma_start(out[:, T * b:T * (b + 1)], state(b)).then_inc(s_store, 16)
            sp.wait_ge(s_store, 16 * NB)

        @block.tensor
        def _(pe):
            loaded(pe, "x")
            loaded(pe, "qk")
            for u in range(2 * NB):
                pe.matmul(bank(u), w["qk"][:, P * (u % 2):P * (u % 2 + 1)], state(u // 2),
                          start=True, stop=True).then_inc(s_qk, 1)
            loaded(pe, "const")
            loaded(pe, "v0")
            for L in range(2):
                pe.matmul(psum[:, 6, 256 * L:256 * L + NB * NKEY], w["xkv"][:, 2 * P * L:2 * P * L + P],
                          w["ctx"][:, :], start=True, stop=True, skip_group_check=True).then_inc(s_kx, 1)
            for b in range(NB):
                pe.wait_ge(s_qk_val, b + 1)
                for k in range(TT):
                    o = psum[:, b, P * k:P * (k + 1)]
                    pe.matmul(o, state(b)[:, P * k:P * (k + 1)], w["v0"][:, 0:P], start=True, stop=False)
                    mm = pe.matmul(o, ones, w["v0"][0:1, P:2 * P], start=False, stop=True)
                mm.then_inc(s_v0, 1)
            pe.wait_ge(s_qk_val, 3)
            for L in range(2):
                for b in range(NB):
                    o = psum[0:NKEY, 2, P * (2 * L + b):P * (2 * L + b + 1)]
                    pe.matmul(o, w["ctx"][:, NKEY * b:NKEY * (b + 1)], w["xkv"][:, 2 * P * L + P:2 * P * (L + 1)],
                              start=True, stop=L == 0)
                    if L == 1:
                        mm = pe.matmul(o, ones[:, 0:NKEY], w["xbv"][0:1, :], start=False, stop=True)
            mm.then_inc(s_vx, 1)

            def turn(kind, n, j=0):
                i = next(i for i in users if (kind, n, j) in users[i])
                at = users[i].index((kind, n, j))
                if at > 0:
                    kind, n, j = users[i][at - 1]
                    if kind == "max":
                        pe.wait_ge(s_mx, NM * n + j + 1)
                    if kind == "rowmax":
                        pe.wait_ge(s_mval, n + 1)
                    if kind == "score":
                        pe.wait_ge(s_exp, NX * n + j + 1)
                return bank(i)

            def product(o, first, rest, src, start, stop, with_first, with_rest):
                _, src_first, src_rest = src
                if with_first:
                    mm = pe.matmul(o, first, src_first, start=start, stop=False)
                    mm = pe.matmul(o, rest, src_first, start=False, stop=stop and not with_rest)
                if with_rest:
                    mm = pe.matmul(o, first, src_rest, start=False, stop=stop)
                return mm

            for kind, n, j, step, b, at in order("tensor"):
                nb = OWN_BANKS[b]
                g = n % NG0
                if kind == "max":
                    i, h0, nh = MAX_UNITS[j]
                    if g == 0 and j == 0:
                        pe.wait_ge(s_stack[2 * b], 16 * NS)
                        pe.wait_ge(s_stack[2 * b + 1], 16 * NS)
                        pe.wait_ge(s_zero, 7 * b + 3)
                    o = turn(kind, n, j)
                    width = P * (i + 1)
                    for k in range(nh):
                        h = G * g + h0 + k
                        pe.matmul(o[:, width * k:width * (k + 1)], qstack[b][:, h, P * i:P * (i + 1)],
                                  kstack[b][:, h, 0:width], start=True, stop=True, skip_group_check=True)
                        mm = pe.matmul(o[:, width * (k + 1) - P:width * (k + 1)], ident_b[:, :], mask_b[:, :],
                                       start=False, stop=True, skip_group_check=True)
                    mm.then_inc(s_msc, 1)
                if kind == "rowmax":
                    o = turn(kind, n)
                    pe.wait_ge(s_mx, NM * (n + 1))
                    pe.transpose(o[0:G * TT, 0:P], mx[n % 2][:, 0:G * TT], ident).then_inc(s_mt, 1)
                if kind == "score":
                    v = NX * n + j
                    if j == 0:
                        pe.wait_ge(s_maug, 48 * (n + 1))
                    o = turn(kind, n, j)
                    if n == NG0 and j == 0:
                        pe.wait_ge(s_div, n - 1)
                    if v < len(SCORE_BANKS[0]):
                        pe.wait_ge(s_kx_val, 2)
                        pe.wait_ge(s_qk_val, 4)
                        pe.wait_ge(s_v0_out, 2)
                        pe.wait_ge(s_vx_out, 4)
                    for h, k, c in EXP_UNITS[j]:
                        width = T - P * k
                        mm = pe.matmul(o[:, c:c + width], kstack[b][:, G * g + h, P * k:P * (k + 1)],
                                       qstack[b][:, G * g + h, P * k:T], start=True, stop=True,
                                       skip_group_check=True)
                    mm.then_inc(s_sc, 1)
                if kind in VALUE_UNITS:
                    units = VALUE_UNITS[kind]
                    pe.wait_ge(s_mask, NX * n + units[-1] + 1)
                    if units[0] == 0 and n >= 2:
                        pe.wait_ge(s_div, n - 1 if n < NG0 else n)
                    blocks = [(k, h, u, c) for u in units for h, k, c in EXP_UNITS[u]]
                    for k, h, u, c in sorted(blocks):
                        width = T - P * k
                        mm = pe.matmul(psum[VW * h:VW * (h + 1), out_bank(n), P * k:T], v0[:, b, k, G * g + h, :],
                                       probs[:, (NX * n + u) % NPROB, c:c + width], start=k == 0, stop=k == 2,
                                       skip_group_check=True, tile_position=(0, VW * h))
                    mm.then_inc(s_pv, len(units))
                if kind == "project":
                    if b == 0:
                        loaded(pe, "o0")
                    pe.wait_ge(s_div, NG0 * (b + 1))
                    for k in range(NG0):
                        mm = pe.matmul(own(b, 2), w["o0"][:, P * k:P * (k + 1)], w4[b][:, k, :],
                                       start=k == 0, stop=k == NG0 - 1)
                    mm.then_inc(s_proj[b], 1)

                if step.startswith("norm_mean"):
                    pe.wait_ge(s_z[b], int(step[-1]) + 1)
                    pe.matmul(own(b, 0), center, z[b][:, :], start=True, stop=True).then_inc(s_cent[b], 1)
                if step.startswith("norm_var"):
                    pe.wait_ge(s_sq[b], int(step[-1]) + 1)
                    pe.matmul(own(b, 1), mean, sq[b][:, :], start=True, stop=True).then_inc(s_var[b], 1)
                for L in range(2):
                    q = qx[b] if L == 0 else qstack[b]
                    if step == f"cross_query{L}":
                        loaded(pe, "xq")
                        pe.wait_ge(s_x[b], 1 if L == 0 else 5)
                        pe.matmul(own(b, 0), w["xq"][:, P * L:P * (L + 1)], state(b),
                                  start=True, stop=True).then_inc(x_q[b], 1)
                    if step == f"cross_max{L}":
                        i, g = at
                        u = i * (HX[L] // G) + g
                        if u == 0:
                            pe.wait_ge(x_stack[b], L * FIRST["stack"] + 16 * NS)
                            pe.wait_ge(s_kx_stack, 2 * 16 * NS)
                        if u >= nb:
                            pe.wait_ge(x_mx[b], L * FIRST["mx"] + u - nb + 1)
                        for k in range(G):
                            h = G * g + k
                            mm = pe.matmul(own(b, u % nb)[:, NKEY * k:NKEY * (k + 1)], q[:, h, P * i:P * (i + 1)],
                                           kx[L][:, h, NKEY * b:NKEY * (b + 1)], start=True, stop=True)
                        mm.then_inc(x_msc[b], 1)
                    if step == f"cross_rowmax{L}":
                        n = TT * HX[L]
                        pe.wait_ge(x_mx[b], L * FIRST["mx"] + TT * HX[L] // G)
                        pe.transpose(own(b, 2)[0:n, 0:P], xmx[b][:, 0:n], ident).then_inc(x_mt[b], 1)
                    if step == f"cross_score{L}":
                        h, = at
                        if h == 0:
                            pe.wait_ge(x_maug[b], L * FIRST["maug"] + 48)
                        if h >= 2:
                            pe.wait_ge(x_exp[b], L * FIRST["exp"] + h - 1)
                        pe.matmul(own(b, h % 2)[0:NKEY, :], kx[L][:, h, NKEY * b:NKEY * (b + 1)], q[:, h, :],
                                  start=True, stop=True).then_inc(x_sc[b], 1)
                    if step == f"cross_values{L}":
                        g, = at
                        pe.wait_ge(x_exp[b], L * FIRST["exp"] + G * (g + 1))
                        if g >= nb - 2:
                            pe.wait_ge(x_div[b], L * FIRST["div"] + g - nb + 3)
                        for k in range(G):
                            h = G * g + k
                            mm = pe.matmul(own(b, 2 + g % (nb - 2))[VW * k:VW * (k + 1), :], vx[L][:, b, h, :],
                                           cross_probs(L, b, h), start=True, stop=True, skip_group_check=True,
                                           tile_position=(0, VW * k))
                        mm.then_inc(x_pv[b], 1)
                    if step == f"cross_out{L}":
                        ng = HX[L] // G
                        loaded(pe, "xo")
                        pe.wait_ge(x_div[b], L * FIRST["div"] + ng)
                        for k in range(ng):
                            c = P * (2 * L + k)
                            mm = pe.matmul(own(b, 0), w["xo"][:, c:c + P], w4[b][:, k, :],
                                           start=k == 0, stop=k == ng - 1)
                        mm.then_inc(x_out[b], 1)
                if step == "ffn_up":
                    loaded(pe, "ffn")
                    pe.wait_ge(s_x[b], 2)
                    for j in range(NF):
                        if j >= nb:
                            pe.wait_ge(s_relu[b], j - nb + 1)
                        pe.matmul(own(b, j % nb), w["ffn"][:, P * j:P * (j + 1)], qe[b][:, :],
                                  start=True, stop=True).then_inc(s_up[b], 1)
                if step == "ffn_down":
                    for j in range(NF):
                        pe.wait_ge(s_relu[b], max(j + 1, 2))
                        mm = pe.matmul(own(b, 1), w["ffn"][:, P * (NF + j):P * (NF + j + 1)], w4[b][:, j, :],
                                       start=j == 0, stop=j == NF - 1)
                    mm.then_inc(s_down[b], 1)
                if step == "route":
                    loaded(pe, "route")
                    pe.wait_ge(s_x[b], 3)
                    pe.matmul(own(b, 2)[0:1, 0:NE], xs[b][:, 1:2], w["route"][:, 0:NE],
                              start=True, stop=True).then_inc(s_rt[b], 1)
                if step == "expert_up":
                    for k in range(TOPK):
                        pe.wait_ge(s_pick[b], k + 1)
                        pe.matmul(own(b, k), work[b][:, MOE * k:MOE * k + P], state(b),
                                  start=True, stop=True).then_inc(s_eup[b], 1)
                if step == "expert_down":
                    for k in range(TOPK):
                        pe.wait_ge(s_egelu[b], k + 1)
                        mm = pe.matmul(own(b, 2), work[b][:, MOE * k + P:MOE * k + 2 * P], w4[b][:, k, :],
                                       start=k == 0, stop=k == TOPK - 1)
                    mm.then_inc(s_edown[b], 1)
                if step == "mix_in":
                    pe.wait_ge(s_wmix, 6)
                    pe.wait_ge(s_x[b], 4)
                    for i in range(3):
                        pe.matmul(own(b, i), wmix[i][:, 0, :], state(b), start=True, stop=False)
                        pe.matmul(own(b, i), wmix[i][:, 1, :], xs[b][:, 0:T], start=False, stop=True) \
                            .then_inc(s_rk[b], 1)
                if step == "mix_out":
                    pe.wait_ge(s_rscan[b], MIX_DVE)
                    pe.matmul(own(b, 0), w["mix"][:, 3 * P:4 * P], scratch[b][:, 7, :],
                              start=True, stop=True).then_inc(s_rout[b], 1)
                if step == "gate":
                    loaded(pe, "gate")
                    pe.wait_ge(s_x[b], 6)
                    j, = at
                    if b == 0 and j == 0:
                        pe.wait_ge(s_exp, NX * NB * NG0)
                    if j >= 2:
                        pe.wait_ge(s_gs[b], j - 1)
                    if j == 0:
                        pe.wait_ge(s_wrest, 3 * NF)
                        pe.wait_ge(s_rest[b], 1)
                    x = (None, fp32r[f"z{b}"][:, :], fp32r[f"sq{b}"][:, :])
                    product(own(b, 2 * j % 4), wg_first[j], wg_rest[j], x, True, True, True, True) \
                        .then_inc(s_ga[b], 1)
                    if j >= 2:
                        pe.wait_ge(s_gh[b], j - 1)
                    product(own(b, (2 * j + 1) % 4), wg_first[NF + j], wg_rest[NF + j], x, True, True, True, True) \
                        .then_inc(s_gb[b], 1)
                for i, (name, done) in enumerate((("hidden1", s_h1), ("hidden2", s_h2))):
                    if step == name:
                        j, k = at
                        blocks = wh_first[i][:, :, P * j:P * (j + 1)], wh_rest[i][:, :, P * j:P * (j + 1)]
                        if k < NF:
                            if j == 0:
                                pe.wait_ge(s_first[b], 1 + NF * i + max(k + 1, 3 - 2 * i))
                            product(own(b, j), blocks[0][:, k], blocks[1][:, k], inner[b][i][k],
                                    k == 0, False, True, False)
                        else:
                            for k in range(NF):
                                if j == 0:
                                    pe.wait_ge(s_rest[b], 1 + NF * i + k + 1)
                                mm = product(own(b, j), blocks[0][:, k], blocks[1][:, k], inner[b][i][k],
                                             False, k == NF - 1, False, True)
                            mm.then_inc(done[b], 1)
                if step == "down":
                    for k in range(NF):
                        pe.wait_ge(s_first[b], 1 + 2 * NF + k + 1)
                        product(own(b, 0), wg_first[2 * NF + k], wg_rest[2 * NF + k], inner[b][2][k],
                                k == 0, False, True, False)
                    for k in range(NF):
                        pe.wait_ge(s_rest[b], 1 + 2 * NF + k + 1)
                        mm = product(own(b, 0), wg_first[2 * NF + k], wg_rest[2 * NF + k], inner[b][2][k],
                                     False, k == NF - 1, False, True)
                    mm.then_inc(s_dn[b], 1)

        @block.scalar
        def _(act):
            def value_and_first(src, dst, first, bias, scale=1.0):
                if bias is None:
                    act.activation(dst, src, ACT.Copy, scale=scale)
                    return act.activation(first, src, ACT.Copy, scale=scale)
                act.activation(dst, src, ACT.Identity, bias=bias)
                return act.activation(first, src, ACT.Identity, bias=bias)

            def reciprocal(tile, chain, done):
                act.activation(tile, tile, ACT.Ln).then_inc(chain, 1)
                act.wait_ge(chain, done + 1)
                act.activation(tile, tile, ACT.Exp, scale=-1.0).then_inc(chain, 1)

            held = [None]

            def tables(name):
                if held[0] != name:
                    act.preload_act_table_set(name)
                    held[0] = name

            tables(LN_EXP)
            loaded(act, "cols")
            act.activation(decay[:, 0:1], col["decay"], ACT.Exp).then_inc(s_small, 1)
            act.activation(keep[:, 0:1], col["lambda"], ACT.Exp, scale=-1.0).then_inc(s_small, 1)
            for u in range(2 * NB):
                act.wait_ge(s_qk, u + 1)
                value, _, parts = (q_split, k_split)[u % 2][u // 2]
                value_and_first(bank(u), value, parts[:, 0, :], col["bq" if u % 2 == 0 else "bk"]) \
                    .then_inc(s_qk_val, 1)
            for L in range(2):
                act.wait_ge(s_kx, 2)
                value, _, parts = kx_split[L]
                value_and_first(psum[:, 6, 256 * L:256 * L + NB * NKEY], value, parts[:, 0, :],
                                None if L == 0 else col["xbk"]).then_inc(s_kx_val, 1)

            for kind, n, j, step, b, at in order("scalar"):
                nb = OWN_BANKS[b]
                if kind == "rowmax":
                    act.wait_ge(s_mt, n + 1)
                    if n >= 2:
                        act.wait_ge(s_maug, 48 * (n - 1))
                    o = item_bank(kind, n)[0:G * TT, 0:P]
                    value_and_first(o, mt[n % 2][0:G * TT, 0, :], mp[n % 2][0:G * TT, 0, :], None, -1.0) \
                        .then_inc(s_mval, 1)
                if kind == "score":
                    v = NX * n + j
                    act.wait_ge(s_sc, v + 1)
                    if v >= NPROB:
                        act.wait_ge(s_pv, v - NPROB + 1)
                    tables(LN_EXP)
                    act.activation(probs[:, v % NPROB, :], item_bank(kind, n, j), ACT.Exp, scale=float(D0) ** -0.5) \
                        .then_inc(s_exp, 1)
                if kind == "denominator":
                    act.wait_ge(s_den, n + 1)
                    tables(LN_EXP)
                    reciprocal(den_tile(b, n), s_rec, 2 * n)

                if step.startswith("norm_mean"):
                    act.wait_ge(s_cent[b], int(step[-1]) + 1)
                    act.activation(sq[b][:, :], own(b, 0), ACT.Square).then_inc(s_sq[b], 1)
                if step.startswith(("norm_var", "mix_scan", "mix_divide", "cross_score", "cross_den")):
                    tables(LN_EXP)
                if step.startswith("norm_var"):
                    n = int(step[-1])
                    act.wait_ge(s_var[b], n + 1)
                    if n == 0:
                        act.wait_ge(s_vzero, 1)
                    act.activation(rstd[b][:, :], own(b, 1), ACT.Ln, bias=eps[:, 0:1]).then_inc(s_ln[b], 1)
                    act.wait_ge(s_ln[b], n + 1)
                    act.activation(rstd[b][:, :], rstd[b][:, :], ACT.Exp, scale=-0.5).then_inc(s_rstd[b], 1)
                for L in range(2):
                    if step == f"cross_query{L}":
                        act.wait_ge(x_q[b], L * FIRST["q"] + 1)
                        value, _, parts = q_split[b]
                        value_and_first(own(b, 0), value, parts[:, 0, :], None if L == 0 else col["xbq"]) \
                            .then_inc(x_val[b], 1)
                    if step == f"cross_rowmax{L}":
                        n = TT * HX[L]
                        act.wait_ge(x_mt[b], L * FIRST["mt"] + 1)
                        value_and_first(own(b, 2)[0:n, 0:P], xmt[b][0:n, 0, :], xmp[b][0:n, 0, :], None, -1.0) \
                            .then_inc(x_mval[b], 1)
                    if step == f"cross_score{L}":
                        h, = at
                        act.wait_ge(x_sc[b], L * FIRST["sc"] + h + 1)
                        if h >= 2 * G:
                            act.wait_ge(x_pv[b], L * FIRST["pv"] + h // G - 1)
                        act.activation(cross_probs(L, b, h), own(b, h % 2)[0:NKEY, :], ACT.Exp,
                                       scale=float(DX[L]) ** -0.5).then_inc(x_exp[b], 1)
                    if step == f"cross_den{L}":
                        g, = at
                        act.wait_ge(x_den[b], L * FIRST["den"] + g + 1)
                        reciprocal(den_tile(b, g), x_rec[b], 2 * (L * FIRST["den"] + g))
                if step == "ffn_up":
                    for j in range(NF):
                        act.wait_ge(s_up[b], j + 1)
                        act.activation(w4[b][:, j, :], own(b, j % nb), ACT.Relu, bias=col["ffn_b1"][:, j:j + 1]) \
                            .then_inc(s_relu[b], 1)
                if step == "expert_up":
                    tables("gelu_and_others")
                    for k in range(TOPK):
                        act.wait_ge(s_eup[b], k + 1)
                        act.activation(w4[b][:, k, :], own(b, k), ACT.Gelu,
                                       bias=work[b][:, MOE * k + 2 * P:MOE * k + 2 * P + 1]).then_inc(s_egelu[b], 1)
                if step == "mix_in":
                    for i in range(3):
                        act.wait_ge(s_rk[b], i + 1)
                        if i < 2:
                            act.copy(scratch[b][:, i, :], own(b, i)).then_inc(s_rcp[b], 1)
                        else:
                            tables("sigmoid_and_others")
                            act.activation(scratch[b][:, 6, :], own(b, i), ACT.Sigmoid) \
                                .then_inc(s_rcp[b], 1)
                if step == "mix_scan":
                    s = scratch[b]
                    act.wait_ge(s_rscan[b], 5)
                    act.activation(s[:, 2:4, :], s[:, 2:4, :], ACT.Exp).then_inc(s_rexp[b], 1)
                    act.wait_ge(s_rpool[b], 1)
                    act.wait_ge(s_rscan[b], 6)
                    act.activation(s[:, 4:6, :], s[:, 4:6, :], ACT.Exp).then_inc(s_rexp[b], 1)
                if step == "mix_divide":
                    s = scratch[b]
                    act.wait_ge(s_rscan[b], 11)
                    reciprocal(s[:, 2, :], s_rexp[b], 2)
                if step == "gate":
                    tables("silu_and_others")
                    j, = at
                    act.wait_ge(s_ga[b], j + 1)
                    act.activation(w4[b][:, j, :], own(b, 2 * j % 4), ACT.Silu,
                                   scale=col["w1_s"][:, j:j + 1]).then_inc(s_gs[b], 1)
                for i, (name, ready, scale, done) in enumerate((("hidden1", s_h1, "h1_s", s_g1),
                                                                ("hidden2", s_h2, "h2_s", s_g2))):
                    if step == name and at[1] == NF:
                        tables("gelu_and_others")
                        j = at[0]
                        act.wait_ge(ready[b], j + 1)
                        act.activation(inner[b][i + 1][j][0], own(b, j), ACT.Gelu, scale=col[scale][:, j:j + 1]) \
                            .then_inc(done[b], 1)

        @block.vector
        def _(dve):
            def split_rest(value, rest, parts, chain, done):
                dve.tensor_tensor(rest, value, parts[:, 0, :], ALU.subtract).then_inc(chain, 1)
                dve.wait_ge(chain, done + 1)
                dve.tensor_copy(parts[:, 1, :], rest).then_inc(chain, 1)
                dve.wait_ge(chain, done + 2)
                dve.tensor_tensor(parts[:, 2, :], rest, parts[:, 1, :], ALU.subtract).then_inc(chain, 1)

            def split_two(value, first, rest, b, n):
                dve.tensor_copy(first, value).then_inc(s_first[b], 1)
                dve.wait_ge(s_first[b], n + 1)
                dve.tensor_tensor(rest, value, first.bitcast(F32), ALU.subtract).then_inc(s_rest[b], 1)

            def stack_parts(u):
                dve.wait_ge(s_qk_val, u + 1)
                split_rest(*(q_split, k_split)[u % 2][u // 2], s_qk_split, 3 * u)

            dve.memset(eps[:, :], EPS)
            dve.memset(qstack[0][:, :, :].rearrange("p h t -> p (h t)").bitcast(F32), 0.0).then_inc(s_vzero, 1)
            for u in range(2):
                stack_parts(u)

            for kind, n, j, step, b, at in order("vector"):
                nb = OWN_BANKS[b]
                g = n % NG0
                if kind == "max":
                    i, h0, nh = MAX_UNITS[j]
                    if n == 1 and j in (0, 2):
                        c = j // 2
                        dve.wait_ge(s_zero, 5)
                        dve.wait_ge(s_v0, c + 1)
                        dve.tensor_copy(v0[:, c, :, :, 0:D0].rearrange("p k h d -> p (k h) d"),
                                        bank(c).rearrange("p (k d) -> p k d", d=D0)).then_inc(s_v0_out, 1)
                    if n == 1 and j == 8:
                        dve.wait_ge(s_small, 2)
                        dve.tensor_scalar(keep[:, 1:2], keep[:, 0:1], 1.0, None, ALU.add).then_inc(s_param, 1)
                        dve.wait_ge(s_param, 1)
                        dve.reciprocal(keep[:, 0:1], keep[:, 1:2]).then_inc(s_param, 1)
                        dve.wait_ge(s_param, 2)
                        dve.tensor_scalar(keep[:, 2:3], keep[:, 0:1], -1.0, 1.0, ALU.mult, ALU.add).then_inc(s_param, 1)
                        dve.tensor_scalar(decay[:, 1:2], decay[:, 0:1], -1.0, None, ALU.mult).then_inc(s_param, 1)
                        dve.tensor_scalar(omm[:, :], col["mix"], -1.0, 1.0, ALU.mult, ALU.add).then_inc(s_param, 1)
                        for c in range(NB):
                            dve.memset(xs[c][:, 0:1], 0.0).then_inc(s_param, 1)
                    if n == 1 and j in (4, 6):
                        L = (j - 4) // 2
                        dve.wait_ge(s_kx_val, L + 1)
                        split_rest(*kx_split[L], s_kx_split, 3 * L)
                    if n == 1 and j in (5, 7):
                        L = (j - 5) // 2
                        dve.wait_ge(s_vx, 1)
                        dve.wait_ge(s_zero, 12)
                        for c in range(NB):
                            o = psum[0:NKEY, 2, P * (2 * L + c):P * (2 * L + c + 1)]
                            dve.tensor_copy(vx[L][:, c, :, 0:DX[L]], o.rearrange("p (h d) -> p h d", d=DX[L])) \
                                .then_inc(s_vx_out, 1)
                    if n == 2 and j in (0, 4):
                        stack_parts(2 + j // 4)
                    if n >= 2 and j == 0:
                        dve.wait_ge(s_mt, n - 1)
                    dve.wait_ge(s_msc, NM * n + j + 1)
                    width = P * (i + 1)
                    src = item_bank(kind, n, j)[:, 0:nh * width].rearrange("p (h k) -> p h k", h=nh)
                    dve.tensor_reduce(mx[n % 2][:, TT * h0 + i:TT * (h0 + nh - 1) + i + 1:TT], src, AX.X, ALU.max) \
                        .then_inc(s_mx, 1)
                if kind == "rowmax":
                    dve.wait_ge(s_mval, n + 1)
                    split_rest(mt[n % 2][0:G * TT, 0, :], mt[n % 2][0:G * TT, 1, :], mp[n % 2][0:G * TT],
                               s_msplit, 3 * n)
                if kind == "denominator":
                    dve.wait_ge(s_pv, NX * (n + 1))
                    dve.stream_shuffle(den_tile(b, n), bank(out_bank(n)), [D0] * VW).then_inc(s_den, 1)
                if kind == "divide":
                    dve.wait_ge(s_rec, 2 * (n + 1))
                    dve.tensor_tensor(w4[b][:, g, :], bank(out_bank(n)), den_tile(b, n), ALU.mult) \
                        .then_inc(s_div, 1)
                if kind == "project":
                    dve.wait_ge(s_proj[b], 1)
                    dve.scalar_tensor_tensor(out=z[b][:, :], in0=own(b, 2), scalar=col["bo"], in1=state(b),
                                             op0=ALU.add, op1=ALU.add).then_inc(s_z[b], 1)

                if step.startswith("norm_var"):
                    n = int(step[-1])
                    dve.wait_ge(s_rstd[b], n + 1)
                    if n in (1, 2):
                        dst = qe[b] if n == 1 else z[b]
                        dve.scalar_tensor_tensor(out=dst[:, :], in0=own(b, 0), scalar=col[f"ln{n}_g"],
                                                 in1=rstd[b][:, :], op0=ALU.mult, op1=ALU.mult) \
                            .then_inc(s_aff[b], 1)
                        dve.wait_ge(s_aff[b], n)
                        if n == 1:
                            dve.tensor_scalar(qe[b][:, :], qe[b][:, :], col["ln1_b"], None, ALU.add) \
                                .then_inc(s_x[b], 1)
                        else:
                            dve.scalar_tensor_tensor(out=z[b][:, :], in0=z[b][:, :], scalar=col["ln2_b"],
                                                     in1=state(b), op0=ALU.add, op1=ALU.add) \
                                .then_inc(s_z[b], 1)
                    else:
                        dve.tensor_tensor(state(b), own(b, 0), rstd[b][:, :], ALU.mult).then_inc(s_x[b], 1)
                    if n == 6:
                        dve.wait_ge(s_x[b], 6)
                        split_two(state(b), fp32r[f"z{b}"][:, :], fp32r[f"sq{b}"][:, :], b, 0)
                for L in range(2):
                    if step == f"cross_query{L}":
                        dve.wait_ge(x_val[b], L * FIRST["val"] + 1)
                        split_rest(*q_split[b], x_split[b], L * FIRST["split"])
                    if step == f"cross_max{L}":
                        i, g = at
                        u = i * (HX[L] // G) + g
                        dve.wait_ge(x_msc[b], L * FIRST["msc"] + u + 1)
                        src = own(b, u % nb)[:, 0:G * NKEY].rearrange("p (h k) -> p h k", h=G)
                        dst = xmx[b][:, TT * G * g + i:TT * (G * (g + 1) - 1) + i + 1:TT]
                        dve.tensor_reduce(dst, src, AX.X, ALU.max).then_inc(x_mx[b], 1)
                    if step == f"cross_rowmax{L}":
                        n = TT * HX[L]
                        dve.wait_ge(x_mval[b], L * FIRST["mval"] + 1)
                        split_rest(xmt[b][0:n, 0, :], xmt[b][0:n, 1, :], xmp[b][0:n], x_msplit[b], L * FIRST["msplit"])
                    if step == f"cross_den{L}":
                        g, = at
                        dve.wait_ge(x_pv[b], L * FIRST["pv"] + g + 1)
                        dve.stream_shuffle(den_tile(b, g), own(b, 2 + g % (nb - 2)), [DX[L]] * VW).then_inc(x_den[b], 1)
                    if step == f"cross_div{L}":
                        g, = at
                        dve.wait_ge(x_rec[b], 2 * (L * FIRST["den"] + g + 1))
                        if L == 0:
                            dve.scalar_tensor_tensor(out=w4[b][:, g, :], in0=own(b, 2 + g % (nb - 2)),
                                                     scalar=keep[:, 2:3], in1=den_tile(b, g),
                                                     op0=ALU.mult, op1=ALU.mult).then_inc(x_div[b], 1)
                        else:
                            dve.tensor_tensor(w4[b][:, g, :], own(b, 2 + g % (nb - 2)), den_tile(b, g), ALU.mult) \
                                .then_inc(x_div[b], 1)
                    if step == f"cross_out{L}":
                        dve.wait_ge(x_out[b], L * FIRST["out"] + 1)
                        if L == 0:
                            dve.tensor_tensor(z[b][:, :], own(b, 0), state(b), ALU.add).then_inc(s_z[b], 1)
                        else:
                            dve.scalar_tensor_tensor(out=z[b][:, :], in0=own(b, 0), scalar=col["xbo"],
                                                     in1=state(b), op0=ALU.add, op1=ALU.add).then_inc(s_z[b], 1)
                if step == "ffn_down":
                    dve.wait_ge(s_down[b], 1)
                    dve.scalar_tensor_tensor(out=z[b][:, :], in0=own(b, 1), scalar=col["ffn_b2"],
                                             in1=qe[b][:, :], op0=ALU.add, op1=ALU.add).then_inc(s_z[b], 1)
                if step == "route":
                    r = route[b]
                    dve.wait_ge(s_rt[b], 1)
                    dve.tensor_tensor(r[:, 0:NE], own(b, 2)[0:1, 0:NE], w["route"][0:1, NE:2 * NE], ALU.add) \
                        .then_inc(s_rchain[b], 1)
                    dve.wait_ge(s_rchain[b], 1)
                    dve.max(r[:, NE:2 * NE], r[:, 0:NE]).then_inc(s_rchain[b], 1)
                    dve.wait_ge(s_rchain[b], 2)
                    dve.max_index(choice[b][:, :], r[:, NE:2 * NE], r[:, 0:NE]).then_inc(s_choice[b], 1)
                if step == "expert_down":
                    dve.wait_ge(s_edown[b], 1)
                    dve.wait_ge(s_b2s[b], 3)
                    dve.scalar_tensor_tensor(out=z[b][:, :], in0=own(b, 2), scalar=1.0 / TOPK, in1=qe[b][:, :],
                                             op0=ALU.mult, op1=ALU.add).then_inc(s_z[b], 1)
                if step == "mix_in":
                    s, (pp, aa, bb) = scratch[b], carried(wide[b])
                    for t, v in ((pp, NEG), (aa, 0.0), (bb, 0.0)):
                        ins = dve.memset(t[:, 0:1], v)
                    ins.then_inc(s_rscan[b], 1)
                    dve.wait_ge(s_rscan[b], 1)
                    dve.wait_ge(s_rcp[b], 1)
                    dve.tensor_tensor_scan(pp[:, 1:T + 1], decay[:, 1:2].broadcast_to([P, T]), s[:, 0, :], NEG,
                                           ALU.add, ALU.max).then_inc(s_rscan[b], 1)
                    dve.wait_ge(s_rscan[b], 2)
                    dve.scalar_tensor_tensor(out=s[:, 7, :], in0=s[:, 0, :], scalar=col["first"], in1=pp[:, 0:T],
                                             op0=ALU.add, op1=ALU.max).then_inc(s_rscan[b], 1)
                    dve.scalar_tensor_tensor(out=s[:, 2, :], in0=pp[:, 0:T], scalar=decay[:, 1:2],
                                             in1=pp[:, 1:T + 1], op0=ALU.add, op1=ALU.subtract) \
                        .then_inc(s_rscan[b], 1)
                    dve.wait_ge(s_rscan[b], 4)
                    dve.tensor_tensor(s[:, 3, :], s[:, 0, :], pp[:, 1:T + 1], ALU.subtract).then_inc(s_rscan[b], 1)
                    dve.scalar_tensor_tensor(out=s[:, 5, :], in0=s[:, 0, :], scalar=col["first"], in1=s[:, 7, :],
                                             op0=ALU.add, op1=ALU.subtract).then_inc(s_rscan[b], 1)
                if step == "mix_scan":
                    s, (pp, aa, bb) = scratch[b], carried(wide[b])
                    dve.wait_ge(s_rexp[b], 1)
                    dve.tensor_tensor_scan(bb[:, 1:T + 1], s[:, 2, :], s[:, 3, :], 0.0, ALU.mult, ALU.add) \
                        .then_inc(s_rscan[b], 1)
                    dve.wait_ge(s_rpool[b], 2)
                    dve.tensor_tensor_scan(aa[:, 1:T + 1], s[:, 2, :], s[:, 7, :], 0.0, ALU.mult, ALU.add) \
                        .then_inc(s_rscan[b], 1)
                    dve.wait_ge(s_rscan[b], 8)
                    dve.wait_ge(s_rexp[b], 2)
                    dve.tensor_tensor(s[:, 2, :], s[:, 4, :], bb[:, 0:T], ALU.mult).then_inc(s_rscan[b], 1)
                    dve.tensor_tensor(s[:, 0, :], s[:, 4, :], aa[:, 0:T], ALU.mult).then_inc(s_rscan[b], 1)
                    dve.wait_ge(s_rscan[b], 9)
                    dve.tensor_tensor(s[:, 2, :], s[:, 2, :], s[:, 5, :], ALU.add).then_inc(s_rscan[b], 1)
                    dve.wait_ge(s_rscan[b], 10)
                    dve.wait_ge(s_rpool[b], 3)
                    dve.wait_ge(s_rcp[b], 3)
                    dve.tensor_tensor(s[:, 0, :], s[:, 0, :], s[:, 1, :], ALU.add).then_inc(s_rscan[b], 1)
                    dve.wait_ge(s_rscan[b], 12)
                    dve.tensor_tensor(s[:, 0, :], s[:, 0, :], s[:, 6, :], ALU.mult).then_inc(s_rscan[b], 1)
                if step == "mix_divide":
                    s = scratch[b]
                    dve.wait_ge(s_rexp[b], 4)
                    dve.wait_ge(s_rscan[b], 13)
                    dve.tensor_tensor(s[:, 7, :], s[:, 0, :], s[:, 2, :], ALU.mult).then_inc(s_rscan[b], 1)
                if step == "mix_out":
                    dve.wait_ge(s_rout[b], 1)
                    dve.tensor_tensor(z[b][:, :], own(b, 0), state(b), ALU.add).then_inc(s_z[b], 1)
                if step == "gate":
                    j, = at
                    dve.wait_ge(s_gb[b], j + 1)
                    dve.wait_ge(s_gs[b], j + 1)
                    dve.scalar_tensor_tensor(out=scratch[b][:, j, :], in0=own(b, (2 * j + 1) % 4),
                                             scalar=col["w2_s"][:, j:j + 1], in1=w4[b][:, j, :],
                                             op0=ALU.mult, op1=ALU.mult).then_inc(s_gh[b], 1)
                    dve.wait_ge(s_gh[b], j + 1)
                    split_two(*inner[b][0][j], b, 1 + j)
                for i, (name, done) in enumerate((("hidden1", s_g1), ("hidden2", s_g2))):
                    if step == name and at[1] == NF:
                        dve.wait_ge(done[b], at[0] + 1)
                        split_two(*inner[b][i + 1][at[0]], b, 1 + NF * (i + 1) + at[0])
                if step == "down":
                    dve.wait_ge(s_dn[b], 1)
                    dve.scalar_tensor_tensor(out=z[b][:, :], in0=own(b, 0), scalar=col["w3_s"], in1=state(b),
                                             op0=ALU.mult, op1=ALU.add).then_inc(s_z[b], 1)

        @block.gpsimd
        def _(pool):
            def fill(stack, first, end, value):
                return pool.memset(stack[first:end, :, :].rearrange("p h t -> p (h t)").bitcast(F32), value)

            fill(kstack[0], 32, 64, ONES).then_inc(s_zero, 1)
            pool.wait_ge(s_zero, 1)
            fill(kstack[0], 64, P, 0.0).then_inc(s_zero, 1)
            loaded(pool, "const")
            pool.wait_ge(s_zero, 2)
            pool.tensor_copy(ident_b[:, :], ident)
            pool.tensor_copy(mask_b[:, :], w["const"][:, 4 * P:5 * P]).then_inc(s_zero, 1)
            pool.wait_ge(s_zero, 3)
            pool.memset(v0[:, :, :, :, :].rearrange("p b k h c -> p (b k h c)"), 0.0).then_inc(s_zero, 1)
            pool.wait_ge(s_zero, 4)
            pool.memset(v0[:, :, :, :, D0:D0 + 1].rearrange("p b k h c -> p (b k h) c"), 1.0).then_inc(s_zero, 1)
            pool.wait_ge(s_zero, 5)
            fill(kx[0], 96, P, ONES).then_inc(s_zero, 1)
            pool.wait_ge(s_zero, 6)
            fill(kx[1], 32, 64, 0.0).then_inc(s_zero, 1)
            pool.wait_ge(s_zero, 7)
            fill(kx[1], 64, P, ONES).then_inc(s_zero, 1)
            pool.wait_ge(s_zero, 8)
            fill(kstack[1], 32, 64, ONES).then_inc(s_zero, 1)
            pool.wait_ge(s_zero, 9)
            fill(kstack[1], 64, P, 0.0).then_inc(s_zero, 1)
            pool.wait_ge(s_zero, 10)
            for L in range(2):
                last = pool.memset(vx[L][:, :, :, :], 0.0)
            last.then_inc(s_zero, 1)
            pool.wait_ge(s_zero, 11)
            for L in range(2):
                last = pool.memset(vx[L][:, :, :, DX[L]:DX[L] + 1], 1.0)
            last.then_inc(s_zero, 1)
            pool.wait_ge(s_zero, 12)
            fill(qstack[1], 0, P, 0.0).then_inc(s_zero, 1)
            pool.wait_ge(s_zero, 13)

            for kind, n, j, step, b, at in order("gpsimd"):
                nb = OWN_BANKS[b]
                if kind == "score":
                    v = NX * n + j
                    pool.wait_ge(s_exp, v + 1)
                    apart, m = DIAGONALS[j]
                    view = probs[:, v % NPROB, 0:apart * m].rearrange("p (m s) -> p m s", s=apart)[:, :, 0:P]
                    pool.affine_select(out=view, in_=view, compare_op=ALU.is_ge, fill=0.0, base=0,
                                       pattern=[[0, m], [1, P]], channel_multiplier=-1).then_inc(s_mask, 1)

                if step == "norm_mean0" and b == 0:
                    loaded(pool, "mix")
                    loaded(pool, "moe")
                    pool.wait_ge(s_param, 5)
                    for i in range(3):
                        wi = w["mix"][:, P * i:P * (i + 1)]
                        pool.tensor_scalar(wmix[i][:, 0, :], wi, col["mix"][:, i:i + 1], None, ALU.mult) \
                            .then_inc(s_wmix, 1)
                        pool.tensor_scalar(wmix[i][:, 1, :], wi, omm[:, i:i + 1], None, ALU.mult) \
                            .then_inc(s_wmix, 1)

                if step == "cross_max0" and b == 1 and at[1] == 0:
                    if at[0] == 0:
                        pool.wait_ge(s_proj[1], 1)
                        loaded(pool, "gate")
                    blocks = range(3 * at[0], 3 * at[0] + 3)
                    for i in blocks:
                        last = pool.tensor_copy(wg_first[i], w["gate"][:, P * i:P * (i + 1)])
                    last.then_inc(s_wfirst, 1)
                    pool.wait_ge(s_wfirst, at[0] + 1)
                    for i in blocks:
                        last = pool.tensor_tensor(wg_rest[i], w["gate"][:, P * i:P * (i + 1)],
                                                  wg_first[i].bitcast(F32), ALU.subtract)
                    last.then_inc(s_wrest, 1)
                if step == "cross_score0" and b == 1:
                    i, k = at[0] // NF, at[0] % NF
                    if at[0] == 0:
                        pool.wait_ge(s_wh, 32)
                    pool.tensor_copy(wh_first[i][:, k, :], wh[i][:, k, :]).then_inc(s_wfirst, 1)
                    pool.wait_ge(s_wfirst, NF + at[0] + 1)
                    pool.tensor_tensor(wh_rest[i][:, k, :], wh[i][:, k, :], wh_first[i][:, k, :].bitcast(F32),
                                       ALU.subtract).then_inc(s_wrest, 1)
                if step == "route":
                    pool.wait_ge(s_choice[b], 1)
                    for k in range(TOPK):
                        e = pool.value_load(choice[b][0:1, k:k + 1], min_val=0, max_val=NE - 1)
                        pool.tensor_copy(work[b][:, MOE * k:MOE * (k + 1)],
                                         w["moe"][:, bass.ds(e * MOE, MOE)]).then_inc(s_pick[b], 1)
                    pool.wait_ge(s_pick[b], TOPK)
                    pool.tensor_tensor(b2s[b][:, 0:1], work[b][:, MOE - 1:MOE], work[b][:, 2 * MOE - 1:2 * MOE],
                                       ALU.add).then_inc(s_b2s[b], 1)
                    pool.wait_ge(s_b2s[b], 1)
                    pool.tensor_scalar(b2s[b][:, 1:2], b2s[b][:, 0:1], 1.0 / TOPK, None, ALU.mult) \
                        .then_inc(s_b2s[b], 1)
                    pool.wait_ge(s_b2s[b], 2)
                    pool.tensor_scalar(qe[b][:, :], state(b), b2s[b][:, 1:2], None, ALU.add).then_inc(s_b2s[b], 1)
                if step == "mix_in":
                    s, (pp, _, _) = scratch[b], carried(wide[b])
                    pool.wait_ge(s_rscan[b], 3)
                    pool.tensor_tensor(s[:, 4, :], pp[:, 0:T], s[:, 7, :], ALU.subtract).then_inc(s_rpool[b], 1)
                if step == "mix_scan":
                    s = scratch[b]
                    pool.wait_ge(s_rexp[b], 1)
                    pool.wait_ge(s_rscan[b], 6)
                    pool.wait_ge(s_rpool[b], 1)
                    pool.wait_ge(s_rcp[b], 2)
                    pool.tensor_tensor(s[:, 7, :], s[:, 3, :], s[:, 1, :], ALU.mult).then_inc(s_rpool[b], 1)
                    pool.wait_ge(s_rpool[b], 2)
                    pool.wait_ge(s_rexp[b], 2)
                    pool.tensor_tensor(s[:, 1, :], s[:, 5, :], s[:, 1, :], ALU.mult).then_inc(s_rpool[b], 1)


MIX_DVE = 14
MOE = 2 * P + 2


def carried(area):
    return [area[:, (T + 1) * i:(T + 1) * (i + 1)] for i in range(3)]


_COLS = [("bq", 1), ("bk", 1), ("bo", 1), ("ln1_g", 1), ("ln1_b", 1), ("ln2_g", 1), ("ln2_b", 1), ("ffn_b1", NF),
         ("ffn_b2", 1), ("lambda", 1), ("decay", 1), ("first", 1), ("mix", 3), ("xbq", 1), ("xbk", 1), ("xbo", 1),
         ("w1_s", NF), ("w2_s", NF), ("h1_s", NF), ("h2_s", NF), ("w3_s", 1)]
COLS, _at = [], 0
for _name, _n in _COLS:
    COLS.append((_name, _at, _n))
    _at += _n
NCOL = _at

LOADS = {
    "x": ([P, NB * T], F32), "qk": ([P, 2 * P], F32), "cols": ([P, NCOL], F32), "const": ([P, 5 * P], F32),
    "v0": ([P, 2 * P], F32), "ctx": ([P, NB * NKEY], F32), "xkv": ([P, 4 * P], F32), "xbv": ([1, P], F32),
    "o0": ([P, NG0 * P], F32), "xq": ([P, 2 * P], F32), "xo": ([P, 6 * P], F32), "ffn": ([P, 2 * NF * P], F32),
    "route": ([P, 2 * NE], F32), "moe": ([P, NE * MOE], F32), "mix": ([P, 4 * P], F32),
    "gate": ([P, 3 * NF * P], F32), "h1": ([P, NF, NF * P], F32), "h2": ([P, NF, NF * P], F32),
}
LOAD_GROUPS = {"x": ["x"], "qk": ["qk"], "cols": ["cols"], "const": ["const"],
               "context": ["v0", "ctx", "xkv", "xbv"], "project": ["o0", "xq", "xo"],
               "ffn": ["ffn", "route", "moe"], "mix": ["mix", "gate"]}


def laid_out(i):
    import numpy as np

    i = {k: np.asarray(v) for k, v in i.items()}

    def by_feature(a, heads):
        return a.reshape(*a.shape[:-1], heads, -1).swapaxes(-1, -2).reshape(a.shape)

    def column(a, n=1):
        return np.broadcast_to(a, (P,)).reshape(P, 1) if a.ndim == 0 else a.reshape(n, P).T

    def padded(wo, d):
        g = wo.reshape(-1, G, d, P)
        out = np.zeros((g.shape[0], G, VW, P), np.float32)
        out[:, :, :d] = g
        return out.reshape(-1, P, P).transpose(1, 0, 2).reshape(P, -1)

    def in_rows(a):
        return a.reshape(-1, P, a.shape[-1]).transpose(1, 0, 2).reshape(P, -1)

    out = {}
    out["x"] = i["x"].transpose(2, 0, 1).reshape(P, NB * T)
    wq, wk, wv = np.split(i["L0_attn_w_attn"].T, 3, axis=1)
    bq, bk, bv = np.split(i["L0_attn_b_attn"], 3)
    out["qk"] = np.concatenate([by_feature(wq, H0), by_feature(wk, H0)], 1)
    row = np.zeros((P, P), np.float32)
    row[0] = bv
    out["v0"] = np.concatenate([wv, row], 1)
    out["ctx"] = i["ctx_1024"].transpose(2, 0, 1).reshape(P, NB * NKEY)
    out["xkv"] = np.concatenate([by_feature(i["L0_xattn_Wk"], HX[0]), i["L0_xattn_Wv"],
                                 by_feature(i["L1_xattn_Wk"], HX[1]), i["L1_xattn_Wv"]], 1)
    out["xbv"] = i["L1_xattn_bv"].reshape(1, P)
    out["o0"] = padded(i["L0_attn_w_proj"].T, D0)
    out["xq"] = np.concatenate([by_feature(i["L0_xattn_Wq"], HX[0]), by_feature(i["L1_xattn_Wq"], HX[1])], 1)
    out["xo"] = np.concatenate([padded(i["L0_xattn_Wo"], DX[0]), padded(i["L1_xattn_Wo"], DX[1])], 1)
    out["ffn"] = np.concatenate([i["L0_xattn_ffn_w1"], in_rows(i["L0_xattn_ffn_w2"])], 1)
    br = np.zeros((P, NE), np.float32)
    br[0] = i["L0_ffn_br"]
    out["route"] = np.concatenate([i["L0_ffn_Wr"], br], 1)
    out["moe"] = np.concatenate([i["L0_ffn_W1"], i["L0_ffn_W2"], i["L0_ffn_b1"][:, :, None],
                                 i["L0_ffn_b2"][:, :, None]], 2).transpose(1, 0, 2).reshape(P, -1)
    out["mix"] = np.concatenate([i[f"L1_attn_W{k}"].T for k in "kvro"], 1)
    out["gate"] = np.concatenate([i["L1_ffn_w1_w"].T, i["L1_ffn_w2_w"].T, in_rows(i["L1_ffn_w3_w"].T)], 1)
    for k in ("h1", "h2"):
        out[k] = in_rows(i[f"L1_ffn_{k}_w"].T).reshape(P, NF, NF * P)
    mix = np.stack([i[f"L1_attn_time_mix_{k}"].reshape(P) for k in "kvr"], 1)
    cols = {
        "bq": by_feature(bq, H0), "bk": by_feature(bk, H0), "bo": i["L0_attn_b_proj"],
        "ln1_g": i["L0_xattn_ln1_g"], "ln1_b": i["L0_xattn_ln1_b"], "ln2_g": i["L0_xattn_ln2_g"],
        "ln2_b": i["L0_xattn_ln2_b"], "ffn_b1": i["L0_xattn_ffn_b1"], "ffn_b2": i["L0_xattn_ffn_b2"],
        "lambda": i["L0_xattn_lambda_param"], "decay": i["L1_attn_time_decay"], "first": i["L1_attn_time_first"],
        "xbq": by_feature(i["L1_xattn_bq"], HX[1]), "xbk": by_feature(i["L1_xattn_bk"], HX[1]),
        "xbo": i["L1_xattn_bo"], "w1_s": i["L1_ffn_w1_s"], "w2_s": i["L1_ffn_w2_s"], "h1_s": i["L1_ffn_h1_s"],
        "h2_s": i["L1_ffn_h2_s"], "w3_s": i["L1_ffn_w3_s"],
    }
    out["cols"] = np.concatenate([mix if n == "mix" else column(cols[n], k) for n, _, k in COLS], 1)

    eye = np.eye(P, dtype=np.float32)
    p = np.arange(P)
    const = [eye - 1.0 / P, np.full((P, P), 1.0 / P), eye]
    const += [np.ones((P, P)), np.where(p[None, :] > p[:, None], -1e30, 0.0)]
    out["const"] = np.concatenate(const, 1).astype(np.float32)
    return out


def kernel(**inputs):
    import numpy as np
    import concourse.bacc as bacc
    from concourse.bass_utils import run_bass_kernel_spmd

    nc = bacc.Bacc("TRN2", target_bir_lowering=False, num_devices=1)
    arrays, dram = {}, {}
    for name, a in laid_out(inputs).items():
        a = np.ascontiguousarray(a)
        arrays[f"in_{name}"] = a
        dram[name] = nc.dram_tensor(f"in_{name}", a.shape, mybir.dt.from_np(a.dtype), kind="ExternalInput").ap()
    out = nc.dram_tensor("out", [P, NB * T], F32, kind="ExternalOutput").ap()
    decoder(nc, dram, out)
    r = run_bass_kernel_spmd(nc, [arrays], core_ids=[0])
    return r.results[0]["out"].reshape(P, NB, T).transpose(1, 2, 0)
```
